# Optimizing a Trainium2 kernel written in Bass

```python
import numpy as np
import jax
import jax.numpy as jnp

def _softmax(x, axis=-1):
    return jax.nn.softmax(x, axis=axis)

def _gelu(x):
    return jax.nn.gelu(x, approximate=True)

def _silu(x):
    return jax.nn.silu(x)

def _sigmoid(x):
    return jax.nn.sigmoid(x)

def _layernorm(x, axis=-1, eps=1e-05):
    m = jnp.mean(x, axis=axis, keepdims=True)
    v = jnp.var(x, axis=axis, keepdims=True)
    return (x - m) / jnp.sqrt(v + eps)

def _scatter_add(tgt, idx, src, axis=0):
    return tgt.at[idx].add(src)

def _segment_sum(src, seg, n):
    return jax.ops.segment_sum(src, seg, n)
kernel_name = 'mk_macaron_d2_jaxref_r8_03e543'

def setup_inputs(seed: int=0):
    np.random.seed(seed)
    _w = jnp.asarray

    def _L0_attn_setup():
        import jax, jax.numpy as jnp
        import numpy as np
        D_MODEL = 128
        N_HEAD = 16
        SEG = 32
        HEAD_DIM = D_MODEL // N_HEAD
        SCALE = 1.0 / HEAD_DIM ** 0.5
        key = jax.random.key(seed)
        ks = jax.random.split(key, 9)
        B, L, D = (4, 512, D_MODEL)
        s = 1.0 / np.sqrt(D)
        x = jax.random.normal(ks[0], (B, L, D), dtype=jnp.float32)
        Wq = jax.random.uniform(ks[1], (D, D), jnp.float32, -s, s)
        bq = jax.random.uniform(ks[2], (D,), jnp.float32, -s, s)
        Wk = jax.random.uniform(ks[3], (D, D), jnp.float32, -s, s)
        bk = jax.random.uniform(ks[4], (D,), jnp.float32, -s, s)
        Wv = jax.random.uniform(ks[5], (D, D), jnp.float32, -s, s)
        bv = jax.random.uniform(ks[6], (D,), jnp.float32, -s, s)
        Wo = jax.random.uniform(ks[7], (D, D), jnp.float32, -s, s)
        bo = jax.random.uniform(ks[8], (D,), jnp.float32, -s, s)
        return {'x': x, 'Wq': Wq, 'bq': bq, 'Wk': Wk, 'bk': bk, 'Wv': Wv, 'bv': bv, 'Wo': Wo, 'bo': bo}
    _L0_attn_in = _L0_attn_setup()

    def _L0_ffn_setup():
        import jax, jax.numpy as jnp
        import numpy as np
        from jax.scipy.linalg import expm
        B, S, D, E, K, NROT = (2, 256, 128, 8, 2, 3)
        EPS = 1e-05

        def _gelu(x):
            return jax.nn.gelu(x, approximate=False)

        def _forward(x, ln_gamma, ln_beta, abel_w, abel_b, moe_gate_w, moe_gate_b, ew1, eb1, ew2, eb2, gens, gc_w, gc_b):
            residual = x
            mu = jnp.mean(x, axis=-1, keepdims=True)
            var = jnp.mean((x - mu) ** 2, axis=-1, keepdims=True)
            xn = (x - mu) * jax.lax.rsqrt(var + EPS) * ln_gamma + ln_beta
            abel_out = _gelu(xn @ abel_w + abel_b)
            logits = xn @ moe_gate_w + moe_gate_b
            topw, topi = jax.lax.top_k(logits, K)
            topw = jax.nn.softmax(topw, axis=-1)
            w_dense = jnp.sum(jax.nn.one_hot(topi, E, dtype=xn.dtype) * topw[..., None], axis=-2)
            h = _gelu(jnp.einsum('bsd,edh->ebsh', xn, ew1) + eb1[:, None, None, :])
            eo = jnp.einsum('ebsh,ehd->ebsd', h, ew2) + eb2[:, None, None, :]
            moe_out = jnp.einsum('ebsd,bse->bsd', eo, w_dense)
            for i in range(NROT):
                moe_out = moe_out @ expm(gens[i])
            combined = jnp.concatenate([abel_out, moe_out], axis=-1)
            gate = jax.nn.sigmoid(combined @ gc_w + gc_b)
            mixed = abel_out * (1.0 - gate) + moe_out * gate
            return residual + mixed
        key = jax.random.key(seed)
        ks = jax.random.split(key, 16)
        sc = 0.02
        x = jax.random.normal(ks[0], (B, S, D), jnp.float32)
        ln_gamma = 1.0 + sc * jax.random.normal(ks[1], (D,), jnp.float32)
        ln_beta = sc * jax.random.normal(ks[2], (D,), jnp.float32)
        abel_w = sc * jax.random.normal(ks[3], (D, D), jnp.float32)
        abel_b = sc * jax.random.normal(ks[4], (D,), jnp.float32)
        moe_gate_w = sc * jax.random.normal(ks[5], (D, E), jnp.float32)
        moe_gate_b = sc * jax.random.normal(ks[6], (E,), jnp.float32)
        ew1 = sc * jax.random.normal(ks[7], (E, D, 2 * D), jnp.float32)
        eb1 = sc * jax.random.normal(ks[8], (E, 2 * D), jnp.float32)
        ew2 = sc * jax.random.normal(ks[9], (E, 2 * D, D), jnp.float32)
        eb2 = sc * jax.random.normal(ks[10], (E, D), jnp.float32)
        g = sc * jax.random.normal(ks[11], (NROT, D, D), jnp.float32)
        gens = 0.5 * (g - jnp.swapaxes(g, -1, -2))
        gc_w = sc * jax.random.normal(ks[12], (2 * D, 1), jnp.float32)
        gc_b = sc * jax.random.normal(ks[13], (1,), jnp.float32)
        return dict(x=x, ln_gamma=ln_gamma, ln_beta=ln_beta, abel_w=abel_w, abel_b=abel_b, moe_gate_w=moe_gate_w, moe_gate_b=moe_gate_b, ew1=ew1, eb1=eb1, ew2=ew2, eb2=eb2, gens=gens, gc_w=gc_w, gc_b=gc_b)
    _L0_ffn_in = _L0_ffn_setup()

    def _L1_attn_setup():
        import jax, jax.numpy as jnp
        import numpy as np
        DIM = 128
        NUM_HEADS = 16
        HEAD_DIM = DIM // NUM_HEADS
        TAU = 2.0
        V_TH = 1.0
        BN_EPS = 1e-05

        def _branch(x, W, gamma, beta):
            B, N, D = x.shape
            h = jnp.einsum('bnd,ed->bne', x, W)
            hf = h.reshape(B * N, D)
            mean = jnp.mean(hf, axis=0)
            var = jnp.var(hf, axis=0)
            hn = (hf - mean) * jax.lax.rsqrt(var + BN_EPS) * gamma + beta
            hn = hn.reshape(B, N, D)
            return jax.nn.sigmoid(4.0 * (hn - V_TH))

        def _heads(x):
            B, N, D = x.shape
            return x.reshape(B, N, NUM_HEADS, HEAD_DIM).transpose(0, 2, 1, 3)
        key = jax.random.key(seed)
        ks = jax.random.split(key, 12)
        B, N, D = (8, 512, DIM)
        s = 0.02
        return {'x': jax.random.normal(ks[0], (B, N, D), dtype=jnp.float32), 'Wq': jax.random.normal(ks[1], (D, D), dtype=jnp.float32) * s, 'gq': jnp.ones((D,), jnp.float32), 'bq': jnp.zeros((D,), jnp.float32), 'Wk': jax.random.normal(ks[2], (D, D), dtype=jnp.float32) * s, 'gk': jnp.ones((D,), jnp.float32), 'bk': jnp.zeros((D,), jnp.float32), 'Wv': jax.random.normal(ks[3], (D, D), dtype=jnp.float32) * s, 'gv': jnp.ones((D,), jnp.float32), 'bv': jnp.zeros((D,), jnp.float32), 'Wp': jax.random.normal(ks[4], (D, D), dtype=jnp.float32) * s, 'bp': jnp.zeros((D,), jnp.float32)}
    _L1_attn_in = _L1_attn_setup()

    def _L1_ffn_setup():
        import jax, jax.numpy as jnp
        import numpy as np
        B, K, D = (128, 32, 128)
        E = 32
        H = int(D * 0.25)

        def _rsqrt_uniform(key, shape, d):
            bound = d ** (-0.5)
            return jax.random.uniform(key, shape, jnp.float32, -bound, bound)
        key = jax.random.key(seed)
        ks = jax.random.split(key, 7)
        return {'x': jax.random.normal(ks[0], (B, K, D), jnp.float32), 'router_w': _rsqrt_uniform(ks[1], (E, D), D), 'router_b': _rsqrt_uniform(ks[2], (E,), D), 'weights1': _rsqrt_uniform(ks[3], (E, D, H), H), 'bias1': _rsqrt_uniform(ks[4], (E, H), H), 'weights2': _rsqrt_uniform(ks[5], (E, H, D), D), 'bias2': _rsqrt_uniform(ks[6], (E, D), D)}
    _L1_ffn_in = _L1_ffn_setup()
    _d = {'L0_attn_x': _L0_attn_in['x'], 'L0_attn_Wq': _L0_attn_in['Wq'], 'L0_attn_bq': _L0_attn_in['bq'], 'L0_attn_Wk': _L0_attn_in['Wk'], 'L0_attn_bk': _L0_attn_in['bk'], 'L0_attn_Wv': _L0_attn_in['Wv'], 'L0_attn_bv': _L0_attn_in['bv'], 'L0_attn_Wo': _L0_attn_in['Wo'], 'L0_attn_bo': _L0_attn_in['bo'], 'L0_ffn_ln_gamma': _L0_ffn_in['ln_gamma'], 'L0_ffn_ln_beta': _L0_ffn_in['ln_beta'], 'L0_ffn_abel_w': _L0_ffn_in['abel_w'], 'L0_ffn_abel_b': _L0_ffn_in['abel_b'], 'L0_ffn_moe_gate_w': _L0_ffn_in['moe_gate_w'], 'L0_ffn_moe_gate_b': _L0_ffn_in['moe_gate_b'], 'L0_ffn_ew1': _L0_ffn_in['ew1'], 'L0_ffn_eb1': _L0_ffn_in['eb1'], 'L0_ffn_ew2': _L0_ffn_in['ew2'], 'L0_ffn_eb2': _L0_ffn_in['eb2'], 'L0_ffn_gens': _L0_ffn_in['gens'], 'L0_ffn_gc_w': _L0_ffn_in['gc_w'], 'L0_ffn_gc_b': _L0_ffn_in['gc_b'], 'L1_attn_Wq': _L1_attn_in['Wq'], 'L1_attn_gq': _L1_attn_in['gq'], 'L1_attn_bq': _L1_attn_in['bq'], 'L1_attn_Wk': _L1_attn_in['Wk'], 'L1_attn_gk': _L1_attn_in['gk'], 'L1_attn_bk': _L1_attn_in['bk'], 'L1_attn_Wv': _L1_attn_in['Wv'], 'L1_attn_gv': _L1_attn_in['gv'], 'L1_attn_bv': _L1_attn_in['bv'], 'L1_attn_Wp': _L1_attn_in['Wp'], 'L1_attn_bp': _L1_attn_in['bp'], 'L1_ffn_router_w': _L1_ffn_in['router_w'], 'L1_ffn_router_b': _L1_ffn_in['router_b'], 'L1_ffn_weights1': _L1_ffn_in['weights1'], 'L1_ffn_bias1': _L1_ffn_in['bias1'], 'L1_ffn_weights2': _L1_ffn_in['weights2'], 'L1_ffn_bias2': _L1_ffn_in['bias2']}
    _x0 = _d['L0_attn_x']
    _d['L0_attn_x'] = jax.random.normal(jax.random.fold_in(jax.random.key(seed), 1), (2, 2048, 128), dtype=_x0.dtype)
    del _x0
    return _d

def reference(L0_attn_x, L0_attn_Wq, L0_attn_bq, L0_attn_Wk, L0_attn_bk, L0_attn_Wv, L0_attn_bv, L0_attn_Wo, L0_attn_bo, L0_ffn_ln_gamma, L0_ffn_ln_beta, L0_ffn_abel_w, L0_ffn_abel_b, L0_ffn_moe_gate_w, L0_ffn_moe_gate_b, L0_ffn_ew1, L0_ffn_eb1, L0_ffn_ew2, L0_ffn_eb2, L0_ffn_gens, L0_ffn_gc_w, L0_ffn_gc_b, L1_attn_Wq, L1_attn_gq, L1_attn_bq, L1_attn_Wk, L1_attn_gk, L1_attn_bk, L1_attn_Wv, L1_attn_gv, L1_attn_bv, L1_attn_Wp, L1_attn_bp, L1_ffn_router_w, L1_ffn_router_b, L1_ffn_weights1, L1_ffn_bias1, L1_ffn_weights2, L1_ffn_bias2):

    def _L0_attn_ref(x, Wq, bq, Wk, bk, Wv, bv, Wo, bo):
        import jax, jax.numpy as jnp
        import numpy as np
        D_MODEL = 128
        N_HEAD = 16
        SEG = 32
        HEAD_DIM = D_MODEL // N_HEAD
        SCALE = 1.0 / HEAD_DIM ** 0.5
        B, L, D = x.shape
        n_seg = L // SEG
        xs = x.reshape(B, n_seg, SEG, D)
        Q = jnp.einsum('bnsd,ed->bnse', xs, Wq) + bq
        K = jnp.einsum('bnsd,ed->bnse', xs, Wk) + bk
        V = jnp.einsum('bnsd,ed->bnse', xs, Wv) + bv
        scores = jnp.einsum('bnse,bnte->bnst', Q, K) * SCALE
        attn = jax.nn.softmax(scores, axis=-1)
        local = jnp.einsum('bnst,bnte->bnse', attn, V)
        summ = xs[:, :, 0, :]
        Qg = jnp.einsum('bnd,ed->bne', summ, Wq) + bq
        Kg = jnp.einsum('bnd,ed->bne', summ, Wk) + bk
        Vg = jnp.einsum('bnd,ed->bne', summ, Wv) + bv
        scores_g = jnp.einsum('bne,bme->bnm', Qg, Kg) * SCALE
        attn_g = jax.nn.softmax(scores_g, axis=-1)
        global_out = jnp.einsum('bnm,bme->bne', attn_g, Vg)
        out = local + global_out[:, :, None, :]
        out = out.reshape(B, L, D)
        return jnp.einsum('bld,ed->ble', out, Wo) + bo

    def _L0_ffn_ref(x, ln_gamma, ln_beta, abel_w, abel_b, moe_gate_w, moe_gate_b, ew1, eb1, ew2, eb2, gens, gc_w, gc_b):
        import jax, jax.numpy as jnp
        import numpy as np
        from jax.scipy.linalg import expm
        B, S, D, E, K, NROT = (2, 256, 128, 8, 2, 3)
        EPS = 1e-05

        def _gelu(x):
            return jax.nn.gelu(x, approximate=False)

        def _forward(x, ln_gamma, ln_beta, abel_w, abel_b, moe_gate_w, moe_gate_b, ew1, eb1, ew2, eb2, gens, gc_w, gc_b):
            residual = x
            mu = jnp.mean(x, axis=-1, keepdims=True)
            var = jnp.mean((x - mu) ** 2, axis=-1, keepdims=True)
            xn = (x - mu) * jax.lax.rsqrt(var + EPS) * ln_gamma + ln_beta
            abel_out = _gelu(xn @ abel_w + abel_b)
            logits = xn @ moe_gate_w + moe_gate_b
            topw, topi = jax.lax.top_k(logits, K)
            topw = jax.nn.softmax(topw, axis=-1)
            w_dense = jnp.sum(jax.nn.one_hot(topi, E, dtype=xn.dtype) * topw[..., None], axis=-2)
            h = _gelu(jnp.einsum('bsd,edh->ebsh', xn, ew1) + eb1[:, None, None, :])
            eo = jnp.einsum('ebsh,ehd->ebsd', h, ew2) + eb2[:, None, None, :]
            moe_out = jnp.einsum('ebsd,bse->bsd', eo, w_dense)
            for i in range(NROT):
                moe_out = moe_out @ expm(gens[i])
            combined = jnp.concatenate([abel_out, moe_out], axis=-1)
            gate = jax.nn.sigmoid(combined @ gc_w + gc_b)
            mixed = abel_out * (1.0 - gate) + moe_out * gate
            return residual + mixed
        return _forward(x, ln_gamma, ln_beta, abel_w, abel_b, moe_gate_w, moe_gate_b, ew1, eb1, ew2, eb2, gens, gc_w, gc_b)

    def _L1_attn_ref(x, Wq, gq, bq, Wk, gk, bk, Wv, gv, bv, Wp, bp):
        import jax, jax.numpy as jnp
        import numpy as np
        DIM = 128
        NUM_HEADS = 16
        HEAD_DIM = DIM // NUM_HEADS
        TAU = 2.0
        V_TH = 1.0
        BN_EPS = 1e-05

        def _branch(x, W, gamma, beta):
            B, N, D = x.shape
            h = jnp.einsum('bnd,ed->bne', x, W)
            hf = h.reshape(B * N, D)
            mean = jnp.mean(hf, axis=0)
            var = jnp.var(hf, axis=0)
            hn = (hf - mean) * jax.lax.rsqrt(var + BN_EPS) * gamma + beta
            hn = hn.reshape(B, N, D)
            return jax.nn.sigmoid(4.0 * (hn - V_TH))

        def _heads(x):
            B, N, D = x.shape
            return x.reshape(B, N, NUM_HEADS, HEAD_DIM).transpose(0, 2, 1, 3)
        B, N, D = x.shape
        scale = HEAD_DIM ** (-0.5)
        q = _branch(x, Wq, gq, bq)
        k = _branch(x, Wk, gk, bk)
        v = _branch(x, Wv, gv, bv)
        qk = _heads(q * k) * scale
        v_h = _heads(v)
        vv = jnp.einsum('bhnd,bhne->bhde', v_h, v_h)
        out = jnp.einsum('bhnd,bhde->bhne', qk, vv)
        out = out.transpose(0, 2, 1, 3).reshape(B, N, D)
        return jnp.einsum('bnd,ed->bne', out, Wp) + bp

    def _L1_ffn_ref(x, router_w, router_b, weights1, bias1, weights2, bias2):
        import jax, jax.numpy as jnp
        import numpy as np
        B, K, D = (128, 32, 128)
        E = 32
        H = int(D * 0.25)

        def _rsqrt_uniform(key, shape, d):
            bound = d ** (-0.5)
            return jax.random.uniform(key, shape, jnp.float32, -bound, bound)
        b, k, d = x.shape
        x_flat = x.reshape(-1, d)
        n = x_flat.shape[0]
        logits = x_flat @ router_w.T + router_b
        routed_idx = jnp.argmax(logits, axis=-1)

        def expert_mlp(w1, b1, w2, b2):
            h = jax.nn.relu(x_flat @ w1 + b1)
            return jax.nn.relu(h @ w2 + b2)
        y_all = jax.vmap(expert_mlp)(weights1, bias1, weights2, bias2)
        out_flat = y_all[routed_idx, jnp.arange(n)]
        return out_flat.reshape(b, k, d)
    x = L0_attn_x
    x = x + 0.5 * _L0_ffn_ref(_layernorm(x, axis=-1), L0_ffn_ln_gamma, L0_ffn_ln_beta, L0_ffn_abel_w, L0_ffn_abel_b, L0_ffn_moe_gate_w, L0_ffn_moe_gate_b, L0_ffn_ew1, L0_ffn_eb1, L0_ffn_ew2, L0_ffn_eb2, L0_ffn_gens, L0_ffn_gc_w, L0_ffn_gc_b)
    x = x + _L0_attn_ref(_layernorm(x, axis=-1), L0_attn_Wq, L0_attn_bq, L0_attn_Wk, L0_attn_bk, L0_attn_Wv, L0_attn_bv, L0_attn_Wo, L0_attn_bo)
    x = x + 0.5 * _L0_ffn_ref(_layernorm(x, axis=-1), L0_ffn_ln_gamma, L0_ffn_ln_beta, L0_ffn_abel_w, L0_ffn_abel_b, L0_ffn_moe_gate_w, L0_ffn_moe_gate_b, L0_ffn_ew1, L0_ffn_eb1, L0_ffn_ew2, L0_ffn_eb2, L0_ffn_gens, L0_ffn_gc_w, L0_ffn_gc_b)
    x = x + 0.5 * _L1_ffn_ref(_layernorm(x, axis=-1), L1_ffn_router_w, L1_ffn_router_b, L1_ffn_weights1, L1_ffn_bias1, L1_ffn_weights2, L1_ffn_bias2)
    x = x + _L1_attn_ref(_layernorm(x, axis=-1), L1_attn_Wq, L1_attn_gq, L1_attn_bq, L1_attn_Wk, L1_attn_gk, L1_attn_bk, L1_attn_Wv, L1_attn_gv, L1_attn_bv, L1_attn_Wp, L1_attn_bp)
    x = x + 0.5 * _L1_ffn_ref(_layernorm(x, axis=-1), L1_ffn_router_w, L1_ffn_router_b, L1_ffn_weights1, L1_ffn_bias1, L1_ffn_weights2, L1_ffn_bias2)
    return x

_drawn_inputs = setup_inputs


def setup_inputs(seed=0):
    import zlib

    import numpy as np

    out = dict(_drawn_inputs(seed))
    spreads = {'L1_attn_gq': (1.0, 0.2),
     'L1_attn_bq': (0.0, 0.1),
     'L1_attn_gk': (1.0, 0.2),
     'L1_attn_bk': (0.0, 0.1),
     'L1_attn_gv': (1.0, 0.2),
     'L1_attn_bv': (0.0, 0.1),
     'L1_attn_bp': (0.0, 0.317)}
    factors = {'L0_attn_bq': 3.748,
     'L0_attn_bk': 64.0,
     'L0_attn_bo': 2.673,
     'L0_ffn_ln_gamma': 8.0,
     'L0_ffn_ln_beta': 8.0,
     'L0_ffn_abel_b': 8.0,
     'L0_ffn_moe_gate_w': 4.786,
     'L0_ffn_moe_gate_b': 8.0,
     'L0_ffn_ew1': 4.833,
     'L0_ffn_eb1': 8.0,
     'L0_ffn_ew2': 4.778,
     'L0_ffn_eb2': 8.0,
     'L0_ffn_gens': 8.0,
     'L0_ffn_gc_w': 8.0,
     'L1_ffn_router_b': 2.873,
     'L1_ffn_bias1': 24.639,
     'L1_ffn_bias2': 4.417}
    for name, (base, spread) in spreads.items():
        noise = np.random.default_rng([zlib.crc32(name.encode()), seed]).standard_normal(out[name].shape)
        drawn = base * np.exp(spread * noise) if base else spread * noise
        out[name] = jnp.asarray(drawn.astype(out[name].dtype))
    for name, factor in factors.items():
        out[name] = (out[name] * factor).astype(out[name].dtype)
    return out
```

```python
from contextlib import ExitStack

import concourse.bass as bass
from concourse import mybir

F32 = mybir.dt.float32
F32R = mybir.dt.float32r
U32 = mybir.dt.uint32
ALU = mybir.AluOpType
ACT = mybir.ActivationFunctionType
AX = mybir.AxisListType
RMAX = bass.bass_isa.ReduceOp.max

P = 128
BATCH, LENGTH = 2, 2048
TOKENS = BATCH * LENGTH
TILES = TOKENS // P
TPC = 4
CH = TPC * P
NCH = TOKENS // CH
EPS = 1e-5

E0, HC = 8, 2
U0 = E0 * HC
E1, H1 = 32, 32
EPU = P // H1
U1 = E1 // EPU
SEG = 32
SPT = P // SEG
SPC = CH // SEG
HEAD = 8
SCALE = HEAD ** -0.5
BLOCKED = 2.0 ** 100
NROT = 3
DEGREE = 11
SQUARINGS = 18

STAGES = ("ffn0", "attn0", "ffn0", "ffn1", "attn1", "ffn1")


def layout(*fields):
    at, out = 0, {}
    for name, width in fields:
        out[name] = slice(at, at + width)
        at += width
    return out, at


COL, NCOL = layout(("gamma", 1), ("beta", 1), ("eb1", U0), ("eb2", E0), ("bq", 1), ("bk", 1), ("bv", 1),
                   ("gq", 1), ("gk", 1), ("gv", 1), ("tq", 1), ("tk", 1), ("tv", 1), ("b1", U1))
ROW, NROW = layout(("gate_b", E0), ("abel_b", P), ("gate_abel", P), ("gate_moe", P), ("gc_b", 1), ("bo", P),
                   ("bp", P), ("router_b", E1))
MAT, NMAT = layout(("abel", P), ("gate", E0), ("q0", P), ("k0", P), ("v0", P), ("o0", P), ("q1", P), ("k1", P),
                   ("v1", P), ("p1", P), ("router", E1))


class Chip:

    def __init__(self, nc, ctx):
        self.nc, self.ctx, self.sems = nc, ctx, {}
        sb = self.sb
        self.bank = [ctx.enter_context(nc.psum_tensor(f"bank{i}", [P, CH], F32)) for i in range(8)]
        self.x = sb("x", [P, TILES, P])
        self.cols, self.rows, self.mats = sb("cols", [P, NCOL]), sb("rows", [P, NROW]), sb("mats", [P, NMAT])
        self.ew1_hi, self.ew1_lo = (sb(f"ew1_{k}", [P, U0, P], F32R) for k in ("hi", "lo"))
        self.ew2_hi, self.ew2_lo = (sb(f"ew2_{k}", [P, U0, P], F32R) for k in ("hi", "lo"))
        self.w1_hi, self.w1_lo = (sb(f"w1_{k}", [P, U1, P], F32R) for k in ("hi", "lo"))
        self.w2_hi, self.w2_lo = (sb(f"w2_{k}", [P, U1, P], F32R) for k in ("hi", "lo"))
        self.b2_hi, self.b2_lo = (sb(f"b2_{k}", [E1, P], F32R) for k in ("hi", "lo"))
        self.rotation = sb("rotation", [P, P])
        self.ident = sb("ident", [P, P])
        self.iota_row = sb("iota_row", [P, E1])
        self.neg_half = sb("neg_half", [P, 2 * TPC])
        self.half_gc_b = sb("half_gc_b", [P, 1])
        self.pick_expert = sb("pick_expert", [2 * E0, E0, P], F32R)
        self.block_expert = sb("block_expert", [E1, U1, P], F32R)
        self.stats = sb("stats", [P, TPC, 6])
        self.moments = sb("moments", [P, 2, TPC, 2])
        self.powed = sb("powed", [P, 2, TPC])
        self.r_std = sb("r_std", [P, 2, 2, TPC])
        self.mean_r = sb("mean_r", [P, TPC])
        self.keep_scale, self.keep_shift = sb("keep_scale", [P, 2, TPC]), sb("keep_shift", [P, 2, TPC])
        self.xs = sb("xs", [P, TPC, P])
        self.xt = sb("xt", [P, 2, CH])
        self.xt_hi, self.xt_lo = sb("xt_hi", [P, 2, CH], F32R), sb("xt_lo", [P, 2, CH], F32R)
        self.hid_hi, self.hid_lo = sb("hid_hi", [P, 8, CH], F32R), sb("hid_lo", [P, 8, CH], F32R)
        self.logits0, self.logits1 = sb("logits0", [P, TPC, E0]), sb("logits1", [P, TPC, E1])
        self.best, self.best_at = sb("best", [P, TPC, 8]), sb("best_at", [P, TPC, 8], U32)
        self.one_a, self.one_b, self.chosen = sb("one_a", [P, TPC, E0]), sb("one_b", [P, TPC, E0]), sb("chosen", [P, TPC, E1])
        self.pair, self.pair_w = sb("pair", [P, 2, TPC]), sb("pair_w", [P, 2, TPC])
        self.w_split, self.w_turned = sb("w_split", [P, TPC, 2 * E0], F32R), sb("w_turned", [2 * E0, 2, CH], F32R)
        self.chosen_t, self.blocked_t = sb("chosen_t", [E1, 2, CH], F32R), sb("blocked_t", [E1, 2, CH], F32R)
        self.gate = sb("gate", [P, 5, TPC])
        self.room = sb("room", [P, 3 * TOKENS])

    def sb(self, name, shape, dt=F32):
        return self.ctx.enter_context(self.nc.sbuf_tensor(name, shape, dt))

    def sem(self, name):
        if name not in self.sems:
            self.sems[name] = self.ctx.enter_context(self.nc.semaphore(name))
        return self.sems[name]

    def buf(self, name, shape, dt=F32):
        return self.sb(name, shape, dt)

    def rooms(self, *fields):
        at, out = 0, []
        for shape in fields:
            n = 1
            for k in shape:
                n *= k
            view = self.room[:, at:at + n]
            if len(shape) == 2:
                view = view.rearrange("p (a b) -> p a b", a=shape[0])
            if len(shape) == 3:
                view = view.rearrange("p (a b c) -> p a b c", a=shape[0], b=shape[1])
            out.append(view)
            at += n
        assert at <= 3 * TOKENS
        return out


def wait(eng, sem, value):
    if not (isinstance(value, int) and value <= 0):
        eng.wait_ge(sem, value)


def wait_alone(eng, sem, value, passed):
    if not (isinstance(value, int) and value <= 0):
        eng.wait_ge(sem, value)
        if not isinstance(value, int):
            eng.sem_inc(passed, 1)


def chunks(eng, body):
    body(0, 0)
    with eng.Fori(0, (NCH - 2) // 2) as i:
        body(2 * i + 1, 1)
        body(2 * i + 2, 0)
    body(NCH - 1, 1)


def chunks_two(eng, body):
    body(0, 0)
    body(1, 1)
    with eng.Fori(1, (NCH - 2) // 2) as i:
        body(2 * i, 0)
        body(2 * i + 1, 1)
    body(NCH - 2, 0)
    body(NCH - 1, 1)


def halves(eng, body):
    half = NCH // BATCH
    for b in range(BATCH):
        body(half * b, 0, b)
        body(half * b + 1, 1, b)
        with eng.Fori(half // 2 * b + 1, half // 2 * (b + 1)) as i:
            body(2 * i, 0, b)
            body(2 * i + 1, 1, b)


def known(c):
    return c if isinstance(c, int) else None


def across(ap, shape):
    return ap.to_broadcast(shape)



def setup(chip, args):
    nc, x = chip.nc, chip.x
    loaded_x, loaded_small, loaded_gens = chip.sem("loaded_x"), chip.sem("loaded_small"), chip.sem("loaded_gens")
    loaded_w, const_made = chip.sem("loaded_w"), chip.sem("const_made")
    hi_made, lo_made = chip.sem("hi_made"), chip.sem("lo_made")
    raw_ew1, raw_ew2, raw_w1, raw_w2, raw_b2, gens, gens_t, power, power_t, sums, rot12_t = chip.rooms(
        (U0, P), (U0, P), (U1, P), (U1, P), (1, P), (NROT, P), (NROT, P), (NROT, P), (NROT, P), (4, SQUARINGS), (1, P))
    threshold, over, factor = sums[:, 0, :], sums[:, 1, :], sums[:, 2, :]
    col_norm, norm, shrink = sums[:, 3, 0:NROT], sums[:, 3, 4:5], sums[:, 3, 5:6]
    over_bits = chip.sb("over_bits", [P, SQUARINGS], U32)
    col_max = sums[:, 3, 6:7]
    splits = [(raw_ew1, chip.ew1_hi[:], chip.ew1_lo[:]), (raw_ew2, chip.ew2_hi[:], chip.ew2_lo[:]),
              (raw_w1, chip.w1_hi[:], chip.w1_lo[:]), (raw_w2, chip.w2_hi[:], chip.w2_lo[:]),
              (raw_b2[0:E1, 0, :], chip.b2_hi[:], chip.b2_lo[:])]
    norm_step, all_norm, taylor_mm, taylor_done = (
        chip.sem(n) for n in ("norm_step", "all_norm", "taylor_mm", "taylor_done"))
    turned, turned_kept, squared, square_kept = (
        chip.sem(n) for n in ("turned", "turned_kept", "squared", "square_kept"))
    rot_mm, rot_kept = chip.sem("rot_mm"), chip.sem("rot_kept")
    NORM_STEPS = 6
    flat = "p i d -> p (i d)"
    exp_bank, turn_bank = chip.bank[0], chip.bank[1]

    with nc.Block() as block:
        @block.sync
        def _(sp):
            sp.dma_start(gens, args["gens"]).then_inc(loaded_gens, 16)
            sp.dma_start(gens_t, args["gens_t"]).then_inc(loaded_gens, 16)
            sp.dma_start(chip.cols[:], args["cols"]).then_inc(loaded_small, 16)
            sp.dma_start(chip.rows[:], args["rows"]).then_inc(loaded_small, 16)
            sp.dma_start(chip.mats[:], args["mats"]).then_inc(loaded_small, 16)
            sp.dma_start(x[:], args["x"].rearrange("(t p) d -> p t d", p=P)).then_inc(loaded_x, 16)
            for k, (dst, name) in enumerate(((raw_ew1, "ew1"), (raw_ew2, "ew2"), (raw_w1, "w1"), (raw_w2, "w2"))):
                sp.dma_start(dst, args[name]).then_inc(loaded_w, 16)
                sp.wait_ge(loaded_w, 16 * (k + 1))
            sp.dma_start(raw_b2[0:E1, 0, :], args["b2"]).then_inc(loaded_w, 16)
            sp.wait_ge(loaded_x, 16)
            sp.wait_ge(loaded_small, 48)
            sp.wait_ge(loaded_w, 16 * len(splits))

        @block.gpsimd
        def _(pool):
            raw_pick = raw_block = None
            nc.gpsimd.memset(chip.ident[:], 0.0).then_inc(const_made, 1)
            nc.gpsimd.memset(chip.neg_half[:], -0.5).then_inc(const_made, 1)
            nc.gpsimd.iota(chip.iota_row[:], [[1, E1]], base=0, channel_multiplier=0,
                           allow_small_or_imprecise_dtypes=True).then_inc(const_made, 1)
            for j in range(SQUARINGS):
                nc.gpsimd.memset(threshold[:, j:j + 1], 2.0 ** j).then_inc(const_made, 1)
            pool.wait_ge(const_made, 1)
            nc.gpsimd.affine_select(out=chip.ident[:], in_=chip.ident[:], compare_op=ALU.not_equal, fill=1.0, base=0,
                                    pattern=[[-1, P]], channel_multiplier=1).then_inc(const_made, 1)
            pool.wait_ge(norm_step, 2)
            nc.gpsimd.partition_all_reduce(norm, col_max, P, RMAX).then_inc(all_norm, 1)
        consts = 3 + SQUARINGS + 1

        @block.scalar
        def _(act):
            for k, (raw, hi, _) in enumerate(splits):
                act.wait_ge(loaded_w, 16 * (k + 1))
                nc.scalar.activation(hi, raw, ACT.Copy).then_inc(hi_made, 1)
            act.wait_ge(loaded_small, 48)
            nc.scalar.activation(chip.half_gc_b[:], chip.rows[:, ROW["gc_b"]], ACT.Copy, scale=0.5).then_inc(hi_made, 1)

        @block.vector
        def _(dve):
            dve.wait_ge(loaded_gens, 32)
            nc.vector.tensor_reduce(col_norm, gens_t, AX.X, ALU.add, apply_absolute_value=True).then_inc(norm_step, 1)
            dve.wait_ge(norm_step, 1)
            nc.vector.tensor_reduce(col_max, col_norm, AX.X, ALU.max).then_inc(norm_step, 1)
            dve.wait_ge(all_norm, 1)
            dve.wait_ge(const_made, consts)
            nc.vector.tensor_scalar(over, threshold, norm, None, ALU.is_lt).then_inc(norm_step, 1)
            dve.wait_ge(norm_step, 3)
            nc.vector.tensor_copy(over_bits[:], over).then_inc(norm_step, 1)
            nc.vector.tensor_scalar(factor, over, -0.5, 1.0, ALU.mult, ALU.add).then_inc(norm_step, 1)
            dve.wait_ge(norm_step, 5)
            nc.vector.tensor_reduce(shrink, factor, AX.X, ALU.mult).then_inc(norm_step, 1)
            dve.wait_ge(norm_step, 6)
            nc.vector.tensor_scalar(gens, gens, shrink, None, ALU.mult).then_inc(norm_step, 1)
            nc.vector.tensor_scalar(gens_t, gens_t, shrink, None, ALU.mult).then_inc(norm_step, 1)
            one = across(chip.ident[:].unsqueeze(1), [P, NROT, P])
            dve.wait_ge(norm_step, 8)
            nc.vector.scalar_tensor_tensor(out=power, in0=gens, scalar=1.0 / DEGREE, in1=one, op0=ALU.mult,
                                           op1=ALU.add).then_inc(taylor_done, 1)
            for k in range(DEGREE - 1, 0, -1):
                dve.wait_ge(taylor_mm, DEGREE - k)
                nc.vector.scalar_tensor_tensor(
                    out=power, in0=exp_bank[:, 0:NROT * P].rearrange("p (i d) -> p i d", i=NROT), scalar=1.0 / k,
                    in1=one, op0=ALU.mult, op1=ALU.add).then_inc(taylor_done, 1)
                if DEGREE - k <= len(splits):
                    n = DEGREE - k - 1
                    raw, hi, lo = splits[n]
                    dve.wait_ge(hi_made, n + 1)
                    nc.vector.tensor_tensor(lo, raw, hi.bitcast(F32), ALU.subtract).then_inc(lo_made, 1)
            for j in range(SQUARINGS):
                dve.wait_ge(turned, j + 1)
                nc.vector.tensor_copy(power_t, turn_bank[:, 0:NROT * P].rearrange("p (i d) -> p i d", i=NROT)).then_inc(
                    turned_kept, 1)
                dve.wait_ge(squared, j + 1)
                nc.vector.copy_predicated(power.rearrange(flat), across(over_bits[:, j:j + 1], [P, NROT * P]),
                                          exp_bank[:, 0:NROT * P]).then_inc(square_kept, 1)
            dve.wait_ge(turned, SQUARINGS + 1)
            nc.vector.tensor_copy(power_t, turn_bank[:, 0:NROT * P].rearrange("p (i d) -> p i d", i=NROT)).then_inc(
                turned_kept, 1)
            dve.wait_ge(rot_mm, 1)
            nc.vector.tensor_copy(rot12_t[:, 0, :], exp_bank[:, 0:P]).then_inc(rot_kept, 1)
            dve.wait_ge(rot_mm, 2)
            nc.vector.tensor_copy(chip.rotation[:], exp_bank[:, 0:P]).then_inc(rot_kept, 1)

        @block.tensor
        def _(pe):
            for k in range(1, DEGREE):
                pe.wait_ge(taylor_done, k)
                for i in range(NROT):
                    last = nc.tensor.matmul(exp_bank[:, i * P:(i + 1) * P], gens_t[:, i, :], power[:, i, :],
                                            start=True, stop=True)
                last.then_inc(taylor_mm, 1)
            pe.wait_ge(taylor_done, DEGREE)
            for j in range(SQUARINGS + 1):
                wait(pe, square_kept, j)
                for i in range(NROT):
                    last = nc.tensor.transpose(turn_bank[:, i * P:(i + 1) * P], power[:, i, :], chip.ident[:])
                last.then_inc(turned, 1)
                if j == SQUARINGS:
                    break
                pe.wait_ge(turned_kept, j + 1)
                for i in range(NROT):
                    last = nc.tensor.matmul(exp_bank[:, i * P:(i + 1) * P], power_t[:, i, :], power[:, i, :],
                                            start=True, stop=True)
                last.then_inc(squared, 1)
            pe.wait_ge(turned_kept, SQUARINGS + 1)
            nc.tensor.matmul(exp_bank[:, 0:P], power[:, 1, :], power_t[:, 0, :], start=True, stop=True).then_inc(
                rot_mm, 1)
            pe.wait_ge(rot_kept, 1)
            nc.tensor.matmul(exp_bank[:, 0:P], rot12_t[:, 0, :], power[:, 2, :], start=True, stop=True).then_inc(
                rot_mm, 1)


def setup_selectors(chip):
    nc = chip.nc
    sel_step, sel_made = chip.sem("sel_step"), chip.sem("sel_made")
    pick, block_rows = chip.rooms((E0, P), (U1, P))
    with nc.Block() as block:
        @block.gpsimd
        def _(pool):
            nc.gpsimd.memset(pick[0:2 * E0], 0.0).then_inc(sel_step, 1)
            nc.gpsimd.memset(block_rows[0:E1], 0.0).then_inc(sel_step, 1)
            pool.wait_ge(sel_step, 2)
            nc.gpsimd.affine_select(out=pick[0:2 * E0], in_=pick[0:2 * E0], compare_op=ALU.not_equal, fill=1.0,
                                    base=0, pattern=[[-1, E0], [0, P]], channel_multiplier=1).then_inc(sel_step, 1)
            nc.gpsimd.affine_select(out=block_rows[0:E1].rearrange("k u (q h) -> k u q h", q=EPU),
                                    in_=block_rows[0:E1].rearrange("k u (q h) -> k u q h", q=EPU),
                                    compare_op=ALU.not_equal, fill=BLOCKED, base=0,
                                    pattern=[[-EPU, U1], [-1, EPU], [0, H1]], channel_multiplier=1).then_inc(sel_step, 1)
            pool.wait_ge(sel_step, 4)
            nc.gpsimd.affine_select(out=pick[0:2 * E0], in_=pick[0:2 * E0], compare_op=ALU.not_equal, fill=1.0,
                                    base=-E0, pattern=[[-1, E0], [0, P]], channel_multiplier=1).then_inc(sel_step, 1)

        @block.vector
        def _(dve):
            dve.wait_ge(sel_step, 5)
            nc.vector.tensor_copy(chip.pick_expert[:], pick[0:2 * E0]).then_inc(sel_made, 1)
            nc.vector.tensor_copy(chip.block_expert[:], block_rows[0:E1]).then_inc(sel_made, 1)



class Head:

    def __init__(self, chip, name, base, turn_bank, twice, affine, split):
        self.chip, self.base, self.turn_bank = chip, base, turn_bank
        self.twice, self.affine, self.split = twice, affine, split
        s = chip.sem
        self.stats_done, self.moments_done = s(name + "_stats_done"), s(name + "_moments_done")
        self.r_step, self.xs_ready = s(name + "_r_step"), s(name + "_xs_ready")
        self.turned, self.xt_ready = s(name + "_turned"), s(name + "_xt_ready")
        self.r_steps = 6 if twice else 2
        self.xt_steps = 3 if split else 1

    def moments_step(self, dve, c, p):
        nc, chip, n = self.chip.nc, self.chip, self.base + c
        for t in range(TPC):
            nc.vector.bn_stats(chip.stats[:, t, :], chip.x[:, bass.ds(TPC * c + t, 1), :]).then_inc(self.stats_done, 1)
        wait_alone(dve, self.stats_done, TPC * n + TPC, chip.sem("dve_passed"))
        for t in range(TPC):
            nc.vector.bn_aggr(chip.moments[:, p, t, :], chip.stats[:, t, :]).then_inc(self.moments_done, 1)

    def power_step(self, pool, c, p):
        nc, chip, n = self.chip.nc, self.chip, self.base + c
        var = chip.moments[:, p, :, 1]
        pool.wait_ge(self.moments_done, TPC * n + TPC)
        wait_alone(pool, self.r_step, self.r_steps * n, chip.sem("pool_passed"))
        nc.gpsimd.tensor_scalar(chip.powed[:, 0, :], var, 1.0, EPS, ALU.mult, ALU.add).then_inc(self.r_step, 1)
        k = 1
        if self.twice:
            nc.gpsimd.tensor_scalar(chip.powed[:, 1, :], var, 1.0 + EPS, EPS * EPS, ALU.mult, ALU.add).then_inc(
                self.r_step, 1)
            k = 2
        pool.wait_ge(self.r_step, self.r_steps * n + k)
        nc.gpsimd.tensor_tensor(chip.r_std[:, p, 0:k, :], chip.powed[:, 0:k, :],
                                chip.neg_half[:, 0:k * TPC].rearrange("p (a t) -> p a t", a=k), ALU.pow).then_inc(
                                    self.r_step, 1)
        if self.twice:
            pool.wait_ge(self.r_step, self.r_steps * n + 3)
            nc.gpsimd.tensor_tensor(chip.mean_r[:], chip.moments[:, p, :, 0], chip.r_std[:, p, 0, :],
                                    ALU.mult).then_inc(self.r_step, 1)
            nc.gpsimd.tensor_scalar(chip.keep_scale[:, p, :], chip.r_std[:, p, 0, :], 0.5, 1.0, ALU.mult,
                                    ALU.add).then_inc(self.r_step, 1)
            wait_alone(pool, self.r_step, self.r_steps * n + 4, chip.sem("pool_passed"))
            nc.gpsimd.tensor_scalar(chip.keep_shift[:, p, :], chip.mean_r[:], -0.5, 0.0, ALU.mult,
                                    ALU.add).then_inc(self.r_step, 1)

    def normed_step(self, dve, c, p):
        nc, chip, n = self.chip.nc, self.chip, self.base + c
        dve.wait_ge(self.r_step, self.r_steps * n + self.r_steps)
        for t in range(TPC):
            nc.vector.tensor_scalar(chip.xs[:, t, :].unsqueeze(1), chip.x[:, bass.ds(TPC * c + t, 1), :],
                                    chip.moments[:, p, t, 0:1], chip.r_std[:, p, int(self.twice), t:t + 1],
                                    ALU.subtract, ALU.mult).then_inc(self.xs_ready, 1)

    def turn_step(self, pe, c, p):
        nc, chip, n = self.chip.nc, self.chip, self.base + c
        pe.wait_ge(self.xs_ready, TPC * n + TPC)
        for t in range(TPC):
            last = nc.tensor.transpose(self.turn_bank[:, t * P:(t + 1) * P], chip.xs[:, t, :], chip.ident[:])
        last.then_inc(self.turned, 1)

    def keep_step(self, dve, c, p):
        nc, chip, n = self.chip.nc, self.chip, self.base + c
        dve.wait_ge(self.turned, n + 1)
        if self.affine:
            nc.vector.tensor_scalar(chip.xt[:, p, :], self.turn_bank[:], chip.cols[:, COL["gamma"]],
                                    chip.cols[:, COL["beta"]], ALU.mult, ALU.add).then_inc(self.xt_ready, 1)
        else:
            nc.vector.tensor_copy(chip.xt[:, p, :], self.turn_bank[:]).then_inc(self.xt_ready, 1)
        if self.split:
            dve.wait_ge(self.xt_ready, self.xt_steps * n + 1)
            nc.vector.tensor_copy(chip.xt_hi[:, p, :], chip.xt[:, p, :]).then_inc(self.xt_ready, 1)
            dve.wait_ge(self.xt_ready, self.xt_steps * n + 2)
            nc.vector.tensor_tensor(chip.xt_lo[:, p, :], chip.xt[:, p, :], chip.xt_hi[:, p, :].bitcast(F32),
                                    ALU.subtract).then_inc(self.xt_ready, 1)

    def wait_xt(self, eng, c):
        eng.wait_ge(self.xt_ready, self.xt_steps * (self.base + c) + self.xt_steps)



def ffn0_stage(chip, call):
    nc, x = chip.nc, chip.x
    base = call * NCH

    def s(name):
        return chip.sem("ffn0_" + name)

    H, OUT, WIDE, TURN, ROT, ABEL = (0, 1), (2, 3), 4, 5, 6, 7
    head = Head(chip, "ffn0", base, chip.bank[TURN], twice=True, affine=True, split=True)
    LAG = 2
    hid, wide_w, weighted, moe, abel, abel_pre, kept, diff, dots_a, dots_b = chip.rooms(
        (4, CH), (4, CH), (2, CH), (2, CH), (2, CH), (CH,), (TPC, P), (TPC, P), (TPC, P), (TPC, P))
    tiles = "p (t d) -> p t d"

    hid_done, gelu_done, hi_done = s("hid_done"), s("gelu_done"), s("hi_done")
    lo_even, lo_odd = s("lo_even"), s("lo_odd")
    wide_mm, wide_ready, out_done = s("wide_mm"), s("wide_ready"), s("out_done")
    weighted_done, moe_added = s("weighted_done"), s("moe_added")
    logits_done, route_step, pair_tanh = s("logits_done"), s("route_step"), s("pair_tanh")
    w_turn, w_kept = s("w_turn"), s("w_kept")
    abel_mm, abel_biased, abel_done = s("abel_mm"), s("abel_biased"), s("abel_done")
    rot_mm, tail_step, gate_tanh, x_new, kept_done = (
        s("rot_mm"), s("tail_step"), s("gate_tanh"), s("x_new"), s("kept_done"))
    PAIR = TPC + 2
    ROUTE = PAIR + TPC + 2 + 2 + 2 + 3
    DOTS = 2 * TPC + 1
    TAIL = DOTS + 3

    with nc.Block() as block:
        @block.tensor
        def _(pe):
            def logits_step(c, p):
                head.wait_xt(pe, c)
                for t in range(TPC):
                    last = nc.tensor.matmul(chip.bank[TURN][:, t * E0:(t + 1) * E0], chip.xt[:, p, t * P:(t + 1) * P],
                                            chip.mats[:, MAT["gate"]], start=True, stop=True)
                last.then_inc(logits_done, 1)

            def w_turn_step(c):
                pe.wait_ge(route_step, ROUTE * (base + c) + ROUTE)
                for t in range(TPC):
                    last = nc.tensor.transpose(chip.bank[TURN][0:2 * E0, t * P:(t + 1) * P],
                                               chip.w_split[:, t, :].bitcast(F32), chip.ident[:])
                last.then_inc(w_turn, 1)

            def hidden(c, p, e):
                if e == 0:
                    head.wait_xt(pe, c)
                for j in range(HC):
                    u = HC * e + j
                    wait(pe, gelu_done, U0 * (base + c) + u - 1)
                    for k, (w, v) in enumerate(((chip.ew1_hi, chip.xt_hi), (chip.ew1_hi, chip.xt_lo),
                                                (chip.ew1_lo, chip.xt_hi))):
                        last = nc.tensor.matmul(chip.bank[H[u % 2]][:], w[:, u, :], v[:, p, :], start=k == 0,
                                                stop=k == 2)
                    last.then_inc(hid_done, 1)

            def widen(c, p, e):
                if e == 0:
                    pe.wait_ge(w_kept, base + c + 1)
                wait(pe, wide_ready, E0 * (base + c) + e)
                nc.tensor.matmul(chip.bank[WIDE][:], chip.pick_expert[:, e, :], chip.w_turned[:, p, :], start=True,
                                 stop=True).then_inc(wide_mm, 1)

            def out_product(c, e):
                n = E0 * (base + c) + e
                pe.wait_ge(lo_even, n + 1)
                pe.wait_ge(lo_odd, n + 1)
                wait(pe, weighted_done, n - 1)
                k = 0
                for j in range(HC):
                    u = HC * e + j
                    for w, v in ((chip.ew2_hi, chip.hid_hi), (chip.ew2_hi, chip.hid_lo), (chip.ew2_lo, chip.hid_hi)):
                        last = nc.tensor.matmul(chip.bank[OUT[e % 2]][:], w[:, u, :], v[:, u % 8, :], start=k == 0,
                                                stop=k == 5)
                        k += 1
                last.then_inc(out_done, 1)

            def abel_step(c, p):
                wait(pe, abel_biased, base + c)
                for t in range(TPC):
                    last = nc.tensor.matmul(chip.bank[ABEL][:, t * P:(t + 1) * P], chip.xt[:, p, t * P:(t + 1) * P],
                                            chip.mats[:, MAT["abel"]], start=True, stop=True)
                last.then_inc(abel_mm, 1)

            def rot_step(c, p):
                pe.wait_ge(moe_added, (E0 - 1) * (base + c) + E0 - 1)
                for t in range(TPC):
                    last = nc.tensor.matmul(chip.bank[ROT][:, t * P:(t + 1) * P], moe[:, p, t * P:(t + 1) * P],
                                            chip.rotation[:], start=True, stop=True)
                last.then_inc(rot_mm, 1)

            def body(c, p):
                for e in range(E0):
                    hidden(c, p, e)
                    widen(c, p, e)
                    if e >= LAG:
                        out_product(c, e - LAG)
                    elif known(c) != 0:
                        out_product(c - 1, e - LAG + E0)
                    if e == 1:
                        abel_step(c, p)
                    if e == 3 and known(c) != 0:
                        rot_step(c - 1, 1 - p)
                    if known(c) != NCH - 1:
                        if e == 2:
                            wait(pe, w_kept, base + c + 1)
                            head.turn_step(pe, c + 1, 1 - p)
                        if e == 4:
                            logits_step(c + 1, 1 - p)
                        if e == 7:
                            w_turn_step(c + 1)

            head.turn_step(pe, 0, 0)
            logits_step(0, 0)
            w_turn_step(0)
            chunks(pe, body)
            for e in range(E0 - LAG, E0):
                out_product(NCH - 1, e)
            rot_step(NCH - 1, 1)

        @block.scalar
        def _(act):
            def hidden(c, e):
                n = E0 * (base + c) + e
                for j in range(HC):
                    u = HC * e + j
                    act.wait_ge(hid_done, HC * n + j + 1)
                    wait(act, lo_odd if j else lo_even, n - 1)
                    nc.scalar.activation(hid[:, u % 4, :], chip.bank[H[u % 2]][:], ACT.Gelu,
                                         bias=chip.cols[:, COL["eb1"]][:, u:u + 1]).then_inc(gelu_done, 1)
                wait(act, out_done, n - 3)
                for j in range(HC):
                    u = HC * e + j
                    act.wait_ge(gelu_done, HC * n + j + 1)
                    nc.scalar.activation(chip.hid_hi[:, u % 8, :], hid[:, u % 4, :], ACT.Copy).then_inc(hi_done, 1)

            def widen(c, e):
                n = E0 * (base + c) + e
                act.wait_ge(wide_mm, n + 1)
                wait(act, weighted_done, n - 3)
                nc.scalar.activation(wide_w[:, e % 4, :], chip.bank[WIDE][:], ACT.Copy).then_inc(wide_ready, 1)

            def pair_step(c):
                act.wait_ge(route_step, ROUTE * (base + c) + PAIR)
                nc.scalar.activation(chip.pair[:, 1, :], chip.pair[:, 0, :], ACT.Tanh, scale=0.5).then_inc(pair_tanh, 1)

            def w_kept_step(c, p):
                act.wait_ge(w_turn, base + c + 1)
                nc.scalar.activation(chip.w_turned[:, p, :], chip.bank[TURN][0:2 * E0, :], ACT.Copy).then_inc(w_kept, 1)

            def abel_step(c, p):
                act.wait_ge(abel_biased, base + c + 1)
                nc.scalar.activation(abel[:, p, :], abel_pre, ACT.Gelu).then_inc(abel_done, 1)

            def gate_step(c):
                act.wait_ge(tail_step, TAIL * (base + c) + DOTS)
                nc.scalar.activation(chip.gate[:, 3, :], chip.gate[:, 2, :], ACT.Tanh, scale=0.5,
                                     bias=chip.half_gc_b[:]).then_inc(gate_tanh, 1)

            def body(c, p):
                for e in range(E0):
                    hidden(c, e)
                    widen(c, e)
                    if e == 3:
                        abel_step(c, p)
                    if e == 4 and known(c) != 0:
                        gate_step(c - 1)
                    if known(c) != NCH - 1:
                        if e == 5:
                            pair_step(c + 1)
                        if e == 7:
                            w_kept_step(c + 1, 1 - p)

            nc.scalar.preload_act_table(ACT.Gelu)
            pair_step(0)
            w_kept_step(0, 0)
            chunks(act, body)
            gate_step(NCH - 1)

        @block.vector
        def _(dve):
            def route_pair(c):
                r = ROUTE * (base + c)
                dve.wait_ge(logits_done, base + c + 1)
                wait(dve, route_step, r)
                nc.vector.tensor_tensor(chip.logits0[:], chip.bank[TURN][:, 0:TPC * E0].rearrange(
                    "p (t e) -> p t e", t=TPC), across(chip.rows[:, ROW["gate_b"]].unsqueeze(1), [P, TPC, E0]),
                    ALU.add).then_inc(route_step, 1)
                wait_alone(dve, route_step, r + 1, chip.sem("dve_passed"))
                for t in range(TPC):
                    nc.vector.max(chip.best[:, t, :], chip.logits0[:, t, :]).then_inc(route_step, 1)
                dve.wait_ge(route_step, r + 1 + TPC)
                nc.vector.tensor_tensor(chip.pair[:, 0, :], chip.best[:, :, 1], chip.best[:, :, 0],
                                        ALU.subtract).then_inc(route_step, 1)
                for t in range(TPC):
                    nc.vector.max_index(chip.best_at[:, t, :], chip.best[:, t, :], chip.logits0[:, t, :]).then_inc(
                        route_step, 1)
                dve.wait_ge(route_step, r + PAIR + TPC)
                for k, one in enumerate((chip.one_a, chip.one_b)):
                    nc.vector.tensor_tensor(one[:], across(chip.iota_row[:, 0:E0].unsqueeze(1), [P, TPC, E0]),
                                            across(chip.best_at[:, :, k:k + 1], [P, TPC, E0]), ALU.is_equal).then_inc(
                                                route_step, 1)

            def route_weights(c):
                r = ROUTE * (base + c) + PAIR + TPC + 2
                dve.wait_ge(pair_tanh, base + c + 1)
                for k, sign in enumerate((-0.5, 0.5)):
                    nc.vector.tensor_scalar(chip.pair_w[:, k, :], chip.pair[:, 1, :], sign, 0.5, ALU.mult,
                                            ALU.add).then_inc(route_step, 1)
                dve.wait_ge(route_step, r + 2)
                for k, one in enumerate((chip.one_a, chip.one_b)):
                    nc.vector.tensor_tensor(one[:], one[:], across(chip.pair_w[:, k, :].unsqueeze(2), [P, TPC, E0]),
                                            ALU.mult).then_inc(route_step, 1)
                dve.wait_ge(route_step, r + 4)
                nc.vector.tensor_tensor(chip.one_a[:], chip.one_a[:], chip.one_b[:], ALU.add).then_inc(route_step, 1)
                dve.wait_ge(route_step, r + 5)
                wait(dve, w_turn, base + c)
                nc.vector.tensor_copy(chip.w_split[:, :, 0:E0], chip.one_a[:]).then_inc(route_step, 1)
                dve.wait_ge(route_step, r + 6)
                nc.vector.tensor_tensor(chip.w_split[:, :, E0:2 * E0], chip.one_a[:],
                                        chip.w_split[:, :, 0:E0].bitcast(F32), ALU.subtract).then_inc(route_step, 1)

            def low(c, e):
                u = HC * e
                dve.wait_ge(hi_done, U0 * (base + c) + u + 1)
                nc.vector.tensor_tensor(chip.hid_lo[:, u % 8, :], hid[:, u % 4, :],
                                        chip.hid_hi[:, u % 8, :].bitcast(F32), ALU.subtract).then_inc(lo_even, 1)

            def weigh(c, p, e):
                n = E0 * (base + c) + e
                dve.wait_ge(out_done, n + 1)
                dve.wait_ge(wide_ready, n + 1)
                if e:
                    wait(dve, moe_added, (E0 - 1) * (base + c) + max(e - 2, 0))
                nc.vector.scalar_tensor_tensor(out=weighted[:, e % 2, :] if e else moe[:, p, :],
                                               in0=chip.bank[OUT[e % 2]][:],
                                               scalar=chip.cols[:, COL["eb2"]][:, e:e + 1], in1=wide_w[:, e % 4, :],
                                               op0=ALU.add, op1=ALU.mult).then_inc(weighted_done, 1)

            def abel_bias(c):
                dve.wait_ge(abel_mm, base + c + 1)
                wait(dve, abel_done, base + c)
                nc.vector.tensor_tensor(abel_pre.rearrange(tiles, t=TPC), chip.bank[ABEL][:].rearrange(tiles, t=TPC),
                                        across(chip.rows[:, ROW["abel_b"]].unsqueeze(1), [P, TPC, P]),
                                        ALU.add).then_inc(abel_biased, 1)

            def keep_input(c, p):
                wait(dve, x_new, TPC * (base + c))
                for t in range(TPC):
                    nc.vector.tensor_scalar(kept[:, t, :].unsqueeze(1), x[:, bass.ds(TPC * c + t, 1), :],
                                            chip.keep_scale[:, p, t:t + 1], chip.keep_shift[:, p, t:t + 1],
                                            ALU.mult, ALU.add).then_inc(kept_done, 1)

            def gate_dots(c, p):
                r = TAIL * (base + c)
                abel_t = abel[:, p, :].rearrange(tiles, t=TPC)
                moe_t = chip.bank[ROT][:].rearrange(tiles, t=TPC)
                dve.wait_ge(abel_done, base + c + 1)
                dve.wait_ge(kept_done, TPC * (base + c) + TPC)
                dve.wait_ge(rot_mm, base + c + 1)
                wait(dve, tail_step, r)
                for k, (v, w, dots) in enumerate(((abel_t, "gate_abel", dots_a), (moe_t, "gate_moe", dots_b))):
                    for t in range(TPC):
                        nc.vector.tensor_tensor_reduce(
                            out=dots[:, t, :], in0=v[:, t, :], in1=chip.rows[:, ROW[w]], scale=1.0, scalar=0.0,
                            op0=ALU.mult, op1=ALU.add, accum_out=chip.gate[:, k, t:t + 1]).then_inc(tail_step, 1)
                dve.wait_ge(tail_step, r + 2 * TPC)
                nc.vector.tensor_tensor(chip.gate[:, 2, :], chip.gate[:, 0, :], chip.gate[:, 1, :],
                                        ALU.add).then_inc(tail_step, 1)
                nc.vector.tensor_tensor(diff, moe_t, abel_t, ALU.subtract).then_inc(tail_step, 1)
                nc.vector.scalar_tensor_tensor(out=kept.rearrange("p t d -> p (t d)"), in0=abel[:, p, :], scalar=0.5,
                                               in1=kept.rearrange("p t d -> p (t d)"), op0=ALU.mult,
                                               op1=ALU.add).then_inc(tail_step, 1)

            def mix(c):
                r = TAIL * (base + c)
                dve.wait_ge(gate_tanh, base + c + 1)
                nc.vector.tensor_scalar(chip.gate[:, 4, :], chip.gate[:, 3, :], 0.25, 0.25, ALU.mult,
                                        ALU.add).then_inc(tail_step, 1)
                dve.wait_ge(tail_step, r + TAIL)
                for t in range(TPC):
                    nc.vector.scalar_tensor_tensor(out=x[:, bass.ds(TPC * c + t, 1), :], in0=diff[:, t:t + 1, :],
                                                   scalar=chip.gate[:, 4, t:t + 1], in1=kept[:, t:t + 1, :],
                                                   op0=ALU.mult, op1=ALU.add).then_inc(x_new, 1)

            def body(c, p):
                for e in range(E0):
                    low(c, e)
                    if e >= LAG:
                        weigh(c, p, e - LAG)
                    elif known(c) != 0:
                        weigh(c - 1, 1 - p, e - LAG + E0)
                    if e == 2:
                        abel_bias(c)
                    if e == 4 and known(c) != 0:
                        gate_dots(c - 1, 1 - p)
                    if e == 5 and known(c) != 0:
                        mix(c - 1)
                    if e == 6:
                        keep_input(c, p)
                    if known(c) != NCH - 1:
                        if e == 0:
                            head.moments_step(dve, c + 1, 1 - p)
                        if e == 2:
                            head.normed_step(dve, c + 1, 1 - p)
                        if e == 3:
                            head.keep_step(dve, c + 1, 1 - p)
                        if e == 5:
                            route_pair(c + 1)
                        if e == 6:
                            route_weights(c + 1)

            head.moments_step(dve, 0, 0)
            head.normed_step(dve, 0, 0)
            head.keep_step(dve, 0, 0)
            route_pair(0)
            route_weights(0)
            chunks(dve, body)
            for e in range(E0 - LAG, E0):
                weigh(NCH - 1, 1, e)
            gate_dots(NCH - 1, 1)
            mix(NCH - 1)

        @block.gpsimd
        def _(pool):
            def low(c, e):
                u = HC * e + 1
                pool.wait_ge(hi_done, U0 * (base + c) + u + 1)
                nc.gpsimd.tensor_tensor(chip.hid_lo[:, u % 8, :], hid[:, u % 4, :],
                                        chip.hid_hi[:, u % 8, :].bitcast(F32), ALU.subtract).then_inc(lo_odd, 1)

            def add(c, p, e):
                if e == 0:
                    return
                pool.wait_ge(weighted_done, E0 * (base + c) + e + 1)
                wait(pool, moe_added, (E0 - 1) * (base + c) + e - 1)
                nc.gpsimd.tensor_tensor(moe[:, p, :], moe[:, p, :], weighted[:, e % 2, :], ALU.add).then_inc(
                    moe_added, 1)

            def body(c, p):
                for e in range(E0):
                    low(c, e)
                    if e >= LAG:
                        add(c, p, e - LAG)
                    elif known(c) != 0:
                        add(c - 1, 1 - p, e - LAG + E0)
                    if e == 0 and known(c) != NCH - 1:
                        head.power_step(pool, c + 1, 1 - p)

            head.power_step(pool, 0, 0)
            chunks(pool, body)
            for e in range(E0 - LAG, E0):
                add(NCH - 1, 1, e)



def ffn1_stage(chip, call, out, last_call):
    nc, x = chip.nc, chip.x
    base = call * NCH

    def s(name):
        return chip.sem("ffn1_" + name)

    H, SUM, TURN, LOGITS, BACK = (0, 1), (2, 3), 4, 5, 6
    head = Head(chip, "ffn1", base, chip.bank[TURN], twice=False, affine=False, split=True)
    LAG = 2
    hid, y_t = chip.rooms((4, CH), (CH,))
    tiles = "p (t d) -> p t d"

    hid_done, relu_done, hi_done = s("hid_done"), s("relu_done"), s("hi_done")
    lo_even, lo_odd, out_mm, sum_done = s("lo_even"), s("lo_odd"), s("out_mm"), s("sum_done")
    logits_done, route_step, one_turn, one_kept, blocked_made = (
        s("logits_done"), s("route_step"), s("one_turn"), s("one_kept"), s("blocked_made"))
    y_ready, back_done, x_new, stored = s("y_ready"), s("back_done"), s("x_new"), s("stored")
    ROUTE = 2 + 2 * TPC

    with nc.Block() as block:
        @block.sync
        def _(sp):
            if not last_call:
                return
            for c in range(NCH):
                sp.wait_ge(x_new, base + c + 1)
                sp.dma_start(out[c * CH:(c + 1) * CH, :].rearrange("(t p) d -> p t d", p=P),
                             x[:, c * TPC:(c + 1) * TPC, :]).then_inc(stored, 16)
            sp.wait_ge(stored, 16 * NCH)

        @block.tensor
        def _(pe):
            def logits_step(c, p):
                head.wait_xt(pe, c)
                for t in range(TPC):
                    last = nc.tensor.matmul(chip.bank[LOGITS][:, t * E1:(t + 1) * E1], chip.xt[:, p, t * P:(t + 1) * P],
                                            chip.mats[:, MAT["router"]], start=True, stop=True)
                last.then_inc(logits_done, 1)

            def one_turn_step(c):
                pe.wait_ge(route_step, ROUTE * (base + c) + ROUTE)
                for t in range(TPC):
                    last = nc.tensor.transpose(chip.bank[TURN][0:E1, t * P:(t + 1) * P], chip.chosen[:, t, :],
                                               chip.ident[:])
                last.then_inc(one_turn, 1)

            def hidden(c, p, u):
                if u == 0:
                    head.wait_xt(pe, c)
                    pe.wait_ge(blocked_made, base + c + 1)
                wait(pe, relu_done, U1 * (base + c) + u - 1)
                b = chip.bank[H[u % 2]]
                nc.tensor.matmul(b[:], chip.block_expert[:, u, :], chip.blocked_t[:, p, :], start=True, stop=False)
                for k, (w, v) in enumerate(((chip.w1_hi, chip.xt_hi), (chip.w1_hi, chip.xt_lo),
                                            (chip.w1_lo, chip.xt_hi))):
                    last = nc.tensor.matmul(b[:], w[:, u, :], v[:, p, :], start=False, stop=k == 2)
                last.then_inc(hid_done, 1)

            def out_product(c, p, u):
                n = U1 * (base + c) + u
                if u % 2:
                    pe.wait_ge(lo_odd, U1 // 2 * (base + c) + u // 2 + 1)
                else:
                    pe.wait_ge(lo_even, U1 // 2 * (base + c) + u // 2 + 1)
                b = chip.bank[SUM[p]]
                for k, (w, v) in enumerate(((chip.w2_hi, chip.hid_hi), (chip.w2_hi, chip.hid_lo),
                                            (chip.w2_lo, chip.hid_hi))):
                    last = nc.tensor.matmul(b[:], w[:, u, :], v[:, u, :], start=u == 0 and k == 0, stop=False)
                last.then_inc(out_mm, 1)
                if u == U1 - 1:
                    nc.tensor.matmul(b[:], chip.b2_hi[:], chip.chosen_t[:, p, :], start=False, stop=False)
                    nc.tensor.matmul(b[:], chip.b2_lo[:], chip.chosen_t[:, p, :], start=False, stop=True).then_inc(
                        sum_done, 1)

            def back_step(c):
                pe.wait_ge(y_ready, base + c + 1)
                wait(pe, x_new, base + c)
                for t in range(TPC):
                    last = nc.tensor.transpose(chip.bank[BACK][:, t * P:(t + 1) * P], y_t[:, t * P:(t + 1) * P],
                                               chip.ident[:])
                last.then_inc(back_done, 1)

            def body(c, p):
                for u in range(U1):
                    hidden(c, p, u)
                    if u >= LAG:
                        out_product(c, p, u - LAG)
                    elif known(c) != 0:
                        out_product(c - 1, 1 - p, u - LAG + U1)
                    if u == 3 and known(c) != 0:
                        back_step(c - 1)
                    if known(c) != NCH - 1:
                        if u == 2:
                            wait(pe, one_kept, base + c + 1)
                            head.turn_step(pe, c + 1, 1 - p)
                        if u == 4:
                            logits_step(c + 1, 1 - p)
                        if u == 7:
                            one_turn_step(c + 1)

            head.turn_step(pe, 0, 0)
            logits_step(0, 0)
            one_turn_step(0)
            chunks(pe, body)
            for u in range(U1 - LAG, U1):
                out_product(NCH - 1, 1, u)
            back_step(NCH - 1)

        @block.scalar
        def _(act):
            def hidden(c, u):
                n = U1 * (base + c) + u
                act.wait_ge(hid_done, n + 1)
                wait(act, lo_odd if u % 2 else lo_even, U1 // 2 * (base + c) + u // 2 - 1)
                nc.scalar.activation(hid[:, u % 4, :], chip.bank[H[u % 2]][:], ACT.Relu,
                                     bias=chip.cols[:, COL["b1"]][:, u:u + 1]).then_inc(relu_done, 1)
                wait(act, out_mm, n - 7)
                act.wait_ge(relu_done, n + 1)
                nc.scalar.activation(chip.hid_hi[:, u, :], hid[:, u % 4, :], ACT.Copy).then_inc(hi_done, 1)

            def one_kept_step(c, p):
                act.wait_ge(one_turn, base + c + 1)
                nc.scalar.activation(chip.chosen_t[:, p, :], chip.bank[TURN][0:E1, :], ACT.Copy).then_inc(one_kept, 1)

            def y_step(c, p):
                act.wait_ge(sum_done, base + c + 1)
                wait(act, back_done, base + c)
                nc.scalar.activation(y_t, chip.bank[SUM[p]][:], ACT.Relu).then_inc(y_ready, 1)

            def body(c, p):
                for u in range(U1):
                    hidden(c, u)
                    if u == 2 and known(c) != 0:
                        y_step(c - 1, 1 - p)
                    if u == 7 and known(c) != NCH - 1:
                        one_kept_step(c + 1, 1 - p)

            nc.scalar.preload_act_table(ACT.Relu)
            one_kept_step(0, 0)
            chunks(act, body)
            y_step(NCH - 1, 1)

        @block.vector
        def _(dve):
            def route(c):
                r = ROUTE * (base + c)
                dve.wait_ge(logits_done, base + c + 1)
                wait(dve, route_step, r)
                nc.vector.tensor_tensor(chip.logits1[:], chip.bank[LOGITS][:, 0:TPC * E1].rearrange(
                    "p (t e) -> p t e", t=TPC), across(chip.rows[:, ROW["router_b"]].unsqueeze(1), [P, TPC, E1]),
                    ALU.add).then_inc(route_step, 1)
                wait_alone(dve, route_step, r + 1, chip.sem("dve_passed"))
                for t in range(TPC):
                    nc.vector.max(chip.best[:, t, :], chip.logits1[:, t, :]).then_inc(route_step, 1)
                wait_alone(dve, route_step, r + 1 + TPC, chip.sem("dve_passed"))
                for t in range(TPC):
                    nc.vector.max_index(chip.best_at[:, t, :], chip.best[:, t, :], chip.logits1[:, t, :]).then_inc(
                        route_step, 1)
                dve.wait_ge(route_step, r + 1 + 2 * TPC)
                wait(dve, one_turn, base + c)
                nc.vector.tensor_tensor(chip.chosen[:], across(chip.iota_row[:].unsqueeze(1), [P, TPC, E1]),
                                        across(chip.best_at[:, :, 0:1], [P, TPC, E1]), ALU.is_equal).then_inc(
                                            route_step, 1)

            def block_step(c, p):
                dve.wait_ge(one_kept, base + c + 1)
                nc.vector.tensor_scalar(chip.blocked_t[:, p, :], chip.chosen_t[:, p, :].bitcast(F32), -1.0, None,
                                        ALU.add).then_inc(blocked_made, 1)

            def low(c, u):
                dve.wait_ge(hi_done, U1 * (base + c) + u + 1)
                nc.vector.tensor_tensor(chip.hid_lo[:, u, :], hid[:, u % 4, :], chip.hid_hi[:, u, :].bitcast(F32),
                                        ALU.subtract).then_inc(lo_even, 1)

            def add_step(c):
                dve.wait_ge(back_done, base + c + 1)
                tile = x[:, bass.ds(TPC * c, TPC), :]
                nc.vector.scalar_tensor_tensor(out=tile, in0=chip.bank[BACK][:].rearrange(tiles, t=TPC), scalar=0.5,
                                               in1=tile, op0=ALU.mult, op1=ALU.add).then_inc(x_new, 1)

            def body(c, p):
                for u in range(U1):
                    if u % 2 == 0:
                        low(c, u)
                    if u == 4 and known(c) != 0:
                        add_step(c - 1)
                    if known(c) != NCH - 1:
                        if u == 0:
                            head.moments_step(dve, c + 1, 1 - p)
                        if u == 2:
                            head.normed_step(dve, c + 1, 1 - p)
                        if u == 3:
                            head.keep_step(dve, c + 1, 1 - p)
                        if u == 5:
                            route(c + 1)
                        if u == 7:
                            block_step(c + 1, 1 - p)

            head.moments_step(dve, 0, 0)
            head.normed_step(dve, 0, 0)
            head.keep_step(dve, 0, 0)
            route(0)
            block_step(0, 0)
            chunks(dve, body)
            add_step(NCH - 1)

        @block.gpsimd
        def _(pool):
            def low(c, u):
                pool.wait_ge(hi_done, U1 * (base + c) + u + 1)
                nc.gpsimd.tensor_tensor(chip.hid_lo[:, u, :], hid[:, u % 4, :], chip.hid_hi[:, u, :].bitcast(F32),
                                        ALU.subtract).then_inc(lo_odd, 1)

            def body(c, p):
                for u in range(U1):
                    if u % 2:
                        low(c, u)
                    if u == 0 and known(c) != NCH - 1:
                        head.power_step(pool, c + 1, 1 - p)

            head.power_step(pool, 0, 0)
            chunks(pool, body)



def attn0_stage(chip):
    nc, x = chip.nc, chip.x

    def s(name):
        return chip.sem("attn0_" + name)

    TURN, QB, KB, VB, SCORES, ATT, LOCAL, WIDE = range(8)
    head = Head(chip, "attn0", 0, chip.bank[TURN], twice=False, affine=False, split=False)
    NS = TOKENS // SEG
    NB = NS // BATCH
    local, q_t, k_t, v_tok, att, att_t, wide, o_t, added, firsts, glob, glob_w = chip.rooms(
        (TOKENS,), (CH,), (CH,), (2, CH), (TPC, P), (CH,), (TPC, P), (2, CH), (CH,), (3, P), (7, P), (2, P))
    first_q, first_k, first_x = firsts[:, 0, :], firsts[:, 1, :], firsts[:, 2, :]
    g_v, g_att, g_att_t, g_out, g_sc = (glob[:, k, :] for k in range(5))
    sc = wide[:, 0, :].rearrange("p (t j) -> p t j", t=TPC)
    ex = wide[:, 1, :].rearrange("p (t j) -> p t j", t=TPC)
    top, total, inv = (wide[:, 2, 8 * k:8 * k + TPC] for k in range(3))
    tiles = "p (t d) -> p t d"

    zeroed, q_mm, k_mm, v_mm = s("zeroed"), s("q_mm"), s("k_mm"), s("v_mm")
    q_kept, k_kept, v_kept, firsts_kept = s("q_kept"), s("k_kept"), s("v_kept"), s("firsts_kept")
    scores_done, soft_step, exp_done = s("scores_done"), s("soft_step"), s("exp_done")
    att_turn, att_kept, local_mm, local_kept = s("att_turn"), s("att_kept"), s("local_mm"), s("local_kept")
    g_mm, g_step, g_exp = s("g_mm"), s("g_step"), s("g_exp")
    o_ready, o_mm, biased, x_new = s("o_ready"), s("o_mm"), s("biased"), s("x_new")
    SOFT = SPT + 1 + 1 + 1 + 1 + SPT

    with nc.Block() as block:
        @block.tensor
        def _(pe):
            def qkv(c, p):
                head.wait_xt(pe, c)
                wait(pe, q_kept, c)
                nc.tensor.matmul(chip.bank[QB][:], chip.mats[:, MAT["q0"]], chip.xt[:, p, :], start=True,
                                 stop=True).then_inc(q_mm, 1)
                wait(pe, k_kept, c)
                nc.tensor.matmul(chip.bank[KB][:], chip.mats[:, MAT["k0"]], chip.xt[:, p, :], start=True,
                                 stop=True).then_inc(k_mm, 1)
                wait(pe, v_kept, c)
                for t in range(TPC):
                    last = nc.tensor.matmul(chip.bank[VB][:, t * P:(t + 1) * P], chip.xt[:, p, t * P:(t + 1) * P],
                                            chip.mats[:, MAT["v0"]], start=True, stop=True)
                last.then_inc(v_mm, 1)

            def scores(c):
                pe.wait_ge(q_kept, c + 1)
                pe.wait_ge(k_kept, c + 1)
                for t in range(TPC):
                    last = nc.tensor.matmul(chip.bank[SCORES][:, t * P:(t + 1) * P], q_t[:, t * P:(t + 1) * P],
                                            k_t[:, t * P:(t + 1) * P], start=True, stop=True)
                last.then_inc(scores_done, 1)

            def local_step(c, p):
                pe.wait_ge(soft_step, SOFT * c + SOFT)
                for t in range(TPC):
                    last = nc.tensor.transpose(chip.bank[ATT][:, t * P:(t + 1) * P], att[:, t, :], chip.ident[:])
                last.then_inc(att_turn, 1)
                pe.wait_ge(att_kept, c + 1)
                pe.wait_ge(v_kept, c + 1)
                wait(pe, local_kept, c)
                for t in range(TPC):
                    last = nc.tensor.matmul(chip.bank[LOCAL][:, t * P:(t + 1) * P], v_tok[:, p, t * P:(t + 1) * P],
                                            att_t[:, t * P:(t + 1) * P], start=True, stop=True)
                last.then_inc(local_mm, 1)

            def body(c, p):
                qkv(c, p)
                if known(c) != NCH - 1:
                    head.turn_step(pe, c + 1, 1 - p)
                if known(c) != 0:
                    local_step(c - 1, 1 - p)
                scores(c)

            head.turn_step(pe, 0, 0)
            chunks(pe, body)
            local_step(NCH - 1, 1)

            pe.wait_ge(firsts_kept, 3 * NCH)
            nc.tensor.matmul(chip.bank[WIDE][:, 0:P], first_q, first_k, start=True, stop=True).then_inc(g_mm, 1)
            nc.tensor.matmul(chip.bank[VB][:, 0:P], first_x, chip.mats[:, MAT["v0"]], start=True, stop=True).then_inc(
                g_mm, 1)
            pe.wait_ge(g_step, 8 + BATCH)
            nc.tensor.transpose(chip.bank[WIDE][:, 0:P], g_att, chip.ident[:]).then_inc(g_mm, 1)
            pe.wait_ge(g_step, 9 + BATCH)
            nc.tensor.matmul(chip.bank[VB][:, 0:P], g_v, g_att_t, start=True, stop=True).then_inc(g_mm, 1)

            def out_body(c, p):
                pe.wait_ge(o_ready, c + 1)
                if known(c) not in (0, 1):
                    pe.wait_ge(biased, c - 1)
                for t in range(TPC):
                    last = nc.tensor.matmul(chip.bank[(QB, KB)[p]][:, t * P:(t + 1) * P],
                                            o_t[:, p, t * P:(t + 1) * P], chip.mats[:, MAT["o0"]], start=True,
                                            stop=True)
                last.then_inc(o_mm, 1)

            chunks_two(pe, out_body)

        @block.scalar
        def _(act):
            def body(c, p):
                act.wait_ge(q_mm, c + 1)
                wait(act, scores_done, c)
                if known(c) != 0:
                    act.wait_ge(firsts_kept, 3 * c)
                nc.scalar.activation(q_t, chip.bank[QB][:], ACT.Identity, bias=chip.cols[:, COL["bq"]]).then_inc(
                    q_kept, 1)
                act.wait_ge(v_mm, c + 1)
                nc.scalar.activation(v_tok[:, p, :], chip.bank[VB][:], ACT.Copy).then_inc(v_kept, 1)
                if known(c) != 0:
                    att_step(c - 1)
                act.wait_ge(soft_step, SOFT * c + SPT + 2)
                nc.scalar.activation(ex, sc, ACT.Exp, scale=SCALE).then_inc(exp_done, 1)

            def att_step(c):
                act.wait_ge(att_turn, c + 1)
                wait(act, local_mm, c)
                nc.scalar.activation(att_t, chip.bank[ATT][:], ACT.Copy).then_inc(att_kept, 1)

            nc.scalar.preload_act_table(ACT.Exp)
            chunks(act, body)
            att_step(NCH - 1)
            act.wait_ge(g_step, 3 + BATCH)
            nc.scalar.activation(g_sc[:, 0:NB], g_sc[:, 0:NB], ACT.Exp, scale=SCALE).then_inc(g_exp, 1)

        @block.vector
        def _(dve):
            def k_step(c):
                dve.wait_ge(k_mm, c + 1)
                wait(dve, scores_done, c)
                nc.vector.tensor_scalar(k_t, chip.bank[KB][:], chip.cols[:, COL["bk"]], None, ALU.add).then_inc(
                    k_kept, 1)

            def first_step(c, p):
                dve.wait_ge(q_kept, c + 1)
                dve.wait_ge(k_kept, c + 1)
                for dst, src in ((first_q, q_t), (first_k, k_t), (first_x, chip.xt[:, p, :])):
                    nc.vector.tensor_copy(dst[:, bass.ds(SPC * c, SPC)],
                                          src.rearrange("p (n s) -> p n s", s=SEG)[:, :, 0]).then_inc(firsts_kept, 1)

            def softmax(c):
                r = SOFT * c
                dve.wait_ge(scores_done, c + 1)
                wait(dve, soft_step, r)
                for g in range(SPT):
                    rows = slice(SEG * g, SEG * (g + 1))
                    nc.vector.tensor_copy(sc[rows], chip.bank[SCORES][rows, :].rearrange(tiles, t=TPC)[
                        :, :, rows]).then_inc(soft_step, 1)
                dve.wait_ge(soft_step, r + SPT)
                nc.vector.tensor_reduce(top, sc, AX.X, ALU.max).then_inc(soft_step, 1)
                dve.wait_ge(soft_step, r + SPT + 1)
                nc.vector.tensor_tensor(sc, sc, across(top.unsqueeze(2), [P, TPC, SEG]), ALU.subtract).then_inc(
                    soft_step, 1)
                dve.wait_ge(exp_done, c + 1)
                nc.vector.tensor_reduce(total, ex, AX.X, ALU.add).then_inc(soft_step, 1)
                dve.wait_ge(soft_step, r + SPT + 3)
                nc.vector.reciprocal(inv, total).then_inc(soft_step, 1)
                dve.wait_ge(soft_step, r + SPT + 4)
                wait(dve, att_turn, c)
                for g in range(SPT):
                    rows = slice(SEG * g, SEG * (g + 1))
                    nc.vector.tensor_tensor(att[rows, :, rows], ex[rows], across(inv[rows].unsqueeze(2), [SEG, TPC, SEG]),
                                            ALU.mult).then_inc(soft_step, 1)

            def local_step(c):
                dve.wait_ge(local_mm, c + 1)
                nc.vector.tensor_scalar(local[:, bass.ds(CH * c, CH)], chip.bank[LOCAL][:], chip.cols[:, COL["bv"]],
                                        None, ALU.add).then_inc(local_kept, 1)

            def body(c, p):
                k_step(c)
                first_step(c, p)
                if known(c) != NCH - 1:
                    head.moments_step(dve, c + 1, 1 - p)
                if known(c) != NCH - 1:
                    head.normed_step(dve, c + 1, 1 - p)
                    head.keep_step(dve, c + 1, 1 - p)
                if known(c) != 0:
                    local_step(c - 1)
                softmax(c)

            nc.vector.memset(att, 0.0).then_inc(zeroed, 1)
            nc.vector.memset(g_att, 0.0).then_inc(zeroed, 1)
            dve.wait_ge(zeroed, 2)
            head.moments_step(dve, 0, 0)
            head.normed_step(dve, 0, 0)
            head.keep_step(dve, 0, 0)
            chunks(dve, body)
            local_step(NCH - 1)

            dve.wait_ge(g_mm, 2)
            nc.vector.tensor_copy(g_v, chip.bank[VB][:, 0:P]).then_inc(g_step, 1)
            for b in range(BATCH):
                rows = slice(NB * b, NB * (b + 1))
                nc.vector.tensor_copy(g_sc[rows, 0:NB], chip.bank[WIDE][rows, rows]).then_inc(g_step, 1)
            dve.wait_ge(g_step, 1 + BATCH)
            nc.vector.tensor_reduce(top[:, 0:1], g_sc[:, 0:NB], AX.X, ALU.max).then_inc(g_step, 1)
            dve.wait_ge(g_step, 2 + BATCH)
            nc.vector.tensor_scalar(g_sc[:, 0:NB], g_sc[:, 0:NB], top[:, 0:1], None, ALU.subtract).then_inc(g_step, 1)
            dve.wait_ge(g_exp, 1)
            nc.vector.tensor_reduce(total[:, 0:1], g_sc[:, 0:NB], AX.X, ALU.add).then_inc(g_step, 1)
            dve.wait_ge(g_step, 4 + BATCH)
            nc.vector.reciprocal(inv[:, 0:1], total[:, 0:1]).then_inc(g_step, 1)
            dve.wait_ge(g_step, 5 + BATCH)
            for b in range(BATCH):
                rows = slice(NB * b, NB * (b + 1))
                nc.vector.tensor_scalar(g_att[rows, rows], g_sc[rows, 0:NB], inv[rows, 0:1], None, ALU.mult).then_inc(
                    g_step, 1)
            nc.vector.tensor_copy(added[:, 0:1], inv[:, 0:1]).then_inc(g_step, 1)
            dve.wait_ge(g_mm, 3)
            nc.vector.tensor_copy(g_att_t, chip.bank[WIDE][:, 0:P]).then_inc(g_step, 1)
            dve.wait_ge(g_mm, 4)
            nc.vector.tensor_scalar(g_out, chip.bank[VB][:, 0:P], chip.cols[:, COL["bv"]], None, ALU.add).then_inc(
                g_step, 1)
            dve.wait_ge(g_step, 10 + BATCH)

            def sum_step(c, p):
                if known(c) not in (0, 1):
                    dve.wait_ge(o_mm, c - 1)
                nc.vector.tensor_tensor(o_t[:, p, :].rearrange("p (n s) -> p n s", s=SEG),
                                        local[:, bass.ds(CH * c, CH)].rearrange("p (n s) -> p n s", s=SEG),
                                        across(g_out[:, bass.ds(SPC * c, SPC)].unsqueeze(2), [P, SPC, SEG]),
                                        ALU.add).then_inc(o_ready, 1)

            def residual(c, p):
                dve.wait_ge(o_mm, c + 1)
                wait(dve, x_new, c)
                nc.vector.tensor_tensor(added.rearrange(tiles, t=TPC), chip.bank[(QB, KB)[p]][:].rearrange(tiles, t=TPC),
                                        across(chip.rows[:, ROW["bo"]].unsqueeze(1), [P, TPC, P]), ALU.add).then_inc(
                                            biased, 1)
                dve.wait_ge(biased, c + 1)
                tile = x[:, bass.ds(TPC * c, TPC), :]
                nc.vector.tensor_tensor(tile, tile, added.rearrange(tiles, t=TPC), ALU.add).then_inc(x_new, 1)

            def out_body(c, p):
                sum_step(c, p)
                if known(c) != 0:
                    residual(c - 1, 1 - p)

            dve.wait_ge(local_kept, NCH)
            chunks_two(dve, out_body)
            residual(NCH - 1, 1)

        @block.gpsimd
        def _(pool):
            def body(c, p):
                if known(c) != NCH - 1:
                    head.power_step(pool, c + 1, 1 - p)

            head.power_step(pool, 0, 0)
            chunks(pool, body)



def attn1_stage(chip):
    nc, x = chip.nc, chip.x

    def s(name):
        return chip.sem("attn1_" + name)

    TURN = 0
    QKV = ((1, 2, 3), (4, 5, 6))
    V_TURN, GRAM, MIX = (1, 2), (3, 4), 5
    head = Head(chip, "attn1", 0, chip.bank[TURN], twice=False, affine=False, split=False)
    q_all, k_all, v_all = (chip.room[:, k * TOKENS:(k + 1) * TOKENS] for k in range(3))
    names = ("q1", "k1", "v1")
    HALF = NCH // BATCH
    bn, agg, fix = chip.buf("bn", [P, 3, NCH, 6]), chip.buf("bn_agg", [P, 3, 2]), chip.buf("bn_fix", [P, 6, 3])
    head_mask = chip.buf("head_mask", [P, P])
    gram, mix = chip.buf("gram", [P, BATCH, P]), chip.buf("mix", [P, BATCH, P])
    v_s = chip.xt
    v_tok, qk = chip.buf("v_tok", [P, 2, CH]), chip.buf("qk", [P, 2, CH])
    tiles = "p (t d) -> p t d"

    mm, kept, stat = s("mm"), s("kept"), s("stat")
    bn_step, bn_pow, masked = s("bn_step"), s("bn_pow"), s("masked")
    sig_v, sig_q, v_turn, v_kept, gram_mm = s("sig_v"), s("sig_qk"), s("v_turn"), s("v_kept"), s("gram_mm")
    gram_kept, mix_mm, mix_kept = s("gram_kept"), s("mix_mm"), s("mix_kept")
    qk_ready, out_mm, biased, x_new = s("qk_ready"), s("out_mm"), s("biased"), s("x_new")

    with nc.Block() as block:
        @block.tensor
        def _(pe):
            def body(c, p):
                head.wait_xt(pe, c)
                if known(c) not in (0, 1):
                    pe.wait_ge(kept, 3 * (c - 1))
                for k, name in enumerate(names):
                    nc.tensor.matmul(chip.bank[QKV[p][k]][:], chip.mats[:, MAT[name]], chip.xt[:, p, :], start=True,
                                     stop=True).then_inc(mm, 1)
                if known(c) != NCH - 1:
                    head.turn_step(pe, c + 1, 1 - p)

            head.turn_step(pe, 0, 0)
            chunks_two(pe, body)

            pe.wait_ge(kept, 3 * NCH)
            for c in range(NCH + 1):
                if c < NCH:
                    p = c % 2
                    pe.wait_ge(sig_v, c + 1)
                    wait(pe, v_kept, c - 1)
                    for t in range(TPC):
                        last = nc.tensor.transpose(chip.bank[V_TURN[p]][:, t * P:(t + 1) * P],
                                                   v_s[:, p, t * P:(t + 1) * P], chip.ident[:])
                    last.then_inc(v_turn, 1)
                if c > 0:
                    b, p = (c - 1) // HALF, (c - 1) % 2
                    pe.wait_ge(v_kept, c)
                    for t in range(TPC):
                        tile = v_tok[:, p, t * P:(t + 1) * P]
                        last = nc.tensor.matmul(chip.bank[GRAM[b]][:, 0:P], tile, tile,
                                                start=(c - 1) % HALF == 0 and t == 0,
                                                stop=(c - 1) % HALF == HALF - 1 and t == TPC - 1)
                    last.then_inc(gram_mm, 1)
            for b in range(BATCH):
                pe.wait_ge(gram_kept, b + 1)
                wait(pe, mix_kept, b)
                nc.tensor.matmul(chip.bank[MIX][:, 0:P], gram[:, b, :], chip.mats[:, MAT["p1"]], start=True,
                                 stop=True).then_inc(mix_mm, 1)
            pe.wait_ge(mix_kept, BATCH)

            def out_body(c, p, b):
                pe.wait_ge(qk_ready, c + 1)
                if known(c) not in (0, 1):
                    pe.wait_ge(biased, c - 1)
                for t in range(TPC):
                    last = nc.tensor.matmul(chip.bank[V_TURN[p]][:, t * P:(t + 1) * P], qk[:, p, t * P:(t + 1) * P],
                                            mix[:, b, :], start=True, stop=True)
                last.then_inc(out_mm, 1)

            halves(pe, out_body)

        @block.scalar
        def _(act):
            def body(c, p):
                for k, dst in enumerate((q_all, k_all, v_all)):
                    act.wait_ge(mm, 3 * c + k + 1)
                    nc.scalar.activation(dst[:, bass.ds(CH * c, CH)], chip.bank[QKV[p][k]][:], ACT.Copy).then_inc(
                        kept, 1)

            nc.scalar.preload_act_table(ACT.Sigmoid)
            chunks_two(act, body)
            act.wait_ge(bn_step, 3 + 6)
            act.wait_ge(kept, 3 * NCH)
            for c in range(NCH):
                p = c % 2
                wait(act, v_turn, c - 1)
                nc.scalar.activation(v_s[:, p, :], v_all[:, c * CH:(c + 1) * CH], ACT.Sigmoid, bias=fix[:, 5, 2:3],
                                     scale=fix[:, 3, 2:3]).then_inc(sig_v, 1)

            def sigmoids(c, p):
                for k, dst in ((0, q_all), (1, k_all)):
                    nc.scalar.activation(dst[:, bass.ds(CH * c, CH)], dst[:, bass.ds(CH * c, CH)], ACT.Sigmoid,
                                         bias=fix[:, 5, k:k + 1], scale=fix[:, 3, k:k + 1]).then_inc(sig_q, 1)

            chunks_two(act, sigmoids)

        @block.vector
        def _(dve):
            def body(c, p):
                if known(c) != NCH - 1:
                    head.moments_step(dve, c + 1, 1 - p)
                for k, src in enumerate((q_all, k_all, v_all)):
                    dve.wait_ge(kept, 3 * c + k + 1)
                    nc.vector.bn_stats(bn[:, k, bass.ds(c, 1), :], src[:, bass.ds(CH * c, CH)]).then_inc(stat, 1)
                if known(c) != NCH - 1:
                    head.normed_step(dve, c + 1, 1 - p)
                    head.keep_step(dve, c + 1, 1 - p)

            head.moments_step(dve, 0, 0)
            head.normed_step(dve, 0, 0)
            head.keep_step(dve, 0, 0)
            chunks_two(dve, body)
            dve.wait_ge(stat, 3 * NCH)
            for k in range(3):
                nc.vector.bn_aggr(agg[:, k, :], bn[:, k, :, :].rearrange("p c s -> p (c s)")).then_inc(bn_step, 1)
            dve.wait_ge(bn_step, 3)
            nc.vector.tensor_scalar(fix[:, 0, :], agg[:, :, 1], EPS, None, ALU.add).then_inc(bn_step, 1)
            dve.wait_ge(bn_pow, 1)
            gammas = chip.cols[:, COL["gq"].start:COL["gv"].stop]
            betas = chip.cols[:, COL["tq"].start:COL["tv"].stop]
            nc.vector.tensor_tensor(fix[:, 2, :], fix[:, 1, :], gammas, ALU.mult).then_inc(bn_step, 1)
            dve.wait_ge(bn_step, 5)
            nc.vector.tensor_scalar(fix[:, 3, :], fix[:, 2, :], 4.0, None, ALU.mult).then_inc(bn_step, 1)
            nc.vector.tensor_tensor(fix[:, 4, :], agg[:, :, 0], fix[:, 2, :], ALU.mult).then_inc(bn_step, 1)
            dve.wait_ge(bn_step, 7)
            nc.vector.tensor_tensor(fix[:, 4, :], betas, fix[:, 4, :], ALU.subtract).then_inc(bn_step, 1)
            dve.wait_ge(bn_step, 8)
            nc.vector.tensor_scalar(fix[:, 5, :], fix[:, 4, :], 4.0, -4.0, ALU.mult, ALU.add).then_inc(bn_step, 1)
            for c in range(NCH):
                p = c % 2
                dve.wait_ge(v_turn, c + 1)
                wait(dve, gram_mm, c - 1)
                nc.vector.tensor_copy(v_tok[:, p, :], chip.bank[V_TURN[p]][:]).then_inc(v_kept, 1)
            dve.wait_ge(masked, 3)
            for b in range(BATCH):
                dve.wait_ge(gram_mm, HALF * (b + 1))
                nc.vector.tensor_tensor(gram[:, b, :], chip.bank[GRAM[b]][:, 0:P], head_mask[:], ALU.mult).then_inc(
                    gram_kept, 1)
            for b in range(BATCH):
                dve.wait_ge(mix_mm, b + 1)
                nc.vector.tensor_copy(mix[:, b, :], chip.bank[MIX][:, 0:P]).then_inc(mix_kept, 1)

            def product(c, p):
                dve.wait_ge(sig_q, 2 * c + 2)
                if known(c) not in (0, 1):
                    dve.wait_ge(out_mm, c - 1)
                nc.vector.scalar_tensor_tensor(out=qk[:, p, :], in0=q_all[:, bass.ds(CH * c, CH)], scalar=SCALE,
                                               in1=k_all[:, bass.ds(CH * c, CH)], op0=ALU.mult,
                                               op1=ALU.mult).then_inc(qk_ready, 1)

            def residual(c, p):
                dve.wait_ge(out_mm, c + 1)
                wait(dve, x_new, c)
                nc.vector.tensor_tensor(chip.xs[:], chip.bank[V_TURN[p]][:].rearrange(tiles, t=TPC),
                                        across(chip.rows[:, ROW["bp"]].unsqueeze(1), [P, TPC, P]), ALU.add).then_inc(
                                            biased, 1)
                dve.wait_ge(biased, c + 1)
                tile = x[:, bass.ds(TPC * c, TPC), :]
                nc.vector.tensor_tensor(tile, tile, chip.xs[:], ALU.add).then_inc(x_new, 1)

            def out_body(c, p):
                product(c, p)
                if known(c) != 0:
                    residual(c - 1, 1 - p)

            chunks_two(dve, out_body)
            residual(NCH - 1, 1)

        @block.gpsimd
        def _(pool):
            nc.gpsimd.memset(head_mask[:], 1.0).then_inc(masked, 1)
            m = head_mask[:].rearrange("p (h d) -> p h d", d=HEAD)
            for n, (sign, start) in enumerate(((1, 0), (-1, HEAD - 1))):
                pool.wait_ge(masked, n + 1)
                nc.gpsimd.affine_select(out=m, in_=m, compare_op=ALU.is_ge, fill=0.0, base=start,
                                        pattern=[[-sign * HEAD, P // HEAD], [0, HEAD]],
                                        channel_multiplier=sign).then_inc(masked, 1)

            def body(c, p):
                if known(c) != NCH - 1:
                    head.power_step(pool, c + 1, 1 - p)

            head.power_step(pool, 0, 0)
            chunks_two(pool, body)
            pool.wait_ge(bn_step, 4)
            nc.gpsimd.tensor_tensor(fix[:, 1, :], fix[:, 0, :], chip.neg_half[:, 0:3], ALU.pow).then_inc(bn_pow, 1)



_LAID = ("x", "cols", "rows", "mats", "gens", "gens_t", "ew1", "ew2", "w1", "w2", "b2")


def macaron(nc, args, out):
    with ExitStack() as ctx:
        chip = Chip(nc, ctx)
        setup(chip, args)
        setup_selectors(chip)
        calls = {}
        for name in STAGES:
            call = calls.get(name, 0)
            calls[name] = call + 1
            if name == "ffn0":
                ffn0_stage(chip, call)
            elif name == "attn0":
                attn0_stage(chip)
            elif name == "ffn1":
                ffn1_stage(chip, call, out, call == STAGES.count(name) - 1)
            elif name == "attn1":
                attn1_stage(chip)


def lay_out(a):
    import numpy as np

    g = {k: np.asarray(v) for k, v in a.items()}
    col = lambda v: v.reshape(P, 1)
    row = lambda v: np.broadcast_to(v.reshape(1, -1), (P, v.size))
    cols = [col(g["L0_ffn_ln_gamma"]), col(g["L0_ffn_ln_beta"]), g["L0_ffn_eb1"].reshape(U0, P).T, g["L0_ffn_eb2"].T,
            col(g["L0_attn_bq"]), col(g["L0_attn_bk"]), col(g["L0_attn_bv"]),
            col(g["L1_attn_gq"]), col(g["L1_attn_gk"]), col(g["L1_attn_gv"]),
            col(g["L1_attn_bq"]), col(g["L1_attn_bk"]), col(g["L1_attn_bv"]), g["L1_ffn_bias1"].reshape(U1, P).T]
    rows = [row(g["L0_ffn_moe_gate_b"]), row(g["L0_ffn_abel_b"]), row(g["L0_ffn_gc_w"][:P, 0]),
            row(g["L0_ffn_gc_w"][P:, 0]), row(g["L0_ffn_gc_b"]), row(g["L0_attn_bo"]), row(g["L1_attn_bp"]),
            row(g["L1_ffn_router_b"])]
    mats = [g["L0_ffn_abel_w"], g["L0_ffn_moe_gate_w"], g["L0_attn_Wq"].T, g["L0_attn_Wk"].T, g["L0_attn_Wv"].T,
            g["L0_attn_Wo"].T, g["L1_attn_Wq"].T, g["L1_attn_Wk"].T, g["L1_attn_Wv"].T, g["L1_attn_Wp"].T,
            g["L1_ffn_router_w"].T]
    laid = {
        "x": g["L0_attn_x"].reshape(TOKENS, P),
        "cols": np.concatenate(cols, 1), "rows": np.concatenate(rows, 1), "mats": np.concatenate(mats, 1),
        "gens": g["L0_ffn_gens"].transpose(1, 0, 2), "gens_t": g["L0_ffn_gens"].transpose(2, 0, 1),
        "ew1": g["L0_ffn_ew1"].transpose(1, 0, 2).reshape(P, U0, P),
        "ew2": g["L0_ffn_ew2"].reshape(U0, P, P).transpose(1, 0, 2),
        "w1": g["L1_ffn_weights1"].transpose(1, 0, 2).reshape(P, U1, P),
        "w2": g["L1_ffn_weights2"].reshape(U1, P, P).transpose(1, 0, 2),
        "b2": g["L1_ffn_bias2"],
    }
    return {k: np.ascontiguousarray(v) for k, v in laid.items()}


def kernel(**inputs):
    import concourse.bacc as bacc
    from concourse.bass_utils import run_bass_kernel_spmd

    nc = bacc.Bacc("TRN2", target_bir_lowering=False, num_devices=1)
    laid = lay_out(inputs)
    args = {k: nc.dram_tensor(f"in_{k}", laid[k].shape, F32, kind="ExternalInput").ap() for k in _LAID}
    out = nc.dram_tensor("out", (TOKENS, P), F32, kind="ExternalOutput").ap()
    macaron(nc, args, out)
    run = run_bass_kernel_spmd(nc, [{f"in_{k}": laid[k] for k in _LAID}], core_ids=[0])
    return run.results[0]["out"].reshape(BATCH, LENGTH, P)
```

```python
from contextlib import ExitStack

import concourse.bass as bass
from concourse import mybir

F32 = mybir.dt.float32
F32R = mybir.dt.float32r
U32 = mybir.dt.uint32
ALU = mybir.AluOpType
ACT = mybir.ActivationFunctionType
AX = mybir.AxisListType
RMAX = bass.bass_isa.ReduceOp.max

P = 128
BATCH, LENGTH = 2, 2048
TOKENS = BATCH * LENGTH
TILES = TOKENS // P
TPC = 4
CH = TPC * P
NCH = TOKENS // CH
EPS = 1e-5

E0, HC = 8, 2
U0 = E0 * HC
E1, H1 = 32, 32
EPU = P // H1
U1 = E1 // EPU
SEG = 32
SPT = P // SEG
SPC = CH // SEG
HEAD = 8
SCALE = HEAD ** -0.5
BLOCKED = 2.0 ** 100
NROT = 3
DEGREE = 11
SQUARINGS = 18

STAGES = ("ffn0", "attn0", "ffn0", "ffn1", "attn1", "ffn1")


TURN = 6

LAG0, WIDE_LAG0 = 2, 1
AT0 = dict(
    rot=7, abel_mm=13, turn=7, logits=11, w_turn=15,
    abel=15, gate=9, pair=11, w_kept=15,
    abel_bias=14, dots_abel=3, dots_moe=7, difference=8, mix=9, keep_input=14, moments=1, normed=3, keep=7, split=7,
    route_pair=9, route_weights=13,
    power=0)
LAG1 = 2
AT1 = dict(
    back=9, turn=5, logits=9, one_turn=12,
    y=2, one_kept=5,
    add=5, moments=0, normed=0, keep=2, split=3, route=4, block=5)


def layout(*fields):
    at, out = 0, {}
    for name, width in fields:
        out[name] = slice(at, at + width)
        at += width
    return out, at


COL, NCOL = layout(("gamma", 1), ("beta", 1), ("eb1", U0), ("eb2", E0), ("bq", 1), ("bk", 1), ("bv", 1),
                   ("gq", 1), ("gk", 1), ("gv", 1), ("tq", 1), ("tk", 1), ("tv", 1))
ROW, NROW = layout(("gate_b", E0), ("abel_b", P), ("gate_abel", P), ("gate_moe", P), ("gc_b", 1), ("bo", P),
                   ("bp", P), ("router_b", E1))
MAT, NMAT = layout(("abel", P), ("gate", E0), ("q0", P), ("k0", P), ("v0", P), ("o0", P), ("q1", P), ("k1", P),
                   ("v1", P), ("p1", P), ("router", E1))


class Chip:

    def __init__(self, nc, ctx):
        self.nc, self.ctx, self.sems = nc, ctx, {}
        sb = self.sb
        self.bank = [ctx.enter_context(nc.psum_tensor(f"bank{i}", [P, CH], F32)) for i in range(8)]
        self.x = sb("x", [P, TILES, P])
        self.cols, self.rows, self.mats = sb("cols", [P, NCOL]), sb("rows", [P, NROW]), sb("mats", [P, NMAT])
        self.ew1_hi, self.ew1_lo = (sb(f"ew1_{k}", [P, U0, P], F32R) for k in ("hi", "lo"))
        self.ew2_hi, self.ew2_lo = (sb(f"ew2_{k}", [P, U0, P], F32R) for k in ("hi", "lo"))
        self.w1_hi, self.w1_lo = (sb(f"w1_{k}", [P, U1, P], F32R) for k in ("hi", "lo"))
        self.w2_hi, self.w2_lo = (sb(f"w2_{k}", [P, U1, P], F32R) for k in ("hi", "lo"))
        self.b2_split = sb("b2_split", [2 * E1, P], F32R)
        self.rotation = sb("rotation", [P, P])
        self.ident = sb("ident", [P, P])
        self.iota_row = sb("iota_row", [P, 2 * E1])
        self.neg_half = sb("neg_half", [P, 2 * TPC])
        self.half_gc_b = sb("half_gc_b", [P, 1])
        self.pick_expert = sb("pick_expert", [2 * E0, E0, P], F32R)
        self.block_expert = sb("block_expert", [E1 + 2, U1, P], F32R)
        self.stats = sb("stats", [P, TPC, 6])
        self.moments = sb("moments", [P, 2, TPC, 2])
        self.powed = sb("powed", [P, 2, TPC])
        self.r_std = sb("r_std", [P, 2, 2, TPC])
        self.mean_r = sb("mean_r", [P, TPC])
        self.keep_scale, self.keep_shift = sb("keep_scale", [P, 2, TPC]), sb("keep_shift", [P, 2, TPC])
        self.xs = sb("xs", [P, TPC, P])
        self.xt = sb("xt", [P, 2, CH])
        self.xt_hi, self.xt_lo = sb("xt_hi", [P, 2, CH], F32R), sb("xt_lo", [P, 2, CH], F32R)
        self.hid_hi, self.hid_lo = sb("hid_hi", [P, 8, CH], F32R), sb("hid_lo", [P, 8, CH], F32R)
        self.logits0, self.logits1 = sb("logits0", [P, TPC, E0]), sb("logits1", [P, TPC, E1])
        self.best, self.best_at = sb("best", [P, TPC, 8]), sb("best_at", [P, TPC, 8], U32)
        self.one_a, self.one_b, self.chosen = sb("one_a", [P, TPC, E0]), sb("one_b", [P, TPC, E0]), sb("chosen", [P, TPC, 2 * E1])
        self.pair, self.pair_w = sb("pair", [P, 2, TPC]), sb("pair_w", [P, 2, TPC])
        self.w_split, self.w_turned = sb("w_split", [P, TPC, 2 * E0], F32R), sb("w_turned", [2 * E0, 2, CH], F32R)
        self.chosen_t, self.blocked_t = sb("chosen_t", [2 * E1, 2, CH], F32R), sb("blocked_t", [E1 + 2, 2, CH], F32R)
        self.gate = sb("gate", [P, 5, TPC])
        self.room = sb("room", [P, 3 * TOKENS])

    def sb(self, name, shape, dt=F32):
        return self.ctx.enter_context(self.nc.sbuf_tensor(name, shape, dt))

    def sem(self, name):
        if name not in self.sems:
            self.sems[name] = self.ctx.enter_context(self.nc.semaphore(name))
        return self.sems[name]

    def buf(self, name, shape, dt=F32):
        return self.sb(name, shape, dt)

    def rooms(self, *fields):
        at, out = 0, []
        for shape in fields:
            n = 1
            for k in shape:
                n *= k
            view = self.room[:, at:at + n]
            if len(shape) == 2:
                view = view.rearrange("p (a b) -> p a b", a=shape[0])
            if len(shape) == 3:
                view = view.rearrange("p (a b c) -> p a b c", a=shape[0], b=shape[1])
            out.append(view)
            at += n
        assert at <= 3 * TOKENS
        return out


def wait(eng, sem, value):
    if not (isinstance(value, int) and value <= 0):
        eng.wait_ge(sem, value)


def wait_alone(eng, sem, value, passed):
    if not (isinstance(value, int) and value <= 0):
        eng.wait_ge(sem, value)
        if not isinstance(value, int):
            eng.sem_inc(passed, 1)


def chunks(eng, body):
    body(0, 0)
    with eng.Fori(0, (NCH - 2) // 2) as i:
        body(2 * i + 1, 1)
        body(2 * i + 2, 0)
    body(NCH - 1, 1)


def chunks_two(eng, body):
    body(0, 0)
    body(1, 1)
    with eng.Fori(1, (NCH - 2) // 2) as i:
        body(2 * i, 0)
        body(2 * i + 1, 1)
    body(NCH - 2, 0)
    body(NCH - 1, 1)


def halves(eng, body):
    half = NCH // BATCH
    for b in range(BATCH):
        body(half * b, 0, b)
        body(half * b + 1, 1, b)
        with eng.Fori(half // 2 * b + 1, half // 2 * (b + 1)) as i:
            body(2 * i, 0, b)
            body(2 * i + 1, 1, b)


def known(c):
    return c if isinstance(c, int) else None


def across(ap, shape):
    return ap.to_broadcast(shape)



def setup(chip, args, front):
    nc, x = chip.nc, chip.x
    loaded_x, loaded_small, loaded_gens = chip.sem("loaded_x"), chip.sem("loaded_small"), chip.sem("loaded_gens")
    loaded_w, const_made = chip.sem("loaded_w"), chip.sem("const_made")
    hi_made, lo_made = chip.sem("hi_made"), chip.sem("lo_made")
    raw_ew1, raw_ew2, raw_w1, raw_w2, raw_b2, gens, gens_t, power, sums, rot12_t, pick, block_rows, raw_b1, ones = chip.rooms(
        (U0, P), (U0, P), (U1, P), (U1, P), (1, P), (NROT, P), (NROT, P), (NROT, 2, P), (4, SQUARINGS), (1, P),
        (E0, P), (U1, P), (U1, P), (CH,))
    b2_again, b1_low = chip.hid_hi[:, 0, 0:P], chip.hid_hi[:, 1:3, :].rearrange("p a (u h) -> p (a u) h", h=P)
    threshold, over, factor = sums[:, 0, :], sums[:, 1, :], sums[:, 2, :]
    col_norm, norm, shrink = sums[:, 3, 0:NROT], sums[:, 3, 4:5], sums[:, 3, 5:6]
    over_bits = chip.sb("over_bits", [P, SQUARINGS], U32)
    col_max = sums[:, 3, 6:7]
    b1_row = slice(E1, E1 + 1)
    splits = [(raw_ew1, chip.ew1_hi[:], chip.ew1_lo[:]), (raw_ew2, chip.ew2_hi[:], chip.ew2_lo[:]),
              (raw_w1, chip.w1_hi[:], chip.w1_lo[:]), (raw_w2, chip.w2_hi[:], chip.w2_lo[:]),
              (raw_b2[0:E1, 0, :], chip.b2_split[0:E1], None), (raw_b2[E1:2 * E1, 0, :], b2_again[E1:2 * E1], chip.b2_split[E1:2 * E1]),
              (raw_b1[b1_row], chip.block_expert[b1_row], b1_low[b1_row])]
    norm_step, all_norm, taylor_mm, taylor_done = (
        chip.sem(n) for n in ("norm_step", "all_norm", "taylor_mm", "taylor_done"))
    turned, turned_kept, squared, square_kept = (
        chip.sem(n) for n in ("turned", "turned_kept", "squared", "square_kept"))
    rot_mm, rot_kept = chip.sem("rot_mm"), chip.sem("rot_kept")
    sel_step, sel_made = chip.sem("sel_step"), chip.sem("sel_made")
    lows = sum(lo is not None for _, _, lo in splits)
    pair = "p s d -> p (s d)"
    exp_bank = [b[:, 0:2 * P] for b in chip.bank[0:NROT]]

    consts = 3 + SQUARINGS + 1

    with nc.Block() as block:
        @block.sync
        def _(sp):
            sp.dma_start(gens, args["gens"]).then_inc(loaded_gens, 16)
            sp.dma_start(gens_t, args["gens_t"]).then_inc(loaded_gens, 16)
            sp.dma_start(chip.cols[:], args["cols"]).then_inc(loaded_small, 16)
            sp.dma_start(chip.rows[:], args["rows"]).then_inc(loaded_small, 16)
            sp.dma_start(chip.mats[:], args["mats"]).then_inc(loaded_small, 16)
            sp.dma_start(x[:], args["x"].rearrange("(t p) d -> p t d", p=P)).then_inc(loaded_x, 16)
            for k, (dst, name) in enumerate(((raw_ew1, "ew1"), (raw_ew2, "ew2"), (raw_w1, "w1"), (raw_w2, "w2"))):
                sp.dma_start(dst, args[name]).then_inc(loaded_w, 16)
                sp.wait_ge(loaded_w, 16 * (k + 1))
            for k, (dst, name) in enumerate(((raw_b2[0:E1, 0, :], "b2"), (raw_b2[E1:2 * E1, 0, :], "b2"),
                                             (raw_b1[b1_row], "b1_row"))):
                sp.dma_start(dst, args[name]).then_inc(loaded_w, 16)
                sp.wait_ge(loaded_w, 16 * (k + 5))
            sp.wait_ge(lo_made, lows)
            sp.dma_start(chip.block_expert[E1 + 1:E1 + 2].bitcast(F32), b1_low[b1_row].bitcast(F32)).then_inc(loaded_w, 16)
            sp.wait_ge(loaded_x, 16)
            sp.wait_ge(loaded_small, 48)
            sp.wait_ge(loaded_w, 16 * (len(splits) + 1))

        @block.gpsimd
        def _(pool):
            nc.gpsimd.memset(chip.ident[:], 0.0).then_inc(const_made, 1)
            nc.gpsimd.memset(chip.neg_half[:], -0.5).then_inc(const_made, 1)
            nc.gpsimd.iota(chip.iota_row[:], [[0, 2], [1, E1]], base=0, channel_multiplier=0,
                           allow_small_or_imprecise_dtypes=True).then_inc(const_made, 1)
            for j in range(SQUARINGS):
                nc.gpsimd.memset(threshold[:, j:j + 1], 2.0 ** j).then_inc(const_made, 1)
            pool.wait_ge(const_made, 1)
            nc.gpsimd.affine_select(out=chip.ident[:], in_=chip.ident[:], compare_op=ALU.not_equal, fill=1.0, base=0,
                                    pattern=[[-1, P]], channel_multiplier=1).then_inc(const_made, 1)
            pool.wait_ge(norm_step, 2)
            nc.gpsimd.partition_all_reduce(norm, col_max, P, RMAX).then_inc(all_norm, 1)
            nc.gpsimd.memset(pick[0:2 * E0], 0.0).then_inc(sel_step, 1)
            nc.gpsimd.memset(block_rows[0:E1], 0.0).then_inc(sel_step, 1)
            nc.gpsimd.memset(ones[0:E1 + 2], 1.0).then_inc(sel_step, 1)
            pool.wait_ge(sel_step, 3)
            nc.gpsimd.affine_select(out=pick[0:2 * E0], in_=pick[0:2 * E0], compare_op=ALU.not_equal, fill=1.0,
                                    base=0, pattern=[[-1, E0], [0, P]], channel_multiplier=1).then_inc(sel_step, 1)
            nc.gpsimd.affine_select(out=block_rows[0:E1].rearrange("k u (q h) -> k u q h", q=EPU),
                                    in_=block_rows[0:E1].rearrange("k u (q h) -> k u q h", q=EPU),
                                    compare_op=ALU.not_equal, fill=BLOCKED, base=0,
                                    pattern=[[-EPU, U1], [-1, EPU], [0, H1]], channel_multiplier=1).then_inc(sel_step, 1)
            pool.wait_ge(sel_step, 5)
            nc.gpsimd.affine_select(out=pick[0:2 * E0], in_=pick[0:2 * E0], compare_op=ALU.not_equal, fill=1.0,
                                    base=-E0, pattern=[[-1, E0], [0, P]], channel_multiplier=1).then_inc(sel_step, 1)
            for n, (raw, hi, lo) in enumerate(splits):
                if lo is not None:
                    pool.wait_ge(hi_made, n + 1)
                    if n >= 4:
                        pool.wait_ge(lo_made, lows - (len(splits) - n))
                    nc.gpsimd.tensor_tensor(lo, raw, hi.bitcast(F32), ALU.subtract).then_inc(lo_made, 1)
                if n == 0:
                    pool.wait_ge(const_made, consts)
                    front.power_step(pool, 0, 0)
        @block.scalar
        def _(act):
            nc.scalar.preload_act_table(ACT.Gelu)
            for k, (raw, hi, _) in enumerate(splits):
                act.wait_ge(loaded_w, 16 * (k + 1))
                nc.scalar.activation(hi, raw, ACT.Copy).then_inc(hi_made, 1)
            act.wait_ge(loaded_small, 48)
            nc.scalar.activation(chip.half_gc_b[:], chip.rows[:, ROW["gc_b"]], ACT.Copy, scale=0.5).then_inc(hi_made, 1)
            act.wait_ge(sel_step, 6)
            nc.scalar.activation(chip.pick_expert[:], pick[0:2 * E0], ACT.Copy).then_inc(sel_made, 1)
            nc.scalar.activation(chip.block_expert[0:E1], block_rows[0:E1], ACT.Copy).then_inc(sel_made, 1)
            for p in range(2):
                nc.scalar.activation(chip.blocked_t[E1:E1 + 2, p, :], ones[E1:E1 + 2], ACT.Copy).then_inc(sel_made, 1)
            front.pair_step(act, 0, 0)
            front.rows_kept_step(act, 0, 0)

        @block.vector
        def _(dve):
            dve.wait_ge(loaded_gens, 32)
            nc.vector.tensor_reduce(col_norm, gens_t, AX.X, ALU.add, apply_absolute_value=True).then_inc(norm_step, 1)
            dve.wait_ge(norm_step, 1)
            nc.vector.tensor_reduce(col_max, col_norm, AX.X, ALU.max).then_inc(norm_step, 1)
            dve.wait_ge(all_norm, 1)
            dve.wait_ge(const_made, consts)
            nc.vector.tensor_scalar(over, threshold, norm, None, ALU.is_lt).then_inc(norm_step, 1)
            dve.wait_ge(norm_step, 3)
            nc.vector.tensor_copy(over_bits[:], over).then_inc(norm_step, 1)
            nc.vector.tensor_scalar(factor, over, -0.5, 1.0, ALU.mult, ALU.add).then_inc(norm_step, 1)
            dve.wait_ge(norm_step, 5)
            nc.vector.tensor_reduce(shrink, factor, AX.X, ALU.mult).then_inc(norm_step, 1)
            dve.wait_ge(norm_step, 6)
            nc.vector.tensor_scalar(gens, gens, shrink, None, ALU.mult).then_inc(norm_step, 1)
            nc.vector.tensor_scalar(gens_t, gens_t, shrink, None, ALU.mult).then_inc(norm_step, 1)
            dve.wait_ge(norm_step, 8)
            for i in range(NROT):
                nc.vector.scalar_tensor_tensor(out=power[:, i, 0, :], in0=gens[:, i, :], scalar=1.0 / DEGREE,
                                               in1=chip.ident[:], op0=ALU.mult, op1=ALU.add).then_inc(taylor_done, 1)
            for k in range(DEGREE - 1, 0, -1):
                for i in range(NROT):
                    dve.wait_ge(taylor_mm, NROT * (DEGREE - 1 - k) + i + 1)
                    nc.vector.scalar_tensor_tensor(out=power[:, i, 0, :], in0=exp_bank[i][:, 0:P], scalar=1.0 / k,
                                                   in1=chip.ident[:], op0=ALU.mult, op1=ALU.add).then_inc(
                                                       taylor_done, 1)
            for i in range(NROT):
                dve.wait_ge(turned, i + 1)
                nc.vector.tensor_copy(power[:, i, 1, :], exp_bank[i][:, 0:P]).then_inc(turned_kept, 1)
            for j in range(SQUARINGS):
                for i in range(NROT):
                    dve.wait_ge(squared, NROT * j + i + 1)
                    nc.vector.copy_predicated(power[:, i].rearrange(pair), across(over_bits[:, j:j + 1], [P, 2 * P]),
                                              exp_bank[i]).then_inc(square_kept, 1)
                if j == 2:
                    dve.wait_ge(loaded_x, 16)
                    front.moments_step(dve, 0, 0)
                if j == 6:
                    front.normed_step(dve, 0, 0)
                if j == 8:
                    dve.wait_ge(loaded_small, 48)
                    front.keep_step(dve, 0, 0)
                    front.split_step(dve, 0, 0)
                if j == 12:
                    front.route_first(dve, 0, 0)
                if j == 15:
                    front.route_second(dve, 0, 0)
                if j == SQUARINGS - 1:
                    front.route_last(dve, 0, 0)
            dve.wait_ge(rot_mm, 1)
            nc.vector.tensor_copy(rot12_t[:, 0, :], exp_bank[0][:, 0:P]).then_inc(rot_kept, 1)
            dve.wait_ge(rot_mm, 2)
            nc.vector.tensor_copy(chip.rotation[:], exp_bank[0][:, 0:P]).then_inc(rot_kept, 1)
        @block.tensor
        def _(pe):
            for k in range(DEGREE - 1):
                for i in range(NROT):
                    pe.wait_ge(taylor_done, NROT * k + i + 1)
                    nc.tensor.matmul(exp_bank[i][:, 0:P], gens_t[:, i, :], power[:, i, 0, :], start=True,
                                     stop=True).then_inc(taylor_mm, 1)
            for i in range(NROT):
                pe.wait_ge(taylor_done, NROT * (DEGREE - 1) + i + 1)
                nc.tensor.transpose(exp_bank[i][:, 0:P], power[:, i, 0, :], chip.ident[:]).then_inc(turned, 1)
            for j in range(SQUARINGS):
                for i in range(NROT):
                    if j:
                        pe.wait_ge(square_kept, NROT * (j - 1) + i + 1)
                    else:
                        pe.wait_ge(turned_kept, i + 1)
                    for t in (0, 1):
                        last = nc.tensor.matmul(exp_bank[i][:, t * P:(t + 1) * P], power[:, i, 1 - t, :],
                                                power[:, i, t, :], start=True, stop=True)
                    last.then_inc(squared, 1)
                if j == 8:
                    front.turn_step(pe, 0, 0)
                if j == 10:
                    pe.wait_ge(loaded_small, 48)
                    front.logits_step(pe, 0, 0)
                if j == SQUARINGS - 1:
                    front.rows_turn_step(pe, 0, 0)
            pe.wait_ge(square_kept, NROT * SQUARINGS)
            nc.tensor.matmul(exp_bank[0][:, 0:P], power[:, 1, 0, :], power[:, 0, 1, :], start=True, stop=True).then_inc(
                rot_mm, 1)
            pe.wait_ge(rot_kept, 1)
            nc.tensor.matmul(exp_bank[0][:, 0:P], rot12_t[:, 0, :], power[:, 2, 0, :], start=True, stop=True).then_inc(
                rot_mm, 1)



class Front:

    def __init__(self, chip, name, base, behind, twice, affine, split):
        self.chip, self.base, self.behind, self.turn_bank = chip, base, behind, chip.bank[TURN]
        self.twice, self.affine, self.split = twice, affine, split
        s = chip.sem
        self.stats_done, self.moments_done = s(name + "_stats_done"), s(name + "_moments_done")
        self.r_step, self.xs_ready = s(name + "_r_step"), s(name + "_xs_ready")
        self.turned, self.xt_ready = s(name + "_turned"), s(name + "_xt_ready")
        self.r_steps = 6 if twice else 2
        self.xt_steps = 3 if split else 1

    def moments_step(self, dve, c, p):
        nc, chip, n = self.chip.nc, self.chip, self.base + c
        for t in range(TPC):
            nc.vector.bn_stats(chip.stats[:, t, :], chip.x[:, bass.ds(TPC * c + t, 1), :]).then_inc(self.stats_done, 1)
        wait_alone(dve, self.stats_done, TPC * n + TPC, chip.sem("dve_passed"))
        for t in range(TPC):
            nc.vector.bn_aggr(chip.moments[:, p, t, :], chip.stats[:, t, :]).then_inc(self.moments_done, 1)

    def power_step(self, pool, c, p):
        nc, chip, n = self.chip.nc, self.chip, self.base + c
        var = chip.moments[:, p, :, 1]
        pool.wait_ge(self.moments_done, TPC * n + TPC)
        if known(c) != 0:
            wait_alone(pool, self.r_step, self.r_steps * n, chip.sem("pool_passed"))
        elif self.behind:
            pool.wait_ge(self.behind.r_step, self.behind.r_steps * (self.behind.base + NCH))
        nc.gpsimd.tensor_scalar(chip.powed[:, 0, :], var, 1.0, EPS, ALU.mult, ALU.add).then_inc(self.r_step, 1)
        k = 1
        if self.twice:
            nc.gpsimd.tensor_scalar(chip.powed[:, 1, :], var, 1.0 + EPS, EPS * EPS, ALU.mult, ALU.add).then_inc(
                self.r_step, 1)
            k = 2
        pool.wait_ge(self.r_step, self.r_steps * n + k)
        nc.gpsimd.tensor_tensor(chip.r_std[:, p, 0:k, :], chip.powed[:, 0:k, :],
                                chip.neg_half[:, 0:k * TPC].rearrange("p (a t) -> p a t", a=k), ALU.pow).then_inc(
                                    self.r_step, 1)
        if self.twice:
            pool.wait_ge(self.r_step, self.r_steps * n + 3)
            nc.gpsimd.tensor_tensor(chip.mean_r[:], chip.moments[:, p, :, 0], chip.r_std[:, p, 0, :],
                                    ALU.mult).then_inc(self.r_step, 1)
            nc.gpsimd.tensor_scalar(chip.keep_scale[:, p, :], chip.r_std[:, p, 0, :], 0.5, 1.0, ALU.mult,
                                    ALU.add).then_inc(self.r_step, 1)
            wait_alone(pool, self.r_step, self.r_steps * n + 4, chip.sem("pool_passed"))
            nc.gpsimd.tensor_scalar(chip.keep_shift[:, p, :], chip.mean_r[:], -0.5, 0.0, ALU.mult,
                                    ALU.add).then_inc(self.r_step, 1)

    def normed_step(self, dve, c, p):
        nc, chip, n = self.chip.nc, self.chip, self.base + c
        if known(c) != 0:
            dve.wait_ge(self.turned, n)
        dve.wait_ge(self.r_step, self.r_steps * n + self.r_steps)
        for t in range(TPC):
            nc.vector.tensor_scalar(chip.xs[:, t, :].unsqueeze(1), chip.x[:, bass.ds(TPC * c + t, 1), :],
                                    chip.moments[:, p, t, 0:1], chip.r_std[:, p, int(self.twice), t:t + 1],
                                    ALU.subtract, ALU.mult).then_inc(self.xs_ready, 1)

    def turn_step(self, pe, c, p):
        nc, chip, n = self.chip.nc, self.chip, self.base + c
        if known(c) != 0:
            self.wait_bank(pe, c)
        elif self.behind:
            self.behind.wait_bank(pe, NCH)
        pe.wait_ge(self.xs_ready, TPC * n + TPC)
        for t in range(TPC):
            last = nc.tensor.transpose(self.turn_bank[:, t * P:(t + 1) * P], chip.xs[:, t, :], chip.ident[:])
        last.then_inc(self.turned, 1)

    def keep_step(self, dve, c, p):
        nc, chip, n = self.chip.nc, self.chip, self.base + c
        dve.wait_ge(self.turned, n + 1)
        if self.affine:
            nc.vector.tensor_scalar(chip.xt[:, p, :], self.turn_bank[:], chip.cols[:, COL["gamma"]],
                                    chip.cols[:, COL["beta"]], ALU.mult, ALU.add).then_inc(self.xt_ready, 1)
        else:
            nc.vector.tensor_copy(chip.xt[:, p, :], self.turn_bank[:]).then_inc(self.xt_ready, 1)

    def keep_by_scalar(self, act, c, p):
        nc, chip, n = self.chip.nc, self.chip, self.base + c
        act.wait_ge(self.turned, n + 1)
        nc.scalar.activation(chip.xt[:, p, :], self.turn_bank[:], ACT.Copy).then_inc(self.xt_ready, 1)

    def split_step(self, dve, c, p):
        nc, chip, n = self.chip.nc, self.chip, self.base + c
        if self.split:
            dve.wait_ge(self.xt_ready, self.xt_steps * n + 1)
            nc.vector.tensor_copy(chip.xt_hi[:, p, :], chip.xt[:, p, :]).then_inc(self.xt_ready, 1)
            dve.wait_ge(self.xt_ready, self.xt_steps * n + 2)
            nc.vector.tensor_tensor(chip.xt_lo[:, p, :], chip.xt[:, p, :], chip.xt_hi[:, p, :].bitcast(F32),
                                    ALU.subtract).then_inc(self.xt_ready, 1)

    def wait_xt(self, eng, c):
        eng.wait_ge(self.xt_ready, self.xt_steps * (self.base + c) + self.xt_steps)

    routed = 0

    def logits_step(self, pe, c, p):
        pass

    def rows_turn_step(self, pe, c, p):
        pass

    def pair_step(self, act, c, p):
        pass

    def rows_kept_step(self, act, c, p):
        pass

    def route_first(self, dve, c, p):
        pass

    def route_second(self, dve, c, p):
        pass

    def route_last(self, dve, c, p):
        pass

    def wait_bank(self, pe, c):
        pass

    def wait_routed(self, dve, c):
        if known(c) != 0:
            dve.wait_ge(self.route_step, self.routed * (self.base + c))
        elif self.behind and self.behind.routed:
            dve.wait_ge(self.behind.route_step, self.behind.routed * (self.behind.base + NCH))


class Front0(Front):
    PAIR = TPC + 2
    ROUTE = routed = PAIR + TPC + 2 + 2 + 2 + 3

    def __init__(self, chip, call, behind):
        super().__init__(chip, "ffn0", call * NCH, behind, twice=True, affine=True, split=True)
        self.logits_done, self.route_step, self.pair_tanh, self.rows_turn, self.rows_kept = (
            chip.sem("ffn0_" + k) for k in ("logits_done", "route_step", "pair_tanh", "rows_turn", "rows_kept"))

    def wait_bank(self, pe, c):
        wait(pe, self.rows_kept, self.base + c)

    def logits_step(self, pe, c, p):
        nc, chip, n = self.chip.nc, self.chip, self.base + c
        self.wait_xt(pe, c)
        for t in range(TPC):
            last = nc.tensor.matmul(self.turn_bank[:, t * E0:(t + 1) * E0], chip.xt[:, p, t * P:(t + 1) * P],
                                    chip.mats[:, MAT["gate"]], start=True, stop=True)
        last.then_inc(self.logits_done, 1)

    def rows_turn_step(self, pe, c, p):
        nc, chip, n = self.chip.nc, self.chip, self.base + c
        pe.wait_ge(self.route_step, self.ROUTE * n + self.ROUTE)
        for t in range(TPC):
            last = nc.tensor.transpose(self.turn_bank[0:2 * E0, t * P:(t + 1) * P],
                                       chip.w_split[:, t, :].bitcast(F32), chip.ident[:])
        last.then_inc(self.rows_turn, 1)

    def pair_step(self, act, c, p):
        nc, chip, n = self.chip.nc, self.chip, self.base + c
        act.wait_ge(self.route_step, self.ROUTE * n + self.PAIR)
        nc.scalar.activation(chip.pair[:, 1, :], chip.pair[:, 0, :], ACT.Tanh, scale=0.5).then_inc(self.pair_tanh, 1)

    def rows_kept_step(self, act, c, p):
        nc, chip, n = self.chip.nc, self.chip, self.base + c
        act.wait_ge(self.rows_turn, n + 1)
        nc.scalar.activation(chip.w_turned[:, p, :], self.turn_bank[0:2 * E0, :], ACT.Copy).then_inc(self.rows_kept, 1)

    def route_first(self, dve, c, p):
        nc, chip, n = self.chip.nc, self.chip, self.base + c
        r = self.ROUTE * n
        dve.wait_ge(self.logits_done, n + 1)
        self.wait_routed(dve, c)
        nc.vector.tensor_tensor(chip.logits0[:], self.turn_bank[:, 0:TPC * E0].rearrange(
            "p (t e) -> p t e", t=TPC), across(chip.rows[:, ROW["gate_b"]].unsqueeze(1), [P, TPC, E0]),
            ALU.add).then_inc(self.route_step, 1)
        wait_alone(dve, self.route_step, r + 1, chip.sem("dve_passed"))
        for t in range(TPC):
            nc.vector.max(chip.best[:, t, :], chip.logits0[:, t, :]).then_inc(self.route_step, 1)
        dve.wait_ge(self.route_step, r + 1 + TPC)
        nc.vector.tensor_tensor(chip.pair[:, 0, :], chip.best[:, :, 1], chip.best[:, :, 0],
                                ALU.subtract).then_inc(self.route_step, 1)
        for t in range(TPC):
            nc.vector.max_index(chip.best_at[:, t, :], chip.best[:, t, :], chip.logits0[:, t, :]).then_inc(
                self.route_step, 1)
        dve.wait_ge(self.route_step, r + self.PAIR + TPC)
        for k, one in enumerate((chip.one_a, chip.one_b)):
            nc.vector.tensor_tensor(one[:], across(chip.iota_row[:, 0:E0].unsqueeze(1), [P, TPC, E0]),
                                    across(chip.best_at[:, :, k:k + 1], [P, TPC, E0]), ALU.is_equal).then_inc(
                                        self.route_step, 1)

    def route_second(self, dve, c, p):
        nc, chip, n = self.chip.nc, self.chip, self.base + c
        r = self.ROUTE * n + self.PAIR + TPC + 2
        dve.wait_ge(self.pair_tanh, n + 1)
        for k, sign in enumerate((-0.5, 0.5)):
            nc.vector.tensor_scalar(chip.pair_w[:, k, :], chip.pair[:, 1, :], sign, 0.5, ALU.mult,
                                    ALU.add).then_inc(self.route_step, 1)
        dve.wait_ge(self.route_step, r + 2)
        for k, one in enumerate((chip.one_a, chip.one_b)):
            nc.vector.tensor_tensor(one[:], one[:], across(chip.pair_w[:, k, :].unsqueeze(2), [P, TPC, E0]),
                                    ALU.mult).then_inc(self.route_step, 1)
        dve.wait_ge(self.route_step, r + 4)
        nc.vector.tensor_tensor(chip.one_a[:], chip.one_a[:], chip.one_b[:], ALU.add).then_inc(self.route_step, 1)
        dve.wait_ge(self.route_step, r + 5)
        wait(dve, self.rows_turn, n)
        nc.vector.tensor_copy(chip.w_split[:, :, 0:E0], chip.one_a[:]).then_inc(self.route_step, 1)
        dve.wait_ge(self.route_step, r + 6)
        nc.vector.tensor_tensor(chip.w_split[:, :, E0:2 * E0], chip.one_a[:],
                                chip.w_split[:, :, 0:E0].bitcast(F32), ALU.subtract).then_inc(self.route_step, 1)


class Front1(Front):
    ROUTE = routed = 2 + 2 * TPC

    def __init__(self, chip, call, behind):
        super().__init__(chip, "ffn1", call * NCH, behind, twice=False, affine=False, split=True)
        self.logits_done, self.route_step, self.rows_turn, self.rows_kept, self.blocked_made = (
            chip.sem("ffn1_" + k) for k in ("logits_done", "route_step", "rows_turn", "rows_kept", "blocked_made"))

    def wait_bank(self, pe, c):
        wait(pe, self.rows_kept, self.base + c)

    def logits_step(self, pe, c, p):
        nc, chip, n = self.chip.nc, self.chip, self.base + c
        self.wait_xt(pe, c)
        for t in range(TPC):
            last = nc.tensor.matmul(self.turn_bank[:, t * E1:(t + 1) * E1], chip.xt[:, p, t * P:(t + 1) * P],
                                    chip.mats[:, MAT["router"]], start=True, stop=True)
        last.then_inc(self.logits_done, 1)

    def rows_turn_step(self, pe, c, p):
        nc, chip, n = self.chip.nc, self.chip, self.base + c
        wait_alone(pe, self.route_step, self.ROUTE * n + self.ROUTE, chip.sem("pe_passed"))
        for t in range(TPC):
            last = nc.tensor.transpose(self.turn_bank[0:2 * E1, t * P:(t + 1) * P], chip.chosen[:, t, :],
                                       chip.ident[:])
        last.then_inc(self.rows_turn, 1)

    def rows_kept_step(self, act, c, p):
        nc, chip, n = self.chip.nc, self.chip, self.base + c
        act.wait_ge(self.rows_turn, n + 1)
        nc.scalar.activation(chip.chosen_t[:, p, :], self.turn_bank[0:2 * E1, :], ACT.Copy).then_inc(self.rows_kept, 1)

    def route_first(self, dve, c, p):
        nc, chip, n = self.chip.nc, self.chip, self.base + c
        r = self.ROUTE * n
        dve.wait_ge(self.logits_done, n + 1)
        self.wait_routed(dve, c)
        nc.vector.tensor_tensor(chip.logits1[:], self.turn_bank[:, 0:TPC * E1].rearrange(
            "p (t e) -> p t e", t=TPC), across(chip.rows[:, ROW["router_b"]].unsqueeze(1), [P, TPC, E1]),
            ALU.add).then_inc(self.route_step, 1)
        wait_alone(dve, self.route_step, r + 1, chip.sem("dve_passed"))
        for t in range(TPC):
            nc.vector.max(chip.best[:, t, :], chip.logits1[:, t, :]).then_inc(self.route_step, 1)
        wait_alone(dve, self.route_step, r + 1 + TPC, chip.sem("dve_passed"))
        for t in range(TPC):
            nc.vector.max_index(chip.best_at[:, t, :], chip.best[:, t, :], chip.logits1[:, t, :]).then_inc(
                self.route_step, 1)
        dve.wait_ge(self.route_step, r + 1 + 2 * TPC)
        wait(dve, self.rows_turn, n)
        nc.vector.tensor_tensor(chip.chosen[:], across(chip.iota_row[:].unsqueeze(1), [P, TPC, 2 * E1]),
                                across(chip.best_at[:, :, 0:1], [P, TPC, 2 * E1]), ALU.is_equal).then_inc(
                                    self.route_step, 1)

    def route_last(self, dve, c, p):
        nc, chip, n = self.chip.nc, self.chip, self.base + c
        dve.wait_ge(self.rows_kept, n + 1)
        nc.vector.tensor_scalar(chip.blocked_t[0:E1, p, :], chip.chosen_t[0:E1, p, :].bitcast(F32), -1.0, None,
                                ALU.add).then_inc(self.blocked_made, 1)


def coming(front, ahead, c, p):
    if known(c) == NCH - 1:
        return ahead, 0, 0
    return front, c + 1, 1 - p



def ffn0_stage(chip, front, ahead):
    nc, x = chip.nc, chip.x
    base = front.base

    def s(name):
        return chip.sem("ffn0_" + name)

    H, OUT, WIDE, TOKEN_MAJOR = (0, 1), (2, 3), (4, 5), 7
    ROT = ABEL = TOKEN_MAJOR
    LAG, WIDE_LAG = LAG0, WIDE_LAG0
    hid, wide_w, weighted, moe, abel, abel_pre, kept, diff, dots_a, dots_b = chip.rooms(
        (4, CH), (4, CH), (2, CH), (2, CH), (2, CH), (CH,), (TPC, P), (TPC, P), (TPC, P), (TPC, P))
    tiles = "p (t d) -> p t d"

    hid_done, gelu_done, hi_done = s("hid_done"), s("gelu_done"), s("hi_done")
    lo_even, lo_odd = s("lo_even"), s("lo_odd")
    wide_mm, wide_ready, out_done = s("wide_mm"), s("wide_ready"), s("out_done")
    weighted_done, moe_added = s("weighted_done"), s("moe_added")
    abel_mm, abel_biased, abel_done = s("abel_mm"), s("abel_biased"), s("abel_done")
    rot_mm, tail_step, gate_tanh, x_new, kept_done = (
        s("rot_mm"), s("tail_step"), s("gate_tanh"), s("x_new"), s("kept_done"))
    DOTS = 2 * TPC + 1
    TAIL = DOTS + 3

    with nc.Block() as block:
        @block.tensor
        def _(pe):
            def hidden(c, p, e):
                if e == 0:
                    front.wait_xt(pe, c)
                for j in range(HC):
                    u = HC * e + j
                    wait(pe, gelu_done, U0 * (base + c) + u - 1)
                    for k, (w, v) in enumerate(((chip.ew1_hi, chip.xt_hi), (chip.ew1_hi, chip.xt_lo),
                                                (chip.ew1_lo, chip.xt_hi))):
                        last = nc.tensor.matmul(chip.bank[H[u % 2]][:], w[:, u, :], v[:, p, :], start=k == 0,
                                                stop=k == 2)
                    last.then_inc(hid_done, 1)

            def widen(c, p, e):
                if e == 0:
                    pe.wait_ge(front.rows_kept, base + c + 1)
                wait(pe, wide_ready, E0 * (base + c) + e - 1)
                nc.tensor.matmul(chip.bank[WIDE[e % 2]][:], chip.pick_expert[:, e, :], chip.w_turned[:, p, :],
                                 start=True, stop=True).then_inc(wide_mm, 1)

            def out_product(c, e):
                n = E0 * (base + c) + e
                pe.wait_ge(lo_even, n + 1)
                pe.wait_ge(lo_odd, n + 1)
                wait(pe, weighted_done, n - 1)
                k = 0
                for j in range(HC):
                    u = HC * e + j
                    for w, v in ((chip.ew2_hi, chip.hid_hi), (chip.ew2_hi, chip.hid_lo), (chip.ew2_lo, chip.hid_hi)):
                        last = nc.tensor.matmul(chip.bank[OUT[e % 2]][:], w[:, u, :], v[:, u % 8, :], start=k == 0,
                                                stop=k == 5)
                        k += 1
                last.then_inc(out_done, 1)

            def abel_step(c, p):
                if known(c) != 0:
                    pe.wait_ge(tail_step, TAIL * (base + c - 1) + DOTS + 1)
                for t in range(TPC):
                    last = nc.tensor.matmul(chip.bank[ABEL][:, t * P:(t + 1) * P], chip.xt[:, p, t * P:(t + 1) * P],
                                            chip.mats[:, MAT["abel"]], start=True, stop=True)
                last.then_inc(abel_mm, 1)

            def rot_step(c, p):
                pe.wait_ge(moe_added, (E0 - 1) * (base + c) + E0 - 1)
                pe.wait_ge(abel_biased, base + c + 1)
                for t in range(TPC):
                    last = nc.tensor.matmul(chip.bank[ROT][:, t * P:(t + 1) * P], moe[:, p, t * P:(t + 1) * P],
                                            chip.rotation[:], start=True, stop=True)
                last.then_inc(rot_mm, 1)

            def between(slot, c, p):
                if slot == AT0["abel_mm"]:
                    abel_step(c, p)
                if slot == AT0["rot"] and known(c) != 0:
                    rot_step(c - 1, 1 - p)
                f, n, q = coming(front, ahead, c, p)
                if f:
                    if slot == AT0["turn"]:
                        f.turn_step(pe, n, q)
                    if slot == AT0["logits"]:
                        f.logits_step(pe, n, q)
                    if slot == AT0["w_turn"]:
                        f.rows_turn_step(pe, n, q)

            def body(c, p):
                for e in range(E0):
                    hidden(c, p, e)
                    between(2 * e, c, p)
                    if e >= WIDE_LAG:
                        widen(c, p, e - WIDE_LAG)
                    elif known(c) != 0:
                        widen(c - 1, 1 - p, e - WIDE_LAG + E0)
                    if e >= LAG:
                        out_product(c, e - LAG)
                    elif known(c) != 0:
                        out_product(c - 1, e - LAG + E0)
                    between(2 * e + 1, c, p)

            chunks(pe, body)
            for e in range(E0 - WIDE_LAG, E0):
                widen(NCH - 1, 1, e)
            for e in range(E0 - LAG, E0):
                out_product(NCH - 1, e)
            rot_step(NCH - 1, 1)

        @block.scalar
        def _(act):
            def gelus(c, e):
                n = E0 * (base + c) + e
                for j in range(HC):
                    u = HC * e + j
                    act.wait_ge(hid_done, HC * n + j + 1)
                    wait(act, lo_odd if j else lo_even, n - 1)
                    nc.scalar.activation(hid[:, u % 4, :], chip.bank[H[u % 2]][:], ACT.Gelu,
                                         bias=chip.cols[:, COL["eb1"]][:, u:u + 1]).then_inc(gelu_done, 1)

            def high_parts(c, e):
                n = E0 * (base + c) + e
                wait(act, out_done, n - 3)
                for j in range(HC):
                    u = HC * e + j
                    act.wait_ge(gelu_done, HC * n + j + 1)
                    nc.scalar.activation(chip.hid_hi[:, u % 8, :], hid[:, u % 4, :], ACT.Copy).then_inc(hi_done, 1)

            def widen(c, e):
                n = E0 * (base + c) + e
                act.wait_ge(wide_mm, n + 1)
                wait(act, weighted_done, n - 3)
                nc.scalar.activation(wide_w[:, e % 4, :], chip.bank[WIDE[e % 2]][:], ACT.Copy).then_inc(wide_ready, 1)

            def abel_step(c, p):
                act.wait_ge(abel_biased, base + c + 1)
                nc.scalar.activation(abel[:, p, :], abel_pre, ACT.Gelu).then_inc(abel_done, 1)

            def gate_step(c):
                act.wait_ge(tail_step, TAIL * (base + c) + DOTS)
                nc.scalar.activation(chip.gate[:, 3, :], chip.gate[:, 2, :], ACT.Tanh, scale=0.5,
                                     bias=chip.half_gc_b[:]).then_inc(gate_tanh, 1)

            def between(slot, c, p):
                if slot == AT0["abel"]:
                    abel_step(c, p)
                if slot == AT0["gate"] and known(c) != 0:
                    gate_step(c - 1)
                f, n, q = coming(front, ahead, c, p)
                if f:
                    if slot == AT0["pair"]:
                        f.pair_step(act, n, q)
                    if slot == AT0["w_kept"]:
                        f.rows_kept_step(act, n, q)

            def body(c, p):
                for e in range(E0):
                    gelus(c, e)
                    between(2 * e, c, p)
                    high_parts(c, e)
                    if e >= WIDE_LAG:
                        widen(c, e - WIDE_LAG)
                    elif known(c) != 0:
                        widen(c - 1, e - WIDE_LAG + E0)
                    between(2 * e + 1, c, p)

            nc.scalar.preload_act_table(ACT.Gelu)
            chunks(act, body)
            for e in range(E0 - WIDE_LAG, E0):
                widen(NCH - 1, e)
            gate_step(NCH - 1)

        @block.vector
        def _(dve):
            def low(c, e):
                u = HC * e
                dve.wait_ge(hi_done, U0 * (base + c) + u + 1)
                nc.vector.tensor_tensor(chip.hid_lo[:, u % 8, :], hid[:, u % 4, :],
                                        chip.hid_hi[:, u % 8, :].bitcast(F32), ALU.subtract).then_inc(lo_even, 1)

            def weigh(c, p, e):
                n = E0 * (base + c) + e
                dve.wait_ge(out_done, n + 1)
                dve.wait_ge(wide_ready, n + 1)
                if e:
                    wait(dve, moe_added, (E0 - 1) * (base + c) + max(e - 2, 0))
                nc.vector.scalar_tensor_tensor(out=weighted[:, e % 2, :] if e else moe[:, p, :],
                                               in0=chip.bank[OUT[e % 2]][:],
                                               scalar=chip.cols[:, COL["eb2"]][:, e:e + 1], in1=wide_w[:, e % 4, :],
                                               op0=ALU.add, op1=ALU.mult).then_inc(weighted_done, 1)

            def abel_bias(c):
                dve.wait_ge(abel_mm, base + c + 1)
                wait(dve, abel_done, base + c)
                nc.vector.tensor_tensor(abel_pre.rearrange(tiles, t=TPC), chip.bank[ABEL][:].rearrange(tiles, t=TPC),
                                        across(chip.rows[:, ROW["abel_b"]].unsqueeze(1), [P, TPC, P]),
                                        ALU.add).then_inc(abel_biased, 1)

            def keep_input(c, p):
                wait(dve, x_new, TPC * (base + c))
                for t in range(TPC):
                    nc.vector.tensor_scalar(kept[:, t, :].unsqueeze(1), x[:, bass.ds(TPC * c + t, 1), :],
                                            chip.keep_scale[:, p, t:t + 1], chip.keep_shift[:, p, t:t + 1],
                                            ALU.mult, ALU.add).then_inc(kept_done, 1)

            def gate_dots(c, p, k):
                r = TAIL * (base + c)
                if k == 0:
                    dve.wait_ge(abel_done, base + c + 1)
                    wait(dve, tail_step, r)
                    v, w, dots = abel[:, p, :].rearrange(tiles, t=TPC), "gate_abel", dots_a
                else:
                    dve.wait_ge(rot_mm, base + c + 1)
                    v, w, dots = chip.bank[ROT][:].rearrange(tiles, t=TPC), "gate_moe", dots_b
                for t in range(TPC):
                    nc.vector.tensor_tensor_reduce(
                        out=dots[:, t, :], in0=v[:, t, :], in1=chip.rows[:, ROW[w]], scale=1.0, scalar=0.0,
                        op0=ALU.mult, op1=ALU.add, accum_out=chip.gate[:, k, t:t + 1]).then_inc(tail_step, 1)
                if k:
                    dve.wait_ge(tail_step, r + 2 * TPC)
                    nc.vector.tensor_tensor(chip.gate[:, 2, :], chip.gate[:, 0, :], chip.gate[:, 1, :],
                                            ALU.add).then_inc(tail_step, 1)

            def difference(c, p):
                dve.wait_ge(kept_done, TPC * (base + c) + TPC)
                nc.vector.tensor_tensor(diff, chip.bank[ROT][:].rearrange(tiles, t=TPC),
                                        abel[:, p, :].rearrange(tiles, t=TPC), ALU.subtract).then_inc(tail_step, 1)
                nc.vector.scalar_tensor_tensor(out=kept.rearrange("p t d -> p (t d)"), in0=abel[:, p, :], scalar=0.5,
                                               in1=kept.rearrange("p t d -> p (t d)"), op0=ALU.mult,
                                               op1=ALU.add).then_inc(tail_step, 1)

            def mix(c):
                r = TAIL * (base + c)
                dve.wait_ge(gate_tanh, base + c + 1)
                nc.vector.tensor_scalar(chip.gate[:, 4, :], chip.gate[:, 3, :], 0.25, 0.25, ALU.mult,
                                        ALU.add).then_inc(tail_step, 1)
                dve.wait_ge(tail_step, r + TAIL)
                for t in range(TPC):
                    nc.vector.scalar_tensor_tensor(out=x[:, bass.ds(TPC * c + t, 1), :], in0=diff[:, t:t + 1, :],
                                                   scalar=chip.gate[:, 4, t:t + 1], in1=kept[:, t:t + 1, :],
                                                   op0=ALU.mult, op1=ALU.add).then_inc(x_new, 1)

            def between(slot, c, p):
                if slot == AT0["abel_bias"]:
                    abel_bias(c)
                if known(c) != 0:
                    if slot == AT0["dots_abel"]:
                        gate_dots(c - 1, 1 - p, 0)
                    if slot == AT0["dots_moe"]:
                        gate_dots(c - 1, 1 - p, 1)
                    if slot == AT0["difference"]:
                        difference(c - 1, 1 - p)
                    if slot == AT0["mix"]:
                        mix(c - 1)
                if slot == AT0["keep_input"]:
                    keep_input(c, p)
                f, n, q = coming(front, ahead, c, p)
                if f:
                    if slot == AT0["moments"]:
                        f.moments_step(dve, n, q)
                    if slot == AT0["normed"]:
                        f.normed_step(dve, n, q)
                    if slot == AT0["keep"]:
                        f.keep_step(dve, n, q)
                    if slot == AT0["split"]:
                        f.split_step(dve, n, q)
                    if slot == AT0["route_pair"]:
                        f.route_first(dve, n, q)
                    if slot == AT0["route_weights"]:
                        f.route_second(dve, n, q)

            def body(c, p):
                for e in range(E0):
                    low(c, e)
                    between(2 * e, c, p)
                    if e >= LAG:
                        weigh(c, p, e - LAG)
                    elif known(c) != 0:
                        weigh(c - 1, 1 - p, e - LAG + E0)
                    between(2 * e + 1, c, p)

            chunks(dve, body)
            for e in range(E0 - LAG, E0):
                weigh(NCH - 1, 1, e)
            gate_dots(NCH - 1, 1, 0)
            gate_dots(NCH - 1, 1, 1)
            difference(NCH - 1, 1)
            mix(NCH - 1)
            if ahead:
                ahead.route_last(dve, 0, 0)

        @block.gpsimd
        def _(pool):
            def low(c, e):
                u = HC * e + 1
                pool.wait_ge(hi_done, U0 * (base + c) + u + 1)
                nc.gpsimd.tensor_tensor(chip.hid_lo[:, u % 8, :], hid[:, u % 4, :],
                                        chip.hid_hi[:, u % 8, :].bitcast(F32), ALU.subtract).then_inc(lo_odd, 1)

            def add(c, p, e):
                if e == 0:
                    return
                pool.wait_ge(weighted_done, E0 * (base + c) + e + 1)
                wait(pool, moe_added, (E0 - 1) * (base + c) + e - 1)
                nc.gpsimd.tensor_tensor(moe[:, p, :], moe[:, p, :], weighted[:, e % 2, :], ALU.add).then_inc(
                    moe_added, 1)

            def body(c, p):
                for e in range(E0):
                    low(c, e)
                    if e >= LAG:
                        add(c, p, e - LAG)
                    elif known(c) != 0:
                        add(c - 1, 1 - p, e - LAG + E0)
                    f, n, q = coming(front, ahead, c, p)
                    if e == AT0["power"] and f:
                        f.power_step(pool, n, q)

            chunks(pool, body)
            for e in range(E0 - LAG, E0):
                add(NCH - 1, 1, e)



def ffn1_stage(chip, front, ahead, out):
    nc, x = chip.nc, chip.x
    base = front.base

    def s(name):
        return chip.sem("ffn1_" + name)

    H, SUM, BACK = (0, 1, 2, 3), (4, 5), 7
    LAG = LAG1
    y_t, = chip.rooms((CH,))
    tiles = "p (t d) -> p t d"

    hid_done, hi_done, lo_done = s("hid_done"), s("hi_done"), s("lo_done")
    out_mm, sum_done = s("out_mm"), s("sum_done")
    y_ready, back_done, x_new, stored = s("y_ready"), s("back_done"), s("x_new"), s("stored")

    with nc.Block() as block:
        @block.sync
        def _(sp):
            if ahead:
                return
            for c in range(NCH):
                sp.wait_ge(x_new, base + c + 1)
                sp.dma_start(out[c * CH:(c + 1) * CH, :].rearrange("(t p) d -> p t d", p=P),
                             x[:, c * TPC:(c + 1) * TPC, :]).then_inc(stored, 16)
            sp.wait_ge(stored, 16 * NCH)

        @block.tensor
        def _(pe):
            def hidden(c, p, u):
                if u == 0:
                    front.wait_xt(pe, c)
                    pe.wait_ge(front.blocked_made, base + c + 1)
                wait(pe, lo_done, U1 * (base + c) + u - 3)
                b = chip.bank[H[u % 4]]
                nc.tensor.matmul(b[:], chip.block_expert[:, u, :], chip.blocked_t[:, p, :], start=True, stop=False)
                for k, (w, v) in enumerate(((chip.w1_hi, chip.xt_hi), (chip.w1_hi, chip.xt_lo),
                                            (chip.w1_lo, chip.xt_hi))):
                    last = nc.tensor.matmul(b[:], w[:, u, :], v[:, p, :], start=False, stop=k == 2)
                last.then_inc(hid_done, 1)

            def out_product(c, p, u):
                n = U1 * (base + c) + u
                pe.wait_ge(lo_done, n + 1)
                b = chip.bank[SUM[p]]
                for k, (w, v) in enumerate(((chip.w2_hi, chip.hid_hi), (chip.w2_hi, chip.hid_lo),
                                            (chip.w2_lo, chip.hid_hi))):
                    last = nc.tensor.matmul(b[:], w[:, u, :], v[:, u, :], start=u == 0 and k == 0, stop=False)
                last.then_inc(out_mm, 1)
                if u == U1 - 1:
                    nc.tensor.matmul(b[:], chip.b2_split[:], chip.chosen_t[:, p, :], start=False, stop=True).then_inc(
                        sum_done, 1)

            def back_step(c):
                pe.wait_ge(y_ready, base + c + 1)
                wait(pe, x_new, base + c)
                for t in range(TPC):
                    last = nc.tensor.transpose(chip.bank[BACK][:, t * P:(t + 1) * P], y_t[:, t * P:(t + 1) * P],
                                               chip.ident[:])
                last.then_inc(back_done, 1)

            def between(slot, c, p):
                if slot == AT1["back"] and known(c) != 0:
                    back_step(c - 1)
                f, n, q = coming(front, ahead, c, p)
                if f:
                    if slot == AT1["turn"]:
                        f.turn_step(pe, n, q)
                    if slot == AT1["logits"]:
                        f.logits_step(pe, n, q)
                    if slot == AT1["one_turn"]:
                        f.rows_turn_step(pe, n, q)

            def body(c, p):
                for u in range(U1):
                    hidden(c, p, u)
                    between(2 * u, c, p)
                    if u >= LAG:
                        out_product(c, p, u - LAG)
                    elif known(c) != 0:
                        out_product(c - 1, 1 - p, u - LAG + U1)
                    between(2 * u + 1, c, p)

            chunks(pe, body)
            for u in range(U1 - LAG, U1):
                out_product(NCH - 1, 1, u)
            back_step(NCH - 1)

        @block.scalar
        def _(act):
            def high_part(c, u):
                n = U1 * (base + c) + u
                act.wait_ge(hid_done, n + 1)
                wait(act, out_mm, n - 7)
                nc.scalar.activation(chip.hid_hi[:, u, :], chip.bank[H[u % 4]][:], ACT.Relu).then_inc(hi_done, 1)

            def y_step(c, p):
                act.wait_ge(sum_done, base + c + 1)
                wait(act, back_done, base + c)
                nc.scalar.activation(y_t, chip.bank[SUM[p]][:], ACT.Relu).then_inc(y_ready, 1)

            def between(slot, c, p):
                if slot == AT1["y"] and known(c) != 0:
                    y_step(c - 1, 1 - p)
                f, n, q = coming(front, ahead, c, p)
                if slot == AT1["one_kept"] and f:
                    f.rows_kept_step(act, n, q)

            def body(c, p):
                for u in range(U1):
                    high_part(c, u)
                    between(u, c, p)

            nc.scalar.preload_act_table(ACT.Relu)
            chunks(act, body)
            y_step(NCH - 1, 1)

        @block.vector
        def _(dve):
            def low(c, u):
                dve.wait_ge(hi_done, U1 * (base + c) + u + 1)
                nc.vector.scalar_tensor_tensor(out=chip.hid_lo[:, u, :], in0=chip.bank[H[u % 4]][:], scalar=0.0,
                                               in1=chip.hid_hi[:, u, :].bitcast(F32), op0=ALU.max,
                                               op1=ALU.subtract).then_inc(lo_done, 1)

            def add_step(c):
                dve.wait_ge(back_done, base + c + 1)
                tile = x[:, bass.ds(TPC * c, TPC), :]
                nc.vector.scalar_tensor_tensor(out=tile, in0=chip.bank[BACK][:].rearrange(tiles, t=TPC), scalar=0.5,
                                               in1=tile, op0=ALU.mult, op1=ALU.add).then_inc(x_new, 1)

            def between(slot, c, p):
                if slot == AT1["add"] and known(c) != 0:
                    add_step(c - 1)
                f, n, q = coming(front, ahead, c, p)
                if f:
                    if slot == AT1["moments"]:
                        f.moments_step(dve, n, q)
                    if slot == AT1["normed"]:
                        f.normed_step(dve, n, q)
                    if slot == AT1["keep"]:
                        f.keep_step(dve, n, q)
                    if slot == AT1["split"]:
                        f.split_step(dve, n, q)
                    if slot == AT1["route"]:
                        f.route_first(dve, n, q)
                    if slot == AT1["block"]:
                        f.route_last(dve, n, q)

            def body(c, p):
                for u in range(U1):
                    low(c, u)
                    between(u, c, p)

            chunks(dve, body)
            add_step(NCH - 1)

        @block.gpsimd
        def _(pool):
            def body(c, p):
                f, n, q = coming(front, ahead, c, p)
                if f:
                    f.power_step(pool, n, q)

            chunks(pool, body)



def attn0_stage(chip, front, ahead):
    nc, x = chip.nc, chip.x

    def s(name):
        return chip.sem("attn0_" + name)

    QB, KB, VB, SCORES, ATT, LOCAL, WIDE = 0, 1, 2, 3, 4, 5, 7
    NS = TOKENS // SEG
    NB = NS // BATCH
    local, q_t, k_t, v_tok, att, att_t, wide, o_t, firsts, glob = chip.rooms(
        (TOKENS,), (CH,), (CH,), (2, CH), (TPC, P), (CH,), (TPC, P), (2, CH), (3, P), (5, P))
    first_q, first_k, first_x = firsts[:, 0, :], firsts[:, 1, :], firsts[:, 2, :]
    g_v, g_att, g_att_t, g_out, g_sc = (glob[:, k, :] for k in range(5))
    sc = wide[:, 0, :].rearrange("p (t j) -> p t j", t=TPC)
    ex = wide[:, 1, :].rearrange("p (t j) -> p t j", t=TPC)
    top, total, inv = (wide[:, 2, 8 * k:8 * k + TPC] for k in range(3))
    tiles = "p (t d) -> p t d"

    zeroed, q_mm, k_mm, v_mm = s("zeroed"), s("q_mm"), s("k_mm"), s("v_mm")
    q_kept, k_kept, v_kept, firsts_kept = s("q_kept"), s("k_kept"), s("v_kept"), s("firsts_kept")
    scores_done, soft_step, exp_done = s("scores_done"), s("soft_step"), s("exp_done")
    att_turn, att_kept, local_mm, local_kept = s("att_turn"), s("att_kept"), s("local_mm"), s("local_kept")
    g_mm, g_step, g_exp, g_v_kept = s("g_mm"), s("g_step"), s("g_exp"), s("g_v_kept")
    o_ready, o_mm, bo_added, x_new = s("o_ready"), s("o_mm"), s("bo_added"), s("x_new")
    SOFT = SPT + 1 + 1 + 1 + 1 + SPT
    G_ATT = 4 + 2 * BATCH

    with nc.Block() as block:
        @block.tensor
        def _(pe):
            def qk_step(c, p):
                front.wait_xt(pe, c)
                wait(pe, q_kept, c)
                nc.tensor.matmul(chip.bank[QB][:], chip.mats[:, MAT["q0"]], chip.xt[:, p, :], start=True,
                                 stop=True).then_inc(q_mm, 1)
                wait(pe, k_kept, c)
                nc.tensor.matmul(chip.bank[KB][:], chip.mats[:, MAT["k0"]], chip.xt[:, p, :], start=True,
                                 stop=True).then_inc(k_mm, 1)

            def v_step(c, p):
                wait(pe, v_kept, c)
                for t in range(TPC):
                    last = nc.tensor.matmul(chip.bank[VB][:, t * P:(t + 1) * P], chip.xt[:, p, t * P:(t + 1) * P],
                                            chip.mats[:, MAT["v0"]], start=True, stop=True)
                last.then_inc(v_mm, 1)

            def scores(c):
                pe.wait_ge(q_kept, c + 1)
                pe.wait_ge(k_kept, c + 1)
                for t in range(TPC):
                    last = nc.tensor.matmul(chip.bank[SCORES][:, t * P:(t + 1) * P], q_t[:, t * P:(t + 1) * P],
                                            k_t[:, t * P:(t + 1) * P], start=True, stop=True)
                last.then_inc(scores_done, 1)

            def att_turn_step(c):
                pe.wait_ge(soft_step, SOFT * c + SOFT)
                for t in range(TPC):
                    last = nc.tensor.transpose(chip.bank[ATT][:, t * P:(t + 1) * P], att[:, t, :], chip.ident[:])
                last.then_inc(att_turn, 1)

            def local_step(c, p):
                pe.wait_ge(att_kept, c + 1)
                pe.wait_ge(v_kept, c + 1)
                wait(pe, local_kept, c)
                for t in range(TPC):
                    last = nc.tensor.matmul(chip.bank[LOCAL][:, t * P:(t + 1) * P], v_tok[:, p, t * P:(t + 1) * P],
                                            att_t[:, t * P:(t + 1) * P], start=True, stop=True)
                last.then_inc(local_mm, 1)

            def body(c, p):
                qk_step(c, p)
                if known(c) != 0:
                    att_turn_step(c - 1)
                v_step(c, p)
                scores(c)
                if known(c) != NCH - 1:
                    front.turn_step(pe, c + 1, 1 - p)
                if known(c) != 0:
                    local_step(c - 1, 1 - p)

            chunks(pe, body)

            pe.wait_ge(firsts_kept, 3 * NCH)
            pe.wait_ge(v_kept, NCH)
            nc.tensor.matmul(chip.bank[WIDE][:, 0:P], first_q, first_k, start=True, stop=True).then_inc(g_mm, 1)
            nc.tensor.matmul(chip.bank[VB][:, 0:P], first_x, chip.mats[:, MAT["v0"]], start=True, stop=True).then_inc(
                g_mm, 1)
            att_turn_step(NCH - 1)
            local_step(NCH - 1, 1)
            pe.wait_ge(g_step, G_ATT)
            nc.tensor.transpose(chip.bank[WIDE][:, 0:P], g_att, chip.ident[:]).then_inc(g_mm, 1)
            pe.wait_ge(g_step, G_ATT + 1)
            pe.wait_ge(g_v_kept, 1)
            nc.tensor.matmul(chip.bank[VB][:, 0:P], g_v, g_att_t, start=True, stop=True).then_inc(g_mm, 1)

            def out_body(c, p):
                pe.wait_ge(o_ready, c + 1)
                if known(c) not in (0, 1):
                    pe.wait_ge(x_new, c - 1)
                for t in range(TPC):
                    last = nc.tensor.matmul(chip.bank[(QB, KB)[p]][:, t * P:(t + 1) * P],
                                            o_t[:, p, t * P:(t + 1) * P], chip.mats[:, MAT["o0"]], start=True,
                                            stop=True)
                last.then_inc(o_mm, 1)
                if known(c) == NCH - 1:
                    ahead.turn_step(pe, 0, 0)

            chunks_two(pe, out_body)
            ahead.logits_step(pe, 0, 0)
            ahead.rows_turn_step(pe, 0, 0)

        @block.scalar
        def _(act):
            def q_step(c):
                act.wait_ge(q_mm, c + 1)
                wait(act, scores_done, c)
                wait(act, firsts_kept, 3 * c)
                nc.scalar.activation(q_t, chip.bank[QB][:], ACT.Identity, bias=chip.cols[:, COL["bq"]]).then_inc(
                    q_kept, 1)

            def v_step(c, p):
                act.wait_ge(v_mm, c + 1)
                nc.scalar.activation(v_tok[:, p, :], chip.bank[VB][:], ACT.Copy).then_inc(v_kept, 1)

            def att_step(c):
                act.wait_ge(att_turn, c + 1)
                wait(act, local_mm, c)
                nc.scalar.activation(att_t, chip.bank[ATT][:], ACT.Copy).then_inc(att_kept, 1)

            def exp_step(c):
                act.wait_ge(soft_step, SOFT * c + SPT + 2)
                nc.scalar.activation(ex, sc, ACT.Exp, scale=SCALE).then_inc(exp_done, 1)

            def local_step(c):
                act.wait_ge(local_mm, c + 1)
                nc.scalar.activation(local[:, bass.ds(CH * c, CH)], chip.bank[LOCAL][:], ACT.Identity,
                                     bias=chip.cols[:, COL["bv"]]).then_inc(local_kept, 1)

            def body(c, p):
                q_step(c)
                if known(c) != 0:
                    att_step(c - 1)
                v_step(c, p)
                if known(c) != NCH - 1:
                    front.keep_by_scalar(act, c + 1, 1 - p)
                exp_step(c)
                if known(c) != 0:
                    local_step(c - 1)

            nc.scalar.preload_act_table(ACT.Exp)
            chunks(act, body)
            act.wait_ge(g_mm, 2)
            nc.scalar.activation(g_v, chip.bank[VB][:, 0:P], ACT.Copy).then_inc(g_v_kept, 1)
            att_step(NCH - 1)
            act.wait_ge(g_step, BATCH + 2)
            nc.scalar.activation(g_sc[:, 0:NB], g_sc[:, 0:NB], ACT.Exp, scale=SCALE).then_inc(g_exp, 1)
            local_step(NCH - 1)
            ahead.pair_step(act, 0, 0)
            ahead.rows_kept_step(act, 0, 0)

        @block.vector
        def _(dve):
            def k_step(c):
                dve.wait_ge(k_mm, c + 1)
                wait(dve, scores_done, c)
                wait(dve, firsts_kept, 3 * c)
                nc.vector.tensor_scalar(k_t, chip.bank[KB][:], chip.cols[:, COL["bk"]], None, ALU.add).then_inc(
                    k_kept, 1)

            def softmax_first(c):
                r = SOFT * c
                dve.wait_ge(scores_done, c + 1)
                wait(dve, soft_step, r)
                for g in range(SPT):
                    rows = slice(SEG * g, SEG * (g + 1))
                    nc.vector.tensor_copy(sc[rows], chip.bank[SCORES][rows, :].rearrange(tiles, t=TPC)[
                        :, :, rows]).then_inc(soft_step, 1)
                dve.wait_ge(soft_step, r + SPT)
                nc.vector.tensor_reduce(top, sc, AX.X, ALU.max).then_inc(soft_step, 1)
                dve.wait_ge(soft_step, r + SPT + 1)
                nc.vector.tensor_tensor(sc, sc, across(top.unsqueeze(2), [P, TPC, SEG]), ALU.subtract).then_inc(
                    soft_step, 1)

            def softmax_second(c):
                r = SOFT * c
                dve.wait_ge(exp_done, c + 1)
                nc.vector.tensor_reduce(total, ex, AX.X, ALU.add).then_inc(soft_step, 1)
                dve.wait_ge(soft_step, r + SPT + 3)
                nc.vector.reciprocal(inv, total).then_inc(soft_step, 1)
                dve.wait_ge(soft_step, r + SPT + 4)
                wait(dve, att_turn, c)
                for g in range(SPT):
                    rows = slice(SEG * g, SEG * (g + 1))
                    nc.vector.tensor_tensor(att[rows, :, rows], ex[rows], across(inv[rows].unsqueeze(2), [SEG, TPC, SEG]),
                                            ALU.mult).then_inc(soft_step, 1)

            def body(c, p):
                if known(c) != NCH - 1:
                    front.moments_step(dve, c + 1, 1 - p)
                if known(c) != 0:
                    softmax_second(c - 1)
                k_step(c)
                if known(c) != NCH - 1:
                    front.normed_step(dve, c + 1, 1 - p)
                softmax_first(c)

            nc.vector.memset(att, 0.0).then_inc(zeroed, 1)
            nc.vector.memset(g_att, 0.0).then_inc(zeroed, 1)
            dve.wait_ge(zeroed, 2)
            chunks(dve, body)
            softmax_second(NCH - 1)

            dve.wait_ge(g_mm, 1)
            for b in range(BATCH):
                rows = slice(NB * b, NB * (b + 1))
                nc.vector.tensor_copy(g_sc[rows, 0:NB], chip.bank[WIDE][rows, rows]).then_inc(g_step, 1)
            dve.wait_ge(g_step, BATCH)
            nc.vector.tensor_reduce(top[:, 0:1], g_sc[:, 0:NB], AX.X, ALU.max).then_inc(g_step, 1)
            dve.wait_ge(g_step, BATCH + 1)
            nc.vector.tensor_scalar(g_sc[:, 0:NB], g_sc[:, 0:NB], top[:, 0:1], None, ALU.subtract).then_inc(g_step, 1)
            dve.wait_ge(g_exp, 1)
            nc.vector.tensor_reduce(total[:, 0:1], g_sc[:, 0:NB], AX.X, ALU.add).then_inc(g_step, 1)
            dve.wait_ge(g_step, BATCH + 3)
            nc.vector.reciprocal(inv[:, 0:1], total[:, 0:1]).then_inc(g_step, 1)
            dve.wait_ge(g_step, BATCH + 4)
            for b in range(BATCH):
                rows = slice(NB * b, NB * (b + 1))
                nc.vector.tensor_scalar(g_att[rows, rows], g_sc[rows, 0:NB], inv[rows, 0:1], None, ALU.mult).then_inc(
                    g_step, 1)
            dve.wait_ge(g_mm, 3)
            nc.vector.tensor_copy(g_att_t, chip.bank[WIDE][:, 0:P]).then_inc(g_step, 1)
            dve.wait_ge(g_mm, 4)
            nc.vector.tensor_scalar(g_out, chip.bank[VB][:, 0:P], chip.cols[:, COL["bv"]], None, ALU.add).then_inc(
                g_step, 1)
            dve.wait_ge(g_step, G_ATT + 2)

            def sum_step(c, p):
                if known(c) not in (0, 1):
                    dve.wait_ge(o_mm, c - 1)
                nc.vector.tensor_tensor(o_t[:, p, :].rearrange("p (n s) -> p n s", s=SEG),
                                        local[:, bass.ds(CH * c, CH)].rearrange("p (n s) -> p n s", s=SEG),
                                        across(g_out[:, bass.ds(SPC * c, SPC)].unsqueeze(2), [P, SPC, SEG]),
                                        ALU.add).then_inc(o_ready, 1)

            def residual(c, p):
                dve.wait_ge(o_mm, c + 1)
                dve.wait_ge(bo_added, c + 1)
                tile = x[:, bass.ds(TPC * c, TPC), :]
                nc.vector.tensor_tensor(tile, chip.bank[(QB, KB)[p]][:].rearrange(tiles, t=TPC), tile,
                                        ALU.add).then_inc(x_new, 1)

            def out_body(c, p):
                sum_step(c, p)
                if known(c) != 0:
                    residual(c - 1, 1 - p)
                if known(c) == NCH - 2:
                    dve.wait_ge(x_new, 1)
                    ahead.moments_step(dve, 0, 0)
                if known(c) == NCH - 1:
                    ahead.normed_step(dve, 0, 0)

            dve.wait_ge(local_kept, NCH)
            chunks_two(dve, out_body)
            residual(NCH - 1, 1)
            ahead.keep_step(dve, 0, 0)
            ahead.split_step(dve, 0, 0)
            ahead.route_first(dve, 0, 0)
            ahead.route_second(dve, 0, 0)
            ahead.route_last(dve, 0, 0)

        @block.gpsimd
        def _(pool):
            def first_step(c, p):
                pool.wait_ge(q_kept, c + 1)
                pool.wait_ge(k_kept, c + 1)
                for dst, src in ((first_q, q_t), (first_k, k_t), (first_x, chip.xt[:, p, :])):
                    nc.gpsimd.tensor_copy(dst[:, bass.ds(SPC * c, SPC)],
                                          src.rearrange("p (n s) -> p n s", s=SEG)[:, :, 0]).then_inc(firsts_kept, 1)

            def add_bias(c):
                pool.wait_ge(front.xs_ready, TPC * c + TPC)
                tile = x[:, bass.ds(TPC * c, TPC), :]
                nc.gpsimd.tensor_tensor(tile, tile, across(chip.rows[:, ROW["bo"]].unsqueeze(1), [P, TPC, P]),
                                        ALU.add).then_inc(bo_added, 1)

            def body(c, p):
                if known(c) != NCH - 1:
                    front.power_step(pool, c + 1, 1 - p)
                first_step(c, p)
                add_bias(c)

            chunks(pool, body)
            ahead.power_step(pool, 0, 0)



def attn1_stage(chip, front, ahead):
    nc, x = chip.nc, chip.x

    def s(name):
        return chip.sem("attn1_" + name)

    QKV = ((0, 1, 2), (3, 4, 5))
    V_TURN, GRAM, MIX = (0, 1), (2, 3), 4
    q_all, k_all, v_all = (chip.room[:, k * TOKENS:(k + 1) * TOKENS] for k in range(3))
    names = ("q1", "k1", "v1")
    HALF = NCH // BATCH
    bn, agg, fix = chip.buf("bn", [P, 3, NCH, 6]), chip.buf("bn_agg", [P, 3, 2]), chip.buf("bn_fix", [P, 6, 3])
    head_mask = chip.buf("head_mask", [P, P])
    gram, mix = chip.buf("gram", [P, BATCH, P]), chip.buf("mix", [P, BATCH, P])
    v_tok = chip.buf("v_tok", [P, 2, CH])
    tiles = "p (t d) -> p t d"

    mm, kept, stat = s("mm"), s("kept"), s("stat")
    bn_step, bn_pow, masked = s("bn_step"), s("bn_pow"), s("masked")
    sig_v, sig_q, v_turn, v_kept, gram_mm = s("sig_v"), s("sig_qk"), s("v_turn"), s("v_kept"), s("gram_mm")
    gram_kept, mix_mm, mix_kept = s("gram_kept"), s("mix_mm"), s("mix_kept")
    qk_ready, out_mm, bp_added, x_new = s("qk_ready"), s("out_mm"), s("bp_added"), s("x_new")

    with nc.Block() as block:
        @block.tensor
        def _(pe):
            def body(c, p):
                front.wait_xt(pe, c)
                if known(c) not in (0, 1):
                    pe.wait_ge(kept, 3 * (c - 1))
                for k, name in enumerate(names):
                    nc.tensor.matmul(chip.bank[QKV[p][k]][:], chip.mats[:, MAT[name]], chip.xt[:, p, :], start=True,
                                     stop=True).then_inc(mm, 1)
                if known(c) != NCH - 1:
                    front.turn_step(pe, c + 1, 1 - p)

            chunks_two(pe, body)

            pe.wait_ge(kept, 3 * NCH)
            for c in range(NCH + 1):
                if c < NCH:
                    p = c % 2
                    pe.wait_ge(sig_v, c + 1)
                    wait(pe, v_kept, c - 1)
                    for t in range(TPC):
                        last = nc.tensor.transpose(chip.bank[V_TURN[p]][:, t * P:(t + 1) * P],
                                                   v_all[:, c * CH + t * P:c * CH + (t + 1) * P], chip.ident[:])
                    last.then_inc(v_turn, 1)
                if c > 0:
                    b, p = (c - 1) // HALF, (c - 1) % 2
                    pe.wait_ge(v_kept, c)
                    for t in range(TPC):
                        tile = v_tok[:, p, t * P:(t + 1) * P]
                        last = nc.tensor.matmul(chip.bank[GRAM[b]][:, 0:P], tile, tile,
                                                start=(c - 1) % HALF == 0 and t == 0,
                                                stop=(c - 1) % HALF == HALF - 1 and t == TPC - 1)
                    last.then_inc(gram_mm, 1)
            for b in range(BATCH):
                pe.wait_ge(gram_kept, b + 1)
                wait(pe, mix_kept, b)
                nc.tensor.matmul(chip.bank[MIX][:, 0:P], gram[:, b, :], chip.mats[:, MAT["p1"]], start=True,
                                 stop=True).then_inc(mix_mm, 1)
            pe.wait_ge(mix_kept, BATCH)

            for c in range(NCH):
                pe.wait_ge(qk_ready, c + 1)
                wait(pe, x_new, c - 1)
                for t in range(TPC):
                    last = nc.tensor.matmul(chip.bank[V_TURN[c % 2]][:, t * P:(t + 1) * P],
                                            q_all[:, c * CH + t * P:c * CH + (t + 1) * P], mix[:, c // HALF, :],
                                            start=True, stop=True)
                last.then_inc(out_mm, 1)
            ahead.turn_step(pe, 0, 0)
            ahead.logits_step(pe, 0, 0)
            ahead.rows_turn_step(pe, 0, 0)

        @block.scalar
        def _(act):
            def body(c, p):
                for k, dst in enumerate((q_all, k_all, v_all)):
                    act.wait_ge(mm, 3 * c + k + 1)
                    nc.scalar.activation(dst[:, bass.ds(CH * c, CH)], chip.bank[QKV[p][k]][:], ACT.Copy).then_inc(
                        kept, 1)
                if known(c) != NCH - 1:
                    front.keep_by_scalar(act, c + 1, 1 - p)

            nc.scalar.preload_act_table(ACT.Sigmoid)
            chunks_two(act, body)
            act.wait_ge(bn_step, 3 + 6)
            act.wait_ge(kept, 3 * NCH)
            def sigmoid(c, k, dst, done):
                chunk = dst[:, bass.ds(CH * c, CH)]
                nc.scalar.activation(chunk, chunk, ACT.Sigmoid, bias=fix[:, 5, k:k + 1],
                                     scale=fix[:, 3, k:k + 1]).then_inc(done, 1)

            with act.Fori(0, NCH) as c:
                sigmoid(c, 2, v_all, sig_v)
            with act.Fori(0, NCH) as c:
                sigmoid(c, 0, q_all, sig_q)
                sigmoid(c, 1, k_all, sig_q)
            ahead.rows_kept_step(act, 0, 0)

        @block.vector
        def _(dve):
            def batch_stats(c):
                for k, src in enumerate((q_all, k_all, v_all)):
                    dve.wait_ge(kept, 3 * c + k + 1)
                    nc.vector.bn_stats(bn[:, k, bass.ds(c, 1), :], src[:, bass.ds(CH * c, CH)]).then_inc(stat, 1)

            def body(c, p):
                if known(c) != NCH - 1:
                    front.moments_step(dve, c + 1, 1 - p)
                if known(c) != 0:
                    batch_stats(c - 1)
                if known(c) != NCH - 1:
                    front.normed_step(dve, c + 1, 1 - p)

            chunks_two(dve, body)
            batch_stats(NCH - 1)
            dve.wait_ge(stat, 3 * NCH)
            for k in range(3):
                nc.vector.bn_aggr(agg[:, k, :], bn[:, k, :, :].rearrange("p c s -> p (c s)")).then_inc(bn_step, 1)
            dve.wait_ge(bn_step, 3)
            nc.vector.tensor_scalar(fix[:, 0, :], agg[:, :, 1], EPS, None, ALU.add).then_inc(bn_step, 1)
            dve.wait_ge(bn_pow, 1)
            gammas = chip.cols[:, COL["gq"].start:COL["gv"].stop]
            betas = chip.cols[:, COL["tq"].start:COL["tv"].stop]
            nc.vector.tensor_tensor(fix[:, 2, :], fix[:, 1, :], gammas, ALU.mult).then_inc(bn_step, 1)
            dve.wait_ge(bn_step, 5)
            nc.vector.tensor_scalar(fix[:, 3, :], fix[:, 2, :], 4.0, None, ALU.mult).then_inc(bn_step, 1)
            nc.vector.tensor_tensor(fix[:, 4, :], agg[:, :, 0], fix[:, 2, :], ALU.mult).then_inc(bn_step, 1)
            dve.wait_ge(bn_step, 7)
            nc.vector.tensor_tensor(fix[:, 4, :], betas, fix[:, 4, :], ALU.subtract).then_inc(bn_step, 1)
            dve.wait_ge(bn_step, 8)
            nc.vector.tensor_scalar(fix[:, 5, :], fix[:, 4, :], 4.0, -4.0, ALU.mult, ALU.add).then_inc(bn_step, 1)
            for c in range(NCH):
                p = c % 2
                dve.wait_ge(v_turn, c + 1)
                wait(dve, gram_mm, c - 1)
                nc.vector.tensor_copy(v_tok[:, p, :], chip.bank[V_TURN[p]][:]).then_inc(v_kept, 1)
            dve.wait_ge(masked, 3)
            for b in range(BATCH):
                dve.wait_ge(gram_mm, HALF * (b + 1))
                nc.vector.tensor_tensor(gram[:, b, :], chip.bank[GRAM[b]][:, 0:P], head_mask[:], ALU.mult).then_inc(
                    gram_kept, 1)
            for b in range(BATCH):
                dve.wait_ge(mix_mm, b + 1)
                nc.vector.tensor_scalar(mix[:, b, :], chip.bank[MIX][:, 0:P], SCALE, None, ALU.mult).then_inc(
                    mix_kept, 1)

            def residual(c, p):
                dve.wait_ge(out_mm, c + 1)
                dve.wait_ge(bp_added, c + 1)
                tile = x[:, bass.ds(TPC * c, TPC), :]
                nc.vector.tensor_tensor(tile, chip.bank[V_TURN[p]][:].rearrange(tiles, t=TPC), tile,
                                        ALU.add).then_inc(x_new, 1)
                if known(c) == NCH - 2:
                    dve.wait_ge(x_new, 1)
                    ahead.moments_step(dve, 0, 0)

            chunks_two(dve, residual)
            ahead.normed_step(dve, 0, 0)
            ahead.keep_step(dve, 0, 0)
            ahead.split_step(dve, 0, 0)
            ahead.route_first(dve, 0, 0)
            ahead.route_second(dve, 0, 0)
            ahead.route_last(dve, 0, 0)

        @block.gpsimd
        def _(pool):
            nc.gpsimd.memset(head_mask[:], 1.0).then_inc(masked, 1)
            m = head_mask[:].rearrange("p (h d) -> p h d", d=HEAD)
            for n, (sign, start) in enumerate(((1, 0), (-1, HEAD - 1))):
                pool.wait_ge(masked, n + 1)
                nc.gpsimd.affine_select(out=m, in_=m, compare_op=ALU.is_ge, fill=0.0, base=start,
                                        pattern=[[-sign * HEAD, P // HEAD], [0, HEAD]],
                                        channel_multiplier=sign).then_inc(masked, 1)

            def body(c, p):
                if known(c) != NCH - 1:
                    front.power_step(pool, c + 1, 1 - p)
                pool.wait_ge(front.xs_ready, TPC * c + TPC)
                tile = x[:, bass.ds(TPC * c, TPC), :]
                nc.gpsimd.tensor_tensor(tile, tile, across(chip.rows[:, ROW["bp"]].unsqueeze(1), [P, TPC, P]),
                                        ALU.add).then_inc(bp_added, 1)

            chunks_two(pool, body)
            pool.wait_ge(bn_step, 4)
            nc.gpsimd.tensor_tensor(fix[:, 1, :], fix[:, 0, :], chip.neg_half[:, 0:3], ALU.pow).then_inc(bn_pow, 1)
            for c in range(NCH):
                pool.wait_ge(sig_q, 2 * c + 2)
                chunk = slice(c * CH, (c + 1) * CH)
                nc.gpsimd.tensor_tensor(q_all[:, chunk], q_all[:, chunk], k_all[:, chunk], ALU.mult).then_inc(
                    qk_ready, 1)
            ahead.power_step(pool, 0, 0)



_LAID = ("x", "cols", "rows", "mats", "gens", "gens_t", "ew1", "ew2", "w1", "w2", "b2", "b1_row")


def macaron(nc, args, out):
    with ExitStack() as ctx:
        chip = Chip(nc, ctx)
        fronts, front = [], None
        for k, name in enumerate(STAGES):
            call = STAGES[:k].count(name)
            if name == "ffn0":
                front = Front0(chip, call, front)
            elif name == "ffn1":
                front = Front1(chip, call, front)
            else:
                front = Front(chip, name, 0, front, twice=False, affine=False, split=False)
            fronts.append(front)
        setup(chip, args, fronts[0])
        for name, front, ahead in zip(STAGES, fronts, fronts[1:] + [None]):
            if name == "ffn0":
                ffn0_stage(chip, front, ahead)
            elif name == "attn0":
                attn0_stage(chip, front, ahead)
            elif name == "ffn1":
                ffn1_stage(chip, front, ahead, out)
            elif name == "attn1":
                attn1_stage(chip, front, ahead)


def lay_out(a):
    import numpy as np

    g = {k: np.asarray(v) for k, v in a.items()}
    col = lambda v: v.reshape(P, 1)
    row = lambda v: np.broadcast_to(v.reshape(1, -1), (P, v.size))
    cols = [col(g["L0_ffn_ln_gamma"]), col(g["L0_ffn_ln_beta"]), g["L0_ffn_eb1"].reshape(U0, P).T, g["L0_ffn_eb2"].T,
            col(g["L0_attn_bq"]), col(g["L0_attn_bk"]), col(g["L0_attn_bv"]),
            col(g["L1_attn_gq"]), col(g["L1_attn_gk"]), col(g["L1_attn_gv"]),
            col(g["L1_attn_bq"]), col(g["L1_attn_bk"]), col(g["L1_attn_bv"])]
    rows = [row(g["L0_ffn_moe_gate_b"]), row(g["L0_ffn_abel_b"]), row(g["L0_ffn_gc_w"][:P, 0]),
            row(g["L0_ffn_gc_w"][P:, 0]), row(g["L0_ffn_gc_b"]), row(g["L0_attn_bo"]), row(g["L1_attn_bp"]),
            row(g["L1_ffn_router_b"])]
    mats = [g["L0_ffn_abel_w"], g["L0_ffn_moe_gate_w"], g["L0_attn_Wq"].T, g["L0_attn_Wk"].T, g["L0_attn_Wv"].T,
            g["L0_attn_Wo"].T, g["L1_attn_Wq"].T, g["L1_attn_Wk"].T, g["L1_attn_Wv"].T, g["L1_attn_Wp"].T,
            g["L1_ffn_router_w"].T]
    laid = {
        "x": g["L0_attn_x"].reshape(TOKENS, P),
        "cols": np.concatenate(cols, 1), "rows": np.concatenate(rows, 1), "mats": np.concatenate(mats, 1),
        "gens": g["L0_ffn_gens"].transpose(1, 0, 2), "gens_t": g["L0_ffn_gens"].transpose(2, 0, 1),
        "ew1": g["L0_ffn_ew1"].transpose(1, 0, 2).reshape(P, U0, P),
        "ew2": g["L0_ffn_ew2"].reshape(U0, P, P).transpose(1, 0, 2),
        "w1": g["L1_ffn_weights1"].transpose(1, 0, 2).reshape(P, U1, P),
        "w2": g["L1_ffn_weights2"].reshape(U1, P, P).transpose(1, 0, 2),
        "b2": g["L1_ffn_bias2"],
        "b1_row": g["L1_ffn_bias1"].reshape(1, U1, P),
    }
    return {k: np.ascontiguousarray(v) for k, v in laid.items()}


def kernel(**inputs):
    import concourse.bacc as bacc
    from concourse.bass_utils import run_bass_kernel_spmd

    nc = bacc.Bacc("TRN2", target_bir_lowering=False, num_devices=1)
    laid = lay_out(inputs)
    args = {k: nc.dram_tensor(f"in_{k}", laid[k].shape, F32, kind="ExternalInput").ap() for k in _LAID}
    out = nc.dram_tensor("out", (TOKENS, P), F32, kind="ExternalOutput").ap()
    macaron(nc, args, out)
    run = run_bass_kernel_spmd(nc, [{f"in_{k}": laid[k] for k in _LAID}], core_ids=[0])
    return run.results[0]["out"].reshape(BATCH, LENGTH, P)
```

```python
from contextlib import ExitStack

import concourse.bass as bass
from concourse import mybir

F32 = mybir.dt.float32
F32R = mybir.dt.float32r
U32 = mybir.dt.uint32
ALU = mybir.AluOpType
ACT = mybir.ActivationFunctionType
AX = mybir.AxisListType
RMAX = bass.bass_isa.ReduceOp.max

P = 128
BATCH, LENGTH = 2, 2048
TOKENS = BATCH * LENGTH
TILES = TOKENS // P
TPC = 4
CH = TPC * P
NCH = TOKENS // CH
EPS = 1e-5

E0, HC = 8, 2
U0 = E0 * HC
E1, H1 = 32, 32
EPU = P // H1
U1 = E1 // EPU
SEG = 32
SPT = P // SEG
SPC = CH // SEG
HEAD = 8
SCALE = HEAD ** -0.5
BLOCKED = 2.0 ** 100
NROT = 3
DEGREE = 11
SQUARINGS = 18

STAGES = ("ffn0", "attn0", "ffn0", "ffn1", "attn1", "ffn1")

TURN = 6

LAG0 = 2
AT0 = dict(
    rot=7, abel_mm=14, turn=6, logits=10, w_turn=14,
    abel=15, gate=10, pair=12, w_kept=15,
    abel_bias=13, dots_abel=2, dots_moe=7, difference=7, mix=9, keep_input=15, moments=1, normed=3, keep=4, split=6,
    route_pair=9, route_weights=12,
    power=0)
LAG1 = 2
AT1 = dict(
    back=5, turn=6, logits=9, one_turn=12,
    y=0, one_kept=5,
    add=5, moments=0, normed=1, keep=2, split=2, route=4, block=5)


def layout(*fields):
    at, out = 0, {}
    for name, width in fields:
        out[name] = slice(at, at + width)
        at += width
    return out, at


COL, NCOL = layout(("gamma", 1), ("beta", 1), ("eb1", U0), ("eb2", E0), ("bq", 1), ("bk", 1), ("bv", 1),
                   ("gq", 1), ("gk", 1), ("gv", 1), ("tq", 1), ("tk", 1), ("tv", 1))
ROW, NROW = layout(("gate_b", E0), ("abel_b", P), ("gate_abel", P), ("gate_moe", P), ("gc_b", 1), ("bo", P),
                   ("bp", P), ("router_b", E1))
MAT, NMAT = layout(("abel", P), ("gate", E0), ("q0", P), ("k0", P), ("v0", P), ("o0", P), ("q1", P), ("k1", P),
                   ("v1", P), ("p1", P), ("router", E1))


class Chip:

    def __init__(self, nc, ctx):
        self.nc, self.ctx, self.sems = nc, ctx, {}
        sb = self.sb
        self.bank = [ctx.enter_context(nc.psum_tensor(f"bank{i}", [P, CH], F32)) for i in range(8)]
        self.x = sb("x", [P, TILES, P])
        self.cols, self.rows, self.mats = sb("cols", [P, NCOL]), sb("rows", [P, NROW]), sb("mats", [P, NMAT])
        self.ew1_hi, self.ew1_lo = (sb(f"ew1_{k}", [P, U0, P], F32R) for k in ("hi", "lo"))
        self.ew2_hi, self.ew2_lo = (sb(f"ew2_{k}", [P, U0, P], F32R) for k in ("hi", "lo"))
        self.w1_hi, self.w1_lo = (sb(f"w1_{k}", [P, U1, P], F32R) for k in ("hi", "lo"))
        self.w2_hi, self.w2_lo = (sb(f"w2_{k}", [P, U1, P], F32R) for k in ("hi", "lo"))
        self.b2_split = sb("b2_split", [2 * E1, P], F32R)
        self.rotation = sb("rotation", [P, P])
        self.ident = sb("ident", [P, P])
        self.iota_row = sb("iota_row", [P, 2 * E1])
        self.neg_half = sb("neg_half", [P, 2 * TPC])
        self.half_gc_b = sb("half_gc_b", [P, 1])
        self.block_expert = sb("block_expert", [E1 + 2, U1, P], F32R)
        self.stats = sb("stats", [P, TPC, 6])
        self.moments = sb("moments", [P, 2, TPC, 2])
        self.powed = sb("powed", [P, 2, TPC])
        self.r_std = sb("r_std", [P, 2, 2, TPC])
        self.mean_r = sb("mean_r", [P, TPC])
        self.keep_scale, self.keep_shift = sb("keep_scale", [P, 2, TPC]), sb("keep_shift", [P, 2, TPC])
        self.xs = sb("xs", [P, TPC, P])
        self.xt = sb("xt", [P, 2, CH])
        self.xt_hi, self.xt_lo = sb("xt_hi", [P, 2, CH], F32R), sb("xt_lo", [P, 2, CH], F32R)
        self.hid_hi, self.hid_lo = sb("hid_hi", [P, 8, CH], F32R), sb("hid_lo", [P, 8, CH], F32R)
        self.logits0, self.logits1 = sb("logits0", [P, TPC, E0]), sb("logits1", [P, TPC, E1])
        self.best, self.best_at = sb("best", [P, TPC, 8]), sb("best_at", [P, TPC, 8], U32)
        self.one_a, self.one_b = sb("one_a", [P, TPC, E0]), sb("one_b", [P, TPC, E0])
        self.chosen = sb("chosen", [P, TPC, 2 * E1])
        self.pair, self.pair_w = sb("pair", [P, 2, TPC]), sb("pair_w", [P, 2, TPC])
        self.w_rows = sb("w_rows", [E0, CH])
        self.w_rows_dram = nc.dram_tensor("w_rows_dram", (E0, CH), F32, kind="Internal").ap()
        self.chosen_t, self.blocked_t = sb("chosen_t", [2 * E1, 2, CH], F32R), sb("blocked_t", [E1 + 2, 2, CH], F32R)
        self.gate = sb("gate", [P, 5, TPC])
        self.room = sb("room", [P, 3 * TOKENS])

    def sb(self, name, shape, dt=F32):
        return self.ctx.enter_context(self.nc.sbuf_tensor(name, shape, dt))

    def sem(self, name):
        if name not in self.sems:
            self.sems[name] = self.ctx.enter_context(self.nc.semaphore(name))
        return self.sems[name]

    def buf(self, name, shape, dt=F32):
        return self.sb(name, shape, dt)

    def rooms(self, *fields):
        at, out = 0, []
        for shape in fields:
            n = 1
            for k in shape:
                n *= k
            view = self.room[:, at:at + n]
            if len(shape) == 2:
                view = view.rearrange("p (a b) -> p a b", a=shape[0])
            if len(shape) == 3:
                view = view.rearrange("p (a b c) -> p a b c", a=shape[0], b=shape[1])
            out.append(view)
            at += n
        assert at <= 3 * TOKENS
        return out


def wait(eng, sem, value):
    if not (isinstance(value, int) and value <= 0):
        eng.wait_ge(sem, value)


def wait_alone(eng, sem, value, passed):
    if not (isinstance(value, int) and value <= 0):
        eng.wait_ge(sem, value)
        if not isinstance(value, int):
            eng.sem_inc(passed, 1)


def chunks(eng, body):
    body(0, 0)
    with eng.Fori(0, (NCH - 2) // 2) as i:
        body(2 * i + 1, 1)
        body(2 * i + 2, 0)
    body(NCH - 1, 1)


def chunks_two(eng, body):
    body(0, 0)
    body(1, 1)
    with eng.Fori(1, (NCH - 2) // 2) as i:
        body(2 * i, 0)
        body(2 * i + 1, 1)
    body(NCH - 2, 0)
    body(NCH - 1, 1)


def chunks_three(eng, body):
    body(0, 0)
    body(1, 1)
    body(2, 0)
    with eng.Fori(1, (NCH - 2) // 2) as i:
        body(2 * i + 1, 1)
        body(2 * i + 2, 0)
    body(NCH - 1, 1)


def known(c):
    return c if isinstance(c, int) else None


def across(ap, shape):
    return ap.to_broadcast(shape)



def setup(chip, args, front):
    nc, x = chip.nc, chip.x
    loaded_x, loaded_small, loaded_gens = chip.sem("loaded_x"), chip.sem("loaded_small"), chip.sem("loaded_gens")
    loaded_w, const_made = chip.sem("loaded_w"), chip.sem("const_made")
    hi_made, lo_made = chip.sem("hi_made"), chip.sem("lo_made")
    raw_ew1, raw_ew2, raw_w1, raw_w2, raw_b2, gens, gens_t, power, sums, rot12_t, block_rows, raw_b1, ones = chip.rooms(
        (U0, P), (U0, P), (U1, P), (U1, P), (1, P), (NROT, P), (NROT, P), (NROT, 2, P), (4, SQUARINGS), (1, P),
        (U1, P), (U1, P), (CH,))
    b2_again, b1_low = chip.hid_hi[:, 0, 0:P], chip.hid_hi[:, 1:3, :].rearrange("p a (u h) -> p (a u) h", h=P)
    threshold, over, factor = sums[:, 0, :], sums[:, 1, :], sums[:, 2, :]
    col_norm, norm, shrink = sums[:, 3, 0:NROT], sums[:, 3, 4:5], sums[:, 3, 5:6]
    over_bits = chip.sb("over_bits", [P, SQUARINGS], U32)
    col_max = sums[:, 3, 6:7]
    b1_row = slice(E1, E1 + 1)
    splits = [(raw_ew1, chip.ew1_hi[:], chip.ew1_lo[:]), (raw_ew2, chip.ew2_hi[:], chip.ew2_lo[:]),
              (raw_w1, chip.w1_hi[:], chip.w1_lo[:]), (raw_w2, chip.w2_hi[:], chip.w2_lo[:]),
              (raw_b2[0:E1, 0, :], chip.b2_split[0:E1], None),
              (raw_b2[E1:2 * E1, 0, :], b2_again[E1:2 * E1], chip.b2_split[E1:2 * E1]),
              (raw_b1[b1_row], chip.block_expert[b1_row], b1_low[b1_row])]
    norm_step, all_norm, taylor_mm, taylor_done = (
        chip.sem(n) for n in ("norm_step", "all_norm", "taylor_mm", "taylor_done"))
    turned, turned_kept, squared, square_kept = (
        chip.sem(n) for n in ("turned", "turned_kept", "squared", "square_kept"))
    rot_mm, rot_kept = chip.sem("rot_mm"), chip.sem("rot_kept")
    sel_step, sel_made = chip.sem("sel_step"), chip.sem("sel_made")
    lows = sum(lo is not None for _, _, lo in splits)
    pair = "p s d -> p (s d)"
    exp_bank = [b[:, 0:2 * P] for b in chip.bank[0:NROT]]

    consts = 3 + SQUARINGS + 1

    with nc.Block() as block:
        @block.sync
        def _(sp):
            sp.dma_start(gens, args["gens"]).then_inc(loaded_gens, 16)
            sp.dma_start(gens_t, args["gens_t"]).then_inc(loaded_gens, 16)
            sp.dma_start(chip.cols[:], args["cols"]).then_inc(loaded_small, 16)
            sp.dma_start(chip.rows[:], args["rows"]).then_inc(loaded_small, 16)
            sp.dma_start(chip.mats[:], args["mats"]).then_inc(loaded_small, 16)
            sp.dma_start(x[:], args["x"].rearrange("(t p) d -> p t d", p=P)).then_inc(loaded_x, 16)
            for k, (dst, name) in enumerate(((raw_ew1, "ew1"), (raw_ew2, "ew2"), (raw_w1, "w1"), (raw_w2, "w2"))):
                sp.dma_start(dst, args[name]).then_inc(loaded_w, 16)
                sp.wait_ge(loaded_w, 16 * (k + 1))
            for k, (dst, name) in enumerate(((raw_b2[0:E1, 0, :], "b2"), (raw_b2[E1:2 * E1, 0, :], "b2"),
                                             (raw_b1[b1_row], "b1_row"))):
                sp.dma_start(dst, args[name]).then_inc(loaded_w, 16)
                sp.wait_ge(loaded_w, 16 * (k + 5))
            sp.wait_ge(lo_made, lows)
            sp.dma_start(chip.block_expert[E1 + 1:E1 + 2].bitcast(F32), b1_low[b1_row].bitcast(F32)).then_inc(loaded_w, 16)
            sp.wait_ge(loaded_x, 16)
            sp.wait_ge(loaded_small, 48)
            sp.wait_ge(loaded_w, 16 * (len(splits) + 1))

        @block.gpsimd
        def _(pool):
            nc.gpsimd.memset(chip.ident[:], 0.0).then_inc(const_made, 1)
            nc.gpsimd.memset(chip.neg_half[:], -0.5).then_inc(const_made, 1)
            nc.gpsimd.iota(chip.iota_row[:], [[0, 2], [1, E1]], base=0, channel_multiplier=0,
                           allow_small_or_imprecise_dtypes=True).then_inc(const_made, 1)
            for j in range(SQUARINGS):
                nc.gpsimd.memset(threshold[:, j:j + 1], 2.0 ** j).then_inc(const_made, 1)
            pool.wait_ge(const_made, 1)
            nc.gpsimd.affine_select(out=chip.ident[:], in_=chip.ident[:], compare_op=ALU.not_equal, fill=1.0, base=0,
                                    pattern=[[-1, P]], channel_multiplier=1).then_inc(const_made, 1)
            pool.wait_ge(norm_step, 2)
            nc.gpsimd.partition_all_reduce(norm, col_max, P, RMAX).then_inc(all_norm, 1)
            nc.gpsimd.memset(block_rows[0:E1], 0.0).then_inc(sel_step, 1)
            nc.gpsimd.memset(ones[0:E1 + 2], 1.0).then_inc(sel_step, 1)
            pool.wait_ge(sel_step, 2)
            nc.gpsimd.affine_select(out=block_rows[0:E1].rearrange("k u (q h) -> k u q h", q=EPU),
                                    in_=block_rows[0:E1].rearrange("k u (q h) -> k u q h", q=EPU),
                                    compare_op=ALU.not_equal, fill=BLOCKED, base=0,
                                    pattern=[[-EPU, U1], [-1, EPU], [0, H1]], channel_multiplier=1).then_inc(sel_step, 1)
            for n, (raw, hi, lo) in enumerate(splits):
                if lo is not None:
                    pool.wait_ge(hi_made, n + 1)
                    if n >= 4:
                        pool.wait_ge(lo_made, lows - (len(splits) - n))
                    nc.gpsimd.tensor_tensor(lo, raw, hi.bitcast(F32), ALU.subtract).then_inc(lo_made, 1)
                if n == 0:
                    pool.wait_ge(const_made, consts)
                    front.power_step(pool, 0, 0)
        @block.scalar
        def _(act):
            nc.scalar.preload_act_table(ACT.Gelu)
            for k, (raw, hi, _) in enumerate(splits):
                act.wait_ge(loaded_w, 16 * (k + 1))
                nc.scalar.activation(hi, raw, ACT.Copy).then_inc(hi_made, 1)
            act.wait_ge(loaded_small, 48)
            nc.scalar.activation(chip.half_gc_b[:], chip.rows[:, ROW["gc_b"]], ACT.Copy, scale=0.5).then_inc(hi_made, 1)
            act.wait_ge(sel_step, 3)
            nc.scalar.activation(chip.block_expert[0:E1], block_rows[0:E1], ACT.Copy).then_inc(sel_made, 1)
            for p in range(2):
                nc.scalar.activation(chip.blocked_t[E1:E1 + 2, p, :], ones[E1:E1 + 2], ACT.Copy).then_inc(sel_made, 1)
            front.pair_step(act, 0, 0)
            front.rows_kept_step(act, 0, 0)

        @block.vector
        def _(dve):
            dve.wait_ge(loaded_gens, 32)
            nc.vector.tensor_reduce(col_norm, gens_t, AX.X, ALU.add, apply_absolute_value=True).then_inc(norm_step, 1)
            dve.wait_ge(norm_step, 1)
            nc.vector.tensor_reduce(col_max, col_norm, AX.X, ALU.max).then_inc(norm_step, 1)
            dve.wait_ge(all_norm, 1)
            dve.wait_ge(const_made, consts)
            nc.vector.tensor_scalar(over, threshold, norm, None, ALU.is_lt).then_inc(norm_step, 1)
            dve.wait_ge(norm_step, 3)
            nc.vector.tensor_copy(over_bits[:], over).then_inc(norm_step, 1)
            nc.vector.tensor_scalar(factor, over, -0.5, 1.0, ALU.mult, ALU.add).then_inc(norm_step, 1)
            dve.wait_ge(norm_step, 5)
            nc.vector.tensor_reduce(shrink, factor, AX.X, ALU.mult).then_inc(norm_step, 1)
            dve.wait_ge(norm_step, 6)
            nc.vector.tensor_scalar(gens, gens, shrink, None, ALU.mult).then_inc(norm_step, 1)
            nc.vector.tensor_scalar(gens_t, gens_t, shrink, None, ALU.mult).then_inc(norm_step, 1)
            dve.wait_ge(norm_step, 8)
            for i in range(NROT):
                nc.vector.scalar_tensor_tensor(out=power[:, i, 0, :], in0=gens[:, i, :], scalar=1.0 / DEGREE,
                                               in1=chip.ident[:], op0=ALU.mult, op1=ALU.add).then_inc(taylor_done, 1)
            for k in range(DEGREE - 1, 0, -1):
                for i in range(NROT):
                    dve.wait_ge(taylor_mm, NROT * (DEGREE - 1 - k) + i + 1)
                    nc.vector.scalar_tensor_tensor(out=power[:, i, 0, :], in0=exp_bank[i][:, 0:P], scalar=1.0 / k,
                                                   in1=chip.ident[:], op0=ALU.mult, op1=ALU.add).then_inc(
                                                       taylor_done, 1)
            for i in range(NROT):
                dve.wait_ge(turned, i + 1)
                nc.vector.tensor_copy(power[:, i, 1, :], exp_bank[i][:, 0:P]).then_inc(turned_kept, 1)
            for j in range(SQUARINGS):
                for i in range(NROT):
                    dve.wait_ge(squared, NROT * j + i + 1)
                    n = 2 * P
                    nc.vector.copy_predicated(power[:, i].rearrange(pair)[:, 0:n], across(over_bits[:, j:j + 1], [P, n]),
                                              exp_bank[i][:, 0:n]).then_inc(square_kept, 1)
                if j == 2:
                    dve.wait_ge(loaded_x, 16)
                    front.moments_step(dve, 0, 0)
                if j == 6:
                    front.normed_step(dve, 0, 0)
                if j == 8:
                    dve.wait_ge(loaded_small, 48)
                    front.keep_step(dve, 0, 0)
                    front.split_step(dve, 0, 0)
                if j == 12:
                    front.route_first(dve, 0, 0)
                if j == 15:
                    front.route_second(dve, 0, 0)
                if j == SQUARINGS - 1:
                    front.route_last(dve, 0, 0)
            dve.wait_ge(rot_mm, 1)
            nc.vector.tensor_copy(rot12_t[:, 0, :], exp_bank[0][:, 0:P]).then_inc(rot_kept, 1)
            dve.wait_ge(rot_mm, 2)
            nc.vector.tensor_copy(chip.rotation[:], exp_bank[0][:, 0:P]).then_inc(rot_kept, 1)
        @block.tensor
        def _(pe):
            for k in range(DEGREE - 1):
                for i in range(NROT):
                    pe.wait_ge(taylor_done, NROT * k + i + 1)
                    nc.tensor.matmul(exp_bank[i][:, 0:P], gens_t[:, i, :], power[:, i, 0, :], start=True,
                                     stop=True).then_inc(taylor_mm, 1)
            for i in range(NROT):
                pe.wait_ge(taylor_done, NROT * (DEGREE - 1) + i + 1)
                nc.tensor.transpose(exp_bank[i][:, 0:P], power[:, i, 0, :], chip.ident[:]).then_inc(turned, 1)
            for j in range(SQUARINGS):
                for i in range(NROT):
                    if j:
                        pe.wait_ge(square_kept, NROT * (j - 1) + i + 1)
                    else:
                        pe.wait_ge(turned_kept, i + 1)
                    for t in (0, 1):
                        last = nc.tensor.matmul(exp_bank[i][:, t * P:(t + 1) * P], power[:, i, 1 - t, :],
                                                power[:, i, t, :], start=True, stop=True)
                    last.then_inc(squared, 1)
                if j == 8:
                    front.turn_step(pe, 0, 0)
                if j == 10:
                    pe.wait_ge(loaded_small, 48)
                    front.logits_step(pe, 0, 0)
                if j == SQUARINGS - 1:
                    front.rows_turn_step(pe, 0, 0)
            pe.wait_ge(square_kept, NROT * SQUARINGS)
            nc.tensor.matmul(exp_bank[0][:, 0:P], power[:, 1, 0, :], power[:, 0, 1, :], start=True, stop=True).then_inc(
                rot_mm, 1)
            pe.wait_ge(rot_kept, 1)
            nc.tensor.matmul(exp_bank[0][:, 0:P], rot12_t[:, 0, :], power[:, 2, 0, :], start=True, stop=True).then_inc(
                rot_mm, 1)



class Front:

    def __init__(self, chip, name, base, behind, twice, affine, split):
        self.chip, self.base, self.behind, self.turn_bank = chip, base, behind, chip.bank[TURN]
        self.twice, self.affine, self.split = twice, affine, split
        s = chip.sem
        self.stats_done, self.moments_done = s(name + "_stats_done"), s(name + "_moments_done")
        self.r_step, self.xs_ready = s(name + "_r_step"), s(name + "_xs_ready")
        self.turned, self.xt_ready = s(name + "_turned"), s(name + "_xt_ready")
        self.r_steps = 6 if twice else 2
        self.xt_steps = 3 if split else 1

    def moments_step(self, dve, c, p):
        nc, chip, n = self.chip.nc, self.chip, self.base + c
        for t in range(TPC):
            nc.vector.bn_stats(chip.stats[:, t, :], chip.x[:, bass.ds(TPC * c + t, 1), :]).then_inc(self.stats_done, 1)
        wait_alone(dve, self.stats_done, TPC * n + TPC, chip.sem("dve_passed"))
        for t in range(TPC):
            nc.vector.bn_aggr(chip.moments[:, p, t, :], chip.stats[:, t, :]).then_inc(self.moments_done, 1)

    def power_step(self, pool, c, p):
        nc, chip, n = self.chip.nc, self.chip, self.base + c
        var = chip.moments[:, p, :, 1]
        pool.wait_ge(self.moments_done, TPC * n + TPC)
        if known(c) != 0:
            wait_alone(pool, self.r_step, self.r_steps * n, chip.sem("pool_passed"))
        elif self.behind:
            pool.wait_ge(self.behind.r_step, self.behind.r_steps * (self.behind.base + NCH))
        nc.gpsimd.tensor_scalar(chip.powed[:, 0, :], var, 1.0, EPS, ALU.mult, ALU.add).then_inc(self.r_step, 1)
        k = 1
        if self.twice:
            nc.gpsimd.tensor_scalar(chip.powed[:, 1, :], var, 1.0 + EPS, EPS * EPS, ALU.mult, ALU.add).then_inc(
                self.r_step, 1)
            k = 2
        pool.wait_ge(self.r_step, self.r_steps * n + k)
        nc.gpsimd.tensor_tensor(chip.r_std[:, p, 0:k, :], chip.powed[:, 0:k, :],
                                chip.neg_half[:, 0:k * TPC].rearrange("p (a t) -> p a t", a=k), ALU.pow).then_inc(
                                    self.r_step, 1)
        if self.twice:
            pool.wait_ge(self.r_step, self.r_steps * n + 3)
            nc.gpsimd.tensor_tensor(chip.mean_r[:], chip.moments[:, p, :, 0], chip.r_std[:, p, 0, :],
                                    ALU.mult).then_inc(self.r_step, 1)
            nc.gpsimd.tensor_scalar(chip.keep_scale[:, p, :], chip.r_std[:, p, 0, :], 0.5, 1.0, ALU.mult,
                                    ALU.add).then_inc(self.r_step, 1)
            wait_alone(pool, self.r_step, self.r_steps * n + 4, chip.sem("pool_passed"))
            nc.gpsimd.tensor_scalar(chip.keep_shift[:, p, :], chip.mean_r[:], -0.5, 0.0, ALU.mult,
                                    ALU.add).then_inc(self.r_step, 1)

    def normed_step(self, dve, c, p):
        nc, chip, n = self.chip.nc, self.chip, self.base + c
        if known(c) != 0:
            dve.wait_ge(self.turned, n)
        dve.wait_ge(self.r_step, self.r_steps * n + self.r_steps)
        for t in range(TPC):
            nc.vector.tensor_scalar(chip.xs[:, t, :].unsqueeze(1), chip.x[:, bass.ds(TPC * c + t, 1), :],
                                    chip.moments[:, p, t, 0:1], chip.r_std[:, p, int(self.twice), t:t + 1],
                                    ALU.subtract, ALU.mult).then_inc(self.xs_ready, 1)

    def turn_step(self, pe, c, p):
        nc, chip, n = self.chip.nc, self.chip, self.base + c
        if known(c) != 0:
            self.wait_bank(pe, c)
        elif self.behind:
            self.behind.wait_bank(pe, NCH)
        pe.wait_ge(self.xs_ready, TPC * n + TPC)
        for t in range(TPC):
            last = nc.tensor.transpose(self.turn_bank[:, t * P:(t + 1) * P], chip.xs[:, t, :], chip.ident[:])
        last.then_inc(self.turned, 1)

    def keep_step(self, dve, c, p):
        nc, chip, n = self.chip.nc, self.chip, self.base + c
        dve.wait_ge(self.turned, n + 1)
        if self.affine:
            nc.vector.tensor_scalar(chip.xt[:, p, :], self.turn_bank[:], chip.cols[:, COL["gamma"]],
                                    chip.cols[:, COL["beta"]], ALU.mult, ALU.add).then_inc(self.xt_ready, 1)
        else:
            nc.vector.tensor_copy(chip.xt[:, p, :], self.turn_bank[:]).then_inc(self.xt_ready, 1)

    def keep_by_scalar(self, act, c, p):
        nc, chip, n = self.chip.nc, self.chip, self.base + c
        act.wait_ge(self.turned, n + 1)
        nc.scalar.activation(chip.xt[:, p, :], self.turn_bank[:], ACT.Copy).then_inc(self.xt_ready, 1)

    def split_step(self, dve, c, p):
        nc, chip, n = self.chip.nc, self.chip, self.base + c
        if self.split:
            dve.wait_ge(self.xt_ready, self.xt_steps * n + 1)
            nc.vector.tensor_copy(chip.xt_hi[:, p, :], chip.xt[:, p, :]).then_inc(self.xt_ready, 1)
            dve.wait_ge(self.xt_ready, self.xt_steps * n + 2)
            nc.vector.tensor_tensor(chip.xt_lo[:, p, :], chip.xt[:, p, :], chip.xt_hi[:, p, :].bitcast(F32),
                                    ALU.subtract).then_inc(self.xt_ready, 1)

    def wait_xt(self, eng, c):
        eng.wait_ge(self.xt_ready, self.xt_steps * (self.base + c) + self.xt_steps)

    routed = 0

    def logits_step(self, pe, c, p):
        pass

    def rows_turn_step(self, pe, c, p):
        pass

    def pair_step(self, act, c, p):
        pass

    def rows_kept_step(self, act, c, p):
        pass

    def route_first(self, dve, c, p):
        pass

    def route_second(self, dve, c, p):
        pass

    def route_last(self, dve, c, p):
        pass

    def wait_bank(self, pe, c):
        pass

    def wait_routed(self, dve, c):
        if known(c) != 0:
            dve.wait_ge(self.route_step, self.routed * (self.base + c))
        elif self.behind and self.behind.routed:
            dve.wait_ge(self.behind.route_step, self.behind.routed * (self.behind.base + NCH))


class Front0(Front):
    PAIR = TPC + 2
    ROUTE = routed = PAIR + TPC + 2 + 2 + 2 + 1

    def __init__(self, chip, call, behind):
        super().__init__(chip, "ffn0", call * NCH, behind, twice=True, affine=True, split=True)
        self.logits_done, self.route_step, self.pair_tanh, self.rows_turn, self.rows_kept, self.rows_stored = (
            chip.sem("ffn0_" + k) for k in ("logits_done", "route_step", "pair_tanh", "rows_turn", "rows_kept",
                                            "rows_stored"))

    def wait_bank(self, pe, c):
        wait(pe, self.rows_kept, self.base + c)

    def logits_step(self, pe, c, p):
        nc, chip, n = self.chip.nc, self.chip, self.base + c
        self.wait_xt(pe, c)
        for t in range(TPC):
            last = nc.tensor.matmul(self.turn_bank[:, t * E0:(t + 1) * E0], chip.xt[:, p, t * P:(t + 1) * P],
                                    chip.mats[:, MAT["gate"]], start=True, stop=True)
        last.then_inc(self.logits_done, 1)

    def rows_turn_step(self, pe, c, p):
        nc, chip, n = self.chip.nc, self.chip, self.base + c
        pe.wait_ge(self.route_step, self.ROUTE * n + self.ROUTE)
        for t in range(TPC):
            last = nc.tensor.transpose(self.turn_bank[0:E0, t * P:(t + 1) * P],
                                       chip.one_a[:, t, :], chip.ident[:])
        last.then_inc(self.rows_turn, 1)

    def pair_step(self, act, c, p):
        nc, chip, n = self.chip.nc, self.chip, self.base + c
        act.wait_ge(self.route_step, self.ROUTE * n + self.PAIR)
        nc.scalar.activation(chip.pair[:, 1, :], chip.pair[:, 0, :], ACT.Tanh, scale=0.5).then_inc(self.pair_tanh, 1)

    def rows_kept_step(self, act, c, p):
        nc, chip, n = self.chip.nc, self.chip, self.base + c
        act.wait_ge(self.rows_turn, n + 1)
        wait(act, self.rows_stored, 16 * n)
        nc.scalar.activation(chip.w_rows[:], self.turn_bank[0:E0, :], ACT.Copy).then_inc(self.rows_kept, 1)

    def route_first(self, dve, c, p):
        nc, chip, n = self.chip.nc, self.chip, self.base + c
        r = self.ROUTE * n
        dve.wait_ge(self.logits_done, n + 1)
        self.wait_routed(dve, c)
        nc.vector.tensor_tensor(chip.logits0[:], self.turn_bank[:, 0:TPC * E0].rearrange(
            "p (t e) -> p t e", t=TPC), across(chip.rows[:, ROW["gate_b"]].unsqueeze(1), [P, TPC, E0]),
            ALU.add).then_inc(self.route_step, 1)
        wait_alone(dve, self.route_step, r + 1, chip.sem("dve_passed"))
        for t in range(TPC):
            nc.vector.max(chip.best[:, t, :], chip.logits0[:, t, :]).then_inc(self.route_step, 1)
        dve.wait_ge(self.route_step, r + 1 + TPC)
        nc.vector.tensor_tensor(chip.pair[:, 0, :], chip.best[:, :, 1], chip.best[:, :, 0],
                                ALU.subtract).then_inc(self.route_step, 1)
        for t in range(TPC):
            nc.vector.max_index(chip.best_at[:, t, :], chip.best[:, t, :], chip.logits0[:, t, :]).then_inc(
                self.route_step, 1)
        dve.wait_ge(self.route_step, r + self.PAIR + TPC)
        wait(dve, self.rows_turn, n)
        for k, one in enumerate((chip.one_a, chip.one_b)):
            nc.vector.tensor_tensor(one[:], across(chip.iota_row[:, 0:E0].unsqueeze(1), [P, TPC, E0]),
                                    across(chip.best_at[:, :, k:k + 1], [P, TPC, E0]), ALU.is_equal).then_inc(
                                        self.route_step, 1)

    def route_second(self, dve, c, p):
        nc, chip, n = self.chip.nc, self.chip, self.base + c
        r = self.ROUTE * n + self.PAIR + TPC + 2
        dve.wait_ge(self.pair_tanh, n + 1)
        for k, sign in enumerate((-0.5, 0.5)):
            nc.vector.tensor_scalar(chip.pair_w[:, k, :], chip.pair[:, 1, :], sign, 0.5, ALU.mult,
                                    ALU.add).then_inc(self.route_step, 1)
        dve.wait_ge(self.route_step, r + 2)
        for k, one in enumerate((chip.one_a, chip.one_b)):
            nc.vector.tensor_tensor(one[:], one[:], across(chip.pair_w[:, k, :].unsqueeze(2), [P, TPC, E0]),
                                    ALU.mult).then_inc(self.route_step, 1)
        dve.wait_ge(self.route_step, r + 4)
        nc.vector.tensor_tensor(chip.one_a[:], chip.one_a[:], chip.one_b[:], ALU.add).then_inc(self.route_step, 1)


class Front1(Front):
    ROUTE = routed = 2 + 2 * TPC

    def __init__(self, chip, call, behind):
        super().__init__(chip, "ffn1", call * NCH, behind, twice=False, affine=False, split=True)
        self.logits_done, self.route_step, self.rows_turn, self.rows_kept, self.blocked_made = (
            chip.sem("ffn1_" + k) for k in ("logits_done", "route_step", "rows_turn", "rows_kept", "blocked_made"))

    def wait_bank(self, pe, c):
        wait(pe, self.rows_kept, self.base + c)

    def logits_step(self, pe, c, p):
        nc, chip, n = self.chip.nc, self.chip, self.base + c
        self.wait_xt(pe, c)
        for t in range(TPC):
            last = nc.tensor.matmul(self.turn_bank[:, t * E1:(t + 1) * E1], chip.xt[:, p, t * P:(t + 1) * P],
                                    chip.mats[:, MAT["router"]], start=True, stop=True)
        last.then_inc(self.logits_done, 1)

    def rows_turn_step(self, pe, c, p):
        nc, chip, n = self.chip.nc, self.chip, self.base + c
        wait_alone(pe, self.route_step, self.ROUTE * n + self.ROUTE, chip.sem("pe_passed"))
        for t in range(TPC):
            last = nc.tensor.transpose(self.turn_bank[0:2 * E1, t * P:(t + 1) * P], chip.chosen[:, t, :],
                                       chip.ident[:])
        last.then_inc(self.rows_turn, 1)

    def rows_kept_step(self, act, c, p):
        nc, chip, n = self.chip.nc, self.chip, self.base + c
        act.wait_ge(self.rows_turn, n + 1)
        nc.scalar.activation(chip.chosen_t[:, p, :], self.turn_bank[0:2 * E1, :], ACT.Copy).then_inc(self.rows_kept, 1)

    def route_first(self, dve, c, p):
        nc, chip, n = self.chip.nc, self.chip, self.base + c
        r = self.ROUTE * n
        dve.wait_ge(self.logits_done, n + 1)
        self.wait_routed(dve, c)
        nc.vector.tensor_tensor(chip.logits1[:], self.turn_bank[:, 0:TPC * E1].rearrange(
            "p (t e) -> p t e", t=TPC), across(chip.rows[:, ROW["router_b"]].unsqueeze(1), [P, TPC, E1]),
            ALU.add).then_inc(self.route_step, 1)
        wait_alone(dve, self.route_step, r + 1, chip.sem("dve_passed"))
        for t in range(TPC):
            nc.vector.max(chip.best[:, t, :], chip.logits1[:, t, :]).then_inc(self.route_step, 1)
        wait_alone(dve, self.route_step, r + 1 + TPC, chip.sem("dve_passed"))
        for t in range(TPC):
            nc.vector.max_index(chip.best_at[:, t, :], chip.best[:, t, :], chip.logits1[:, t, :]).then_inc(
                self.route_step, 1)
        dve.wait_ge(self.route_step, r + 1 + 2 * TPC)
        wait(dve, self.rows_turn, n)
        nc.vector.tensor_tensor(chip.chosen[:], across(chip.iota_row[:].unsqueeze(1), [P, TPC, 2 * E1]),
                                across(chip.best_at[:, :, 0:1], [P, TPC, 2 * E1]), ALU.is_equal).then_inc(
                                    self.route_step, 1)

    def route_last(self, dve, c, p):
        nc, chip, n = self.chip.nc, self.chip, self.base + c
        dve.wait_ge(self.rows_kept, n + 1)
        nc.vector.tensor_scalar(chip.blocked_t[0:E1, p, :], chip.chosen_t[0:E1, p, :].bitcast(F32), -1.0, None,
                                ALU.add).then_inc(self.blocked_made, 1)


def coming(front, ahead, c, p):
    if known(c) == NCH - 1:
        return ahead, 0, 0
    return front, c + 1, 1 - p



def ffn0_stage(chip, front, ahead):
    nc, x = chip.nc, chip.x
    base = front.base

    def s(name):
        return chip.sem("ffn0_" + name)

    H, OUT, TOKEN_MAJOR = (0, 1, 4, 5), (2, 3), 7
    ROT = ABEL = TOKEN_MAJOR
    LAG = LAG0
    hid, wide, weighted, moe, abel, abel_pre, kept, diff, dots_a, dots_b = chip.rooms(
        (4, CH), (E0, CH), (2, CH), (2, CH), (2, CH), (CH,), (TPC, P), (TPC, P), (TPC, P), (TPC, P))
    tiles = "p (t d) -> p t d"

    hid_done, gelu_done, hi_done = s("hid_done"), s("gelu_done"), s("hi_done")
    lo_even, lo_odd = s("lo_even"), s("lo_odd")
    out_done = s("out_done")
    wide_loaded = [s(f"wide_loaded_{e}") for e in range(E0)]
    weighted_done, moe_added = s("weighted_done"), s("moe_added")
    abel_mm, abel_biased, abel_done = s("abel_mm"), s("abel_biased"), s("abel_done")
    rot_mm, tail_step, gate_tanh, x_new, kept_done = (
        s("rot_mm"), s("tail_step"), s("gate_tanh"), s("x_new"), s("kept_done"))
    DOTS = 2 * TPC + 2
    TAIL = DOTS + 2

    with nc.Block() as block:
        @block.sync
        def _(sp):
            def body(c, p):
                wait_alone(sp, front.rows_kept, base + c + 1, chip.sem("sp_passed"))
                if known(c) != 0:
                    for e in range(E0):
                        wait_alone(sp, wide_loaded[e], 16 * (base + c), chip.sem("sp_passed"))
                sp.dma_start(chip.w_rows_dram, chip.w_rows[:]).then_inc(front.rows_stored, 16)
                wait_alone(sp, front.rows_stored, 16 * (base + c) + 16, chip.sem("sp_passed"))
                for e in range(E0):
                    if known(c) != 0:
                        sp.wait_ge(weighted_done, E0 * (base + c - 1) + e + 1)
                    sp.dma_start(wide[:, e, :], across(chip.w_rows_dram[e:e + 1, :], [P, CH])).then_inc(
                        wide_loaded[e], 16)

            chunks(sp, body)

        @block.tensor
        def _(pe):
            def hidden(c, p, e):
                if e == 0:
                    front.wait_xt(pe, c)
                for j in range(HC):
                    u = HC * e + j
                    wait(pe, gelu_done, U0 * (base + c) + u - 3)
                    for k, (w, v) in enumerate(((chip.ew1_hi, chip.xt_hi), (chip.ew1_hi, chip.xt_lo),
                                                (chip.ew1_lo, chip.xt_hi))):
                        last = nc.tensor.matmul(chip.bank[H[u % 4]][:], w[:, u, :], v[:, p, :], start=k == 0,
                                                stop=k == 2)
                    last.then_inc(hid_done, 1)

            def out_product(c, e):
                n = E0 * (base + c) + e
                pe.wait_ge(lo_even, n + 1)
                pe.wait_ge(lo_odd, n + 1)
                wait(pe, weighted_done, n - 1)
                k = 0
                for j in range(HC):
                    u = HC * e + j
                    for w, v in ((chip.ew2_hi, chip.hid_hi), (chip.ew2_hi, chip.hid_lo), (chip.ew2_lo, chip.hid_hi)):
                        last = nc.tensor.matmul(chip.bank[OUT[e % 2]][:], w[:, u, :], v[:, u % 8, :], start=k == 0,
                                                stop=k == 5)
                        k += 1
                last.then_inc(out_done, 1)

            def abel_step(c, p):
                if known(c) != 0:
                    pe.wait_ge(tail_step, TAIL * (base + c - 1) + DOTS + 1)
                for t in range(TPC):
                    last = nc.tensor.matmul(chip.bank[ABEL][:, t * P:(t + 1) * P], chip.xt[:, p, t * P:(t + 1) * P],
                                            chip.mats[:, MAT["abel"]], start=True, stop=True)
                last.then_inc(abel_mm, 1)

            def rot_step(c, p):
                pe.wait_ge(moe_added, (E0 - 1) * (base + c) + E0 - 1)
                pe.wait_ge(abel_biased, base + c + 1)
                for t in range(TPC):
                    last = nc.tensor.matmul(chip.bank[ROT][:, t * P:(t + 1) * P], moe[:, p, t * P:(t + 1) * P],
                                            chip.rotation[:], start=True, stop=True)
                last.then_inc(rot_mm, 1)

            def between(slot, c, p):
                if slot == AT0["abel_mm"]:
                    abel_step(c, p)
                if slot == AT0["rot"] and known(c) != 0:
                    rot_step(c - 1, 1 - p)
                f, n, q = coming(front, ahead, c, p)
                if f:
                    if slot == AT0["turn"]:
                        f.turn_step(pe, n, q)
                    if slot == AT0["logits"]:
                        f.logits_step(pe, n, q)
                    if slot == AT0["w_turn"]:
                        f.rows_turn_step(pe, n, q)

            def body(c, p):
                for e in range(E0):
                    hidden(c, p, e)
                    between(2 * e, c, p)
                    if e >= LAG:
                        out_product(c, e - LAG)
                    elif known(c) != 0:
                        out_product(c - 1, e - LAG + E0)
                    between(2 * e + 1, c, p)

            chunks(pe, body)
            for e in range(E0 - LAG, E0):
                out_product(NCH - 1, e)
            rot_step(NCH - 1, 1)

        @block.scalar
        def _(act):
            def gelus(c, e):
                n = E0 * (base + c) + e
                for j in range(HC):
                    u = HC * e + j
                    act.wait_ge(hid_done, HC * n + j + 1)
                    wait(act, lo_odd if j else lo_even, n - 1)
                    nc.scalar.activation(hid[:, u % 4, :], chip.bank[H[u % 4]][:], ACT.Gelu,
                                         bias=chip.cols[:, COL["eb1"]][:, u:u + 1]).then_inc(gelu_done, 1)

            def high_parts(c, e):
                n = E0 * (base + c) + e
                wait(act, out_done, n - 3)
                for j in range(HC):
                    u = HC * e + j
                    act.wait_ge(gelu_done, HC * n + j + 1)
                    nc.scalar.activation(chip.hid_hi[:, u % 8, :], hid[:, u % 4, :], ACT.Copy).then_inc(hi_done, 1)

            def abel_step(c, p):
                act.wait_ge(abel_biased, base + c + 1)
                nc.scalar.activation(abel[:, p, :], abel_pre, ACT.Gelu).then_inc(abel_done, 1)

            def gate_step(c):
                act.wait_ge(tail_step, TAIL * (base + c) + DOTS)
                nc.scalar.activation(chip.gate[:, 3, :], chip.gate[:, 2, :], ACT.Tanh, scale=0.5,
                                     bias=chip.half_gc_b[:]).then_inc(gate_tanh, 1)

            def between(slot, c, p):
                if slot == AT0["abel"]:
                    abel_step(c, p)
                if slot == AT0["gate"] and known(c) != 0:
                    gate_step(c - 1)
                f, n, q = coming(front, ahead, c, p)
                if f:
                    if slot == AT0["pair"]:
                        f.pair_step(act, n, q)
                    if slot == AT0["w_kept"]:
                        f.rows_kept_step(act, n, q)

            def body(c, p):
                for e in range(E0):
                    gelus(c, e)
                    between(2 * e, c, p)
                    high_parts(c, e)
                    between(2 * e + 1, c, p)

            chunks(act, body)
            if ahead and not ahead.routed:
                nc.scalar.preload_act_table(ACT.Exp)
            gate_step(NCH - 1)

        @block.vector
        def _(dve):
            def low(c, e):
                u = HC * e
                dve.wait_ge(hi_done, U0 * (base + c) + u + 1)
                nc.vector.tensor_tensor(chip.hid_lo[:, u % 8, :], hid[:, u % 4, :],
                                        chip.hid_hi[:, u % 8, :].bitcast(F32), ALU.subtract).then_inc(lo_even, 1)

            def weigh(c, p, e):
                n = E0 * (base + c) + e
                dve.wait_ge(out_done, n + 1)
                dve.wait_ge(wide_loaded[e], 16 * (base + c) + 16)
                if e:
                    wait(dve, moe_added, (E0 - 1) * (base + c) + max(e - 2, 0))
                nc.vector.scalar_tensor_tensor(out=weighted[:, e % 2, :] if e else moe[:, p, :],
                                               in0=chip.bank[OUT[e % 2]][:],
                                               scalar=chip.cols[:, COL["eb2"]][:, e:e + 1], in1=wide[:, e, :],
                                               op0=ALU.add, op1=ALU.mult).then_inc(weighted_done, 1)

            def abel_bias(c):
                dve.wait_ge(abel_mm, base + c + 1)
                wait(dve, abel_done, base + c)
                nc.vector.tensor_tensor(abel_pre.rearrange(tiles, t=TPC), chip.bank[ABEL][:].rearrange(tiles, t=TPC),
                                        across(chip.rows[:, ROW["abel_b"]].unsqueeze(1), [P, TPC, P]),
                                        ALU.add).then_inc(abel_biased, 1)

            def keep_input(c, p):
                wait(dve, x_new, TPC * (base + c))
                for t in range(TPC):
                    nc.vector.tensor_scalar(kept[:, t, :].unsqueeze(1), x[:, bass.ds(TPC * c + t, 1), :],
                                            chip.keep_scale[:, p, t:t + 1], chip.keep_shift[:, p, t:t + 1],
                                            ALU.mult, ALU.add).then_inc(kept_done, 1)

            def gate_dots(c, p, k):
                r = TAIL * (base + c)
                if k == 0:
                    dve.wait_ge(abel_done, base + c + 1)
                    wait(dve, tail_step, r)
                    v, w, dots = abel[:, p, :].rearrange(tiles, t=TPC), "gate_abel", dots_a
                else:
                    dve.wait_ge(rot_mm, base + c + 1)
                    v, w, dots = chip.bank[ROT][:].rearrange(tiles, t=TPC), "gate_moe", dots_b
                for t in range(TPC):
                    nc.vector.tensor_tensor_reduce(
                        out=dots[:, t, :], in0=v[:, t, :], in1=chip.rows[:, ROW[w]], scale=1.0, scalar=0.0,
                        op0=ALU.mult, op1=ALU.add, accum_out=chip.gate[:, k, t:t + 1]).then_inc(tail_step, 1)
                if k == 0:
                    dve.wait_ge(kept_done, TPC * (base + c) + TPC)
                    nc.vector.scalar_tensor_tensor(out=kept.rearrange("p t d -> p (t d)"), in0=abel[:, p, :],
                                                   scalar=0.5, in1=kept.rearrange("p t d -> p (t d)"), op0=ALU.mult,
                                                   op1=ALU.add).then_inc(tail_step, 1)
                else:
                    dve.wait_ge(tail_step, r + 2 * TPC + 1)
                    nc.vector.tensor_tensor(chip.gate[:, 2, :], chip.gate[:, 0, :], chip.gate[:, 1, :],
                                            ALU.add).then_inc(tail_step, 1)

            def difference(c, p):
                nc.vector.tensor_tensor(diff, chip.bank[ROT][:].rearrange(tiles, t=TPC),
                                        abel[:, p, :].rearrange(tiles, t=TPC), ALU.subtract).then_inc(tail_step, 1)

            def mix(c):
                r = TAIL * (base + c)
                dve.wait_ge(gate_tanh, base + c + 1)
                nc.vector.tensor_scalar(chip.gate[:, 4, :], chip.gate[:, 3, :], 0.25, 0.25, ALU.mult,
                                        ALU.add).then_inc(tail_step, 1)
                dve.wait_ge(tail_step, r + TAIL)
                for t in range(TPC):
                    nc.vector.scalar_tensor_tensor(out=x[:, bass.ds(TPC * c + t, 1), :], in0=diff[:, t:t + 1, :],
                                                   scalar=chip.gate[:, 4, t:t + 1], in1=kept[:, t:t + 1, :],
                                                   op0=ALU.mult, op1=ALU.add).then_inc(x_new, 1)

            def between(slot, c, p):
                if slot == AT0["abel_bias"]:
                    abel_bias(c)
                if known(c) != 0:
                    if slot == AT0["dots_abel"]:
                        gate_dots(c - 1, 1 - p, 0)
                    if slot == AT0["dots_moe"]:
                        gate_dots(c - 1, 1 - p, 1)
                    if slot == AT0["difference"]:
                        difference(c - 1, 1 - p)
                    if slot == AT0["mix"]:
                        mix(c - 1)
                if slot == AT0["keep_input"] - (3 if known(c) == NCH - 1 else 0):
                    keep_input(c, p)
                f, n, q = coming(front, ahead, c, p)
                if f:
                    if slot == AT0["moments"]:
                        f.moments_step(dve, n, q)
                    if slot == AT0["normed"]:
                        f.normed_step(dve, n, q)
                    if slot == AT0["keep"]:
                        f.keep_step(dve, n, q)
                    if slot == AT0["split"]:
                        f.split_step(dve, n, q)
                    if slot == AT0["route_pair"]:
                        f.route_first(dve, n, q)
                    if slot == AT0["route_weights"]:
                        f.route_second(dve, n, q)

            def body(c, p):
                for e in range(E0):
                    low(c, e)
                    between(2 * e, c, p)
                    if e >= LAG:
                        weigh(c, p, e - LAG)
                    elif known(c) != 0:
                        weigh(c - 1, 1 - p, e - LAG + E0)
                    between(2 * e + 1, c, p)

            chunks(dve, body)
            gate_dots(NCH - 1, 1, 0)
            for e in range(E0 - LAG, E0):
                weigh(NCH - 1, 1, e)
                dve.wait_ge(moe_added, (E0 - 1) * (base + NCH - 1) + e - 1)
                dve.wait_ge(weighted_done, E0 * (base + NCH - 1) + e + 1)
                nc.vector.tensor_tensor(moe[:, 1, :], moe[:, 1, :], weighted[:, e % 2, :], ALU.add).then_inc(
                    moe_added, 1)
            gate_dots(NCH - 1, 1, 1)
            difference(NCH - 1, 1)
            mix(NCH - 1)
            if ahead:
                ahead.route_last(dve, 0, 0)

        @block.gpsimd
        def _(pool):
            def low(c, e):
                u = HC * e + 1
                pool.wait_ge(hi_done, U0 * (base + c) + u + 1)
                nc.gpsimd.tensor_tensor(chip.hid_lo[:, u % 8, :], hid[:, u % 4, :],
                                        chip.hid_hi[:, u % 8, :].bitcast(F32), ALU.subtract).then_inc(lo_odd, 1)

            def add(c, p, e):
                if e == 0:
                    return
                pool.wait_ge(weighted_done, E0 * (base + c) + e + 1)
                wait(pool, moe_added, (E0 - 1) * (base + c) + e - 1)
                nc.gpsimd.tensor_tensor(moe[:, p, :], moe[:, p, :], weighted[:, e % 2, :], ALU.add).then_inc(
                    moe_added, 1)

            def body(c, p):
                for e in range(E0):
                    low(c, e)
                    if e >= LAG:
                        add(c, p, e - LAG)
                    elif known(c) != 0:
                        add(c - 1, 1 - p, e - LAG + E0)
                    f, n, q = coming(front, ahead, c, p)
                    if e == AT0["power"] and f:
                        f.power_step(pool, n, q)

            chunks(pool, body)



def ffn1_stage(chip, front, ahead, out):
    nc, x = chip.nc, chip.x
    base = front.base

    def s(name):
        return chip.sem("ffn1_" + name)

    H, SUM, BACK = (0, 1, 2, 3), (4, 5), 7
    LAG = LAG1
    y_t, = chip.rooms((CH,))
    tiles = "p (t d) -> p t d"

    hid_done, hi_done, lo_done = s("hid_done"), s("hi_done"), s("lo_done")
    out_mm, sum_done = s("out_mm"), s("sum_done")
    y_ready, back_done, x_new, stored = s("y_ready"), s("back_done"), s("x_new"), s("stored")

    with nc.Block() as block:
        @block.sync
        def _(sp):
            if ahead:
                return
            for c in range(NCH):
                sp.wait_ge(x_new, base + c + 1)
                sp.dma_start(out[c * CH:(c + 1) * CH, :].rearrange("(t p) d -> p t d", p=P),
                             x[:, c * TPC:(c + 1) * TPC, :]).then_inc(stored, 16)
            sp.wait_ge(stored, 16 * NCH)

        @block.tensor
        def _(pe):
            def hidden(c, p, u):
                if u == 0:
                    front.wait_xt(pe, c)
                    pe.wait_ge(front.blocked_made, base + c + 1)
                wait(pe, lo_done, U1 * (base + c) + u - 3)
                b = chip.bank[H[u % 4]]
                nc.tensor.matmul(b[:], chip.block_expert[:, u, :], chip.blocked_t[:, p, :], start=True, stop=False)
                for k, (w, v) in enumerate(((chip.w1_hi, chip.xt_hi), (chip.w1_hi, chip.xt_lo),
                                            (chip.w1_lo, chip.xt_hi))):
                    last = nc.tensor.matmul(b[:], w[:, u, :], v[:, p, :], start=False, stop=k == 2)
                last.then_inc(hid_done, 1)

            def out_product(c, p, u):
                n = U1 * (base + c) + u
                pe.wait_ge(lo_done, n + 1)
                b = chip.bank[SUM[p]]
                for k, (w, v) in enumerate(((chip.w2_hi, chip.hid_hi), (chip.w2_hi, chip.hid_lo),
                                            (chip.w2_lo, chip.hid_hi))):
                    last = nc.tensor.matmul(b[:], w[:, u, :], v[:, u, :], start=u == 0 and k == 0, stop=False)
                last.then_inc(out_mm, 1)
                if u == U1 - 1:
                    nc.tensor.matmul(b[:], chip.b2_split[:], chip.chosen_t[:, p, :], start=False, stop=True).then_inc(
                        sum_done, 1)

            def back_step(c):
                pe.wait_ge(y_ready, base + c + 1)
                wait(pe, x_new, base + c)
                for t in range(TPC):
                    last = nc.tensor.transpose(chip.bank[BACK][:, t * P:(t + 1) * P], y_t[:, t * P:(t + 1) * P],
                                               chip.ident[:])
                last.then_inc(back_done, 1)

            def between(slot, c, p):
                if slot == AT1["back"] and known(c) != 0:
                    back_step(c - 1)
                f, n, q = coming(front, ahead, c, p)
                if f:
                    if slot == AT1["turn"]:
                        f.turn_step(pe, n, q)
                    if slot == AT1["logits"]:
                        f.logits_step(pe, n, q)
                    if slot == AT1["one_turn"]:
                        f.rows_turn_step(pe, n, q)

            def body(c, p):
                for u in range(U1):
                    hidden(c, p, u)
                    between(2 * u, c, p)
                    if u >= LAG:
                        out_product(c, p, u - LAG)
                    elif known(c) != 0:
                        out_product(c - 1, 1 - p, u - LAG + U1)
                    between(2 * u + 1, c, p)

            chunks(pe, body)
            for u in range(U1 - LAG, U1):
                out_product(NCH - 1, 1, u)
            back_step(NCH - 1)

        @block.scalar
        def _(act):
            def high_part(c, u):
                n = U1 * (base + c) + u
                act.wait_ge(hid_done, n + 1)
                wait(act, out_mm, n - 7)
                nc.scalar.activation(chip.hid_hi[:, u, :], chip.bank[H[u % 4]][:], ACT.Relu).then_inc(hi_done, 1)

            def y_step(c, p):
                act.wait_ge(sum_done, base + c + 1)
                wait(act, back_done, base + c)
                nc.scalar.activation(y_t, chip.bank[SUM[p]][:], ACT.Relu).then_inc(y_ready, 1)

            def between(slot, c, p):
                if slot == AT1["y"] and known(c) != 0:
                    y_step(c - 1, 1 - p)
                f, n, q = coming(front, ahead, c, p)
                if slot == AT1["one_kept"] and f:
                    f.rows_kept_step(act, n, q)

            def body(c, p):
                for u in range(U1):
                    high_part(c, u)
                    between(u, c, p)

            chunks(act, body)
            if ahead:
                nc.scalar.preload_act_table(ACT.Sigmoid)
            y_step(NCH - 1, 1)

        @block.vector
        def _(dve):
            def low(c, u):
                dve.wait_ge(hi_done, U1 * (base + c) + u + 1)
                nc.vector.scalar_tensor_tensor(out=chip.hid_lo[:, u, :], in0=chip.bank[H[u % 4]][:], scalar=0.0,
                                               in1=chip.hid_hi[:, u, :].bitcast(F32), op0=ALU.max,
                                               op1=ALU.subtract).then_inc(lo_done, 1)

            def add_step(c):
                dve.wait_ge(back_done, base + c + 1)
                tile = x[:, bass.ds(TPC * c, TPC), :]
                nc.vector.scalar_tensor_tensor(out=tile, in0=chip.bank[BACK][:].rearrange(tiles, t=TPC), scalar=0.5,
                                               in1=tile, op0=ALU.mult, op1=ALU.add).then_inc(x_new, 1)

            def between(slot, c, p):
                if slot == AT1["add"] and known(c) != 0:
                    add_step(c - 1)
                f, n, q = coming(front, ahead, c, p)
                if f:
                    if slot == AT1["moments"]:
                        f.moments_step(dve, n, q)
                    if slot == AT1["normed"]:
                        f.normed_step(dve, n, q)
                    if slot == AT1["keep"]:
                        f.keep_step(dve, n, q)
                    if slot == AT1["split"]:
                        f.split_step(dve, n, q)
                    if slot == AT1["route"]:
                        f.route_first(dve, n, q)
                    if slot == AT1["block"]:
                        f.route_last(dve, n, q)

            def body(c, p):
                for u in range(U1):
                    low(c, u)
                    between(u, c, p)

            chunks(dve, body)
            add_step(NCH - 1)

        @block.gpsimd
        def _(pool):
            def body(c, p):
                f, n, q = coming(front, ahead, c, p)
                if f:
                    f.power_step(pool, n, q)

            chunks(pool, body)



def attn0_stage(chip, front, ahead):
    nc, x = chip.nc, chip.x

    def s(name):
        return chip.sem("attn0_" + name)

    QB, KB, VB, SCORES, ATT, LOCAL, OUT = 0, 1, 2, 3, 4, 5, 7
    NS = TOKENS // SEG
    NB = NS // BATCH
    local, q_t, k_t, v_tok, att, att_t, wide, o_t, glob, g_small = chip.rooms(
        (TOKENS,), (CH,), (CH,), (2, CH), (TPC, P), (CH,), (TPC, P), (CH,), (8, P), (4, 8))
    g_x, g_xt, g_q, g_k, g_v, g_att, g_att_t, g_out = (glob[:, k, :] for k in range(8))
    g_sc, g_bank = wide[:, 3, 0:NB], chip.bank[OUT]
    g_stats, g_moments, g_r, g_soft = g_small[:, 0, 0:6], g_small[:, 1, 0:2], g_small[:, 2, :], g_small[:, 3, :]
    sc = wide[:, 0, :].rearrange("p (t j) -> p t j", t=TPC)
    ex = wide[:, 1, :].rearrange("p (t j) -> p t j", t=TPC)
    top, total, inv = (wide[:, 2, 8 * k:8 * k + TPC] for k in range(3))
    tiles = "p (t d) -> p t d"

    zeroed, q_mm, k_mm, v_mm = s("zeroed"), s("q_mm"), s("k_mm"), s("v_mm")
    q_kept, k_kept, v_kept = s("q_kept"), s("k_kept"), s("v_kept")
    scores_done, soft_step, exp_done = s("scores_done"), s("soft_step"), s("exp_done")
    att_turn, att_kept, local_mm, local_kept = s("att_turn"), s("att_kept"), s("local_mm"), s("local_kept")
    g_loaded, g_pe, g_act, g_dve, g_pow = s("g_loaded"), s("g_pe"), s("g_act"), s("g_dve"), s("g_pow")
    o_ready, o_mm, bo_added, x_new = s("o_ready"), s("o_mm"), s("bo_added"), s("x_new")
    SOFT = SPT + 1 + 1 + 1 + 1 + SPT
    G_SUB = 5 + BATCH
    G_ATT = G_SUB + 2 + BATCH
    OUT_LAG = 3

    with nc.Block() as block:
        @block.sync
        def _(sp):
            for g in range(SPT):
                sp.dma_start(g_x[g:P:SPT, :], x[SEG * g:SEG * g + 1, :, :]).then_inc(g_loaded, 16)
            sp.wait_ge(g_loaded, 16 * SPT)

        @block.tensor
        def _(pe):
            def qk_step(c, p):
                front.wait_xt(pe, c)
                wait(pe, q_kept, c)
                nc.tensor.matmul(chip.bank[QB][:], chip.mats[:, MAT["q0"]], chip.xt[:, p, :], start=True,
                                 stop=True).then_inc(q_mm, 1)
                wait(pe, k_kept, c)
                nc.tensor.matmul(chip.bank[KB][:], chip.mats[:, MAT["k0"]], chip.xt[:, p, :], start=True,
                                 stop=True).then_inc(k_mm, 1)

            def v_step(c, p):
                wait(pe, v_kept, c)
                for t in range(TPC):
                    last = nc.tensor.matmul(chip.bank[VB][:, t * P:(t + 1) * P], chip.xt[:, p, t * P:(t + 1) * P],
                                            chip.mats[:, MAT["v0"]], start=True, stop=True)
                last.then_inc(v_mm, 1)

            def scores(c):
                pe.wait_ge(q_kept, c + 1)
                pe.wait_ge(k_kept, c + 1)
                for t in range(TPC):
                    last = nc.tensor.matmul(chip.bank[SCORES][:, t * P:(t + 1) * P], q_t[:, t * P:(t + 1) * P],
                                            k_t[:, t * P:(t + 1) * P], start=True, stop=True)
                last.then_inc(scores_done, 1)

            def att_turn_step(c):
                pe.wait_ge(soft_step, SOFT * c + SOFT)
                for t in range(TPC):
                    last = nc.tensor.transpose(chip.bank[ATT][:, t * P:(t + 1) * P], att[:, t, :], chip.ident[:])
                last.then_inc(att_turn, 1)

            def local_step(c, p):
                pe.wait_ge(att_kept, c + 1)
                pe.wait_ge(v_kept, c + 1)
                wait(pe, local_kept, c)
                for t in range(TPC):
                    last = nc.tensor.matmul(chip.bank[LOCAL][:, t * P:(t + 1) * P], v_tok[:, p, t * P:(t + 1) * P],
                                            att_t[:, t * P:(t + 1) * P], start=True, stop=True)
                last.then_inc(local_mm, 1)

            def out_step(c):
                pe.wait_ge(o_ready, c + 1)
                wait(pe, x_new, c)
                for t in range(TPC):
                    last = nc.tensor.matmul(chip.bank[OUT][:, t * P:(t + 1) * P], o_t[:, t * P:(t + 1) * P],
                                            chip.mats[:, MAT["o0"]], start=True, stop=True)
                last.then_inc(o_mm, 1)

            def between_firsts(part):
                if part == 0:
                    pe.wait_ge(g_dve, 3)
                    nc.tensor.transpose(g_bank[:, 0:P], g_x, chip.ident[:]).then_inc(g_pe, 1)
                if part == 1:
                    pe.wait_ge(g_act, 1)
                    nc.tensor.matmul(g_bank[:, 0:P], chip.mats[:, MAT["q0"]], g_xt, start=True, stop=True)
                    nc.tensor.matmul(g_bank[:, P:2 * P], chip.mats[:, MAT["k0"]], g_xt, start=True, stop=True)
                    nc.tensor.matmul(g_bank[:, 2 * P:3 * P], g_xt, chip.mats[:, MAT["v0"]], start=True,
                                     stop=True).then_inc(g_pe, 1)
                if part == 2:
                    pe.wait_ge(g_act, 4)
                    nc.tensor.matmul(g_bank[:, 0:P], g_q, g_k, start=True, stop=True).then_inc(g_pe, 1)
                if part == 3:
                    pe.wait_ge(g_dve, G_ATT)
                    nc.tensor.transpose(g_bank[:, 0:P], g_att, chip.ident[:]).then_inc(g_pe, 1)
                if part == 4:
                    pe.wait_ge(g_act, 6)
                    nc.tensor.matmul(g_bank[:, 0:P], g_v, g_att_t, start=True, stop=True).then_inc(g_pe, 1)

            def body(c, p):
                f, n, q = coming(front, ahead, c, p)
                qk_step(c, p)
                v_step(c, p)
                if known(c) != 0:
                    att_turn_step(c - 1)
                if known(c) == 1:
                    between_firsts(1)
                scores(c)
                if known(c) not in (0, 1, 2):
                    out_step(c - OUT_LAG)
                f.turn_step(pe, n, q)
                if known(c) == 1:
                    between_firsts(2)
                if known(c) == 2:
                    between_firsts(3)
                if known(c) != 0:
                    local_step(c - 1, 1 - p)
                if known(c) == 0:
                    between_firsts(0)
                if known(c) == 2:
                    between_firsts(4)

            chunks_three(pe, body)
            out_step(NCH - 3)
            att_turn_step(NCH - 1)
            ahead.logits_step(pe, 0, 0)
            local_step(NCH - 1, 1)
            out_step(NCH - 2)
            out_step(NCH - 1)
            ahead.rows_turn_step(pe, 0, 0)

        @block.scalar
        def _(act):
            def qk_step(c):
                act.wait_ge(q_mm, c + 1)
                wait(act, scores_done, c)
                nc.scalar.activation(q_t, chip.bank[QB][:], ACT.Identity, bias=chip.cols[:, COL["bq"]]).then_inc(
                    q_kept, 1)
                act.wait_ge(k_mm, c + 1)
                nc.scalar.activation(k_t, chip.bank[KB][:], ACT.Identity, bias=chip.cols[:, COL["bk"]]).then_inc(
                    k_kept, 1)

            def v_step(c, p):
                act.wait_ge(v_mm, c + 1)
                nc.scalar.activation(v_tok[:, p, :], chip.bank[VB][:], ACT.Copy).then_inc(v_kept, 1)

            def att_step(c):
                act.wait_ge(att_turn, c + 1)
                wait(act, local_mm, c)
                nc.scalar.activation(att_t, chip.bank[ATT][:], ACT.Copy).then_inc(att_kept, 1)

            def exp_step(c):
                act.wait_ge(soft_step, SOFT * c + SPT + 2)
                nc.scalar.activation(ex, sc, ACT.Exp, scale=SCALE).then_inc(exp_done, 1)

            def local_step(c):
                act.wait_ge(local_mm, c + 1)
                nc.scalar.activation(local[:, bass.ds(CH * c, CH)], chip.bank[LOCAL][:], ACT.Identity,
                                     bias=chip.cols[:, COL["bv"]]).then_inc(local_kept, 1)

            def between_firsts(part):
                act.wait_ge(g_pe, part + 1)
                if part == 0:
                    nc.scalar.activation(g_xt, g_bank[:, 0:P], ACT.Copy).then_inc(g_act, 1)
                if part == 1:
                    for k, (dst, bias) in enumerate(((g_q, "bq"), (g_k, "bk"))):
                        nc.scalar.activation(dst, g_bank[:, k * P:(k + 1) * P], ACT.Identity,
                                             bias=chip.cols[:, COL[bias]]).then_inc(g_act, 1)
                    nc.scalar.activation(g_v, g_bank[:, 2 * P:3 * P], ACT.Copy).then_inc(g_act, 1)
                if part == 2:
                    act.wait_ge(g_dve, G_SUB)
                    nc.scalar.activation(g_sc, g_sc, ACT.Exp, scale=SCALE).then_inc(g_act, 1)
                if part == 3:
                    nc.scalar.activation(g_att_t, g_bank[:, 0:P], ACT.Copy).then_inc(g_act, 1)
                if part == 4:
                    nc.scalar.activation(g_out, g_bank[:, 0:P], ACT.Identity, bias=chip.cols[:, COL["bv"]]).then_inc(
                        g_act, 1)

            def body(c, p):
                qk_step(c)
                v_step(c, p)
                if known(c) != 0:
                    att_step(c - 1)
                if known(c) == 1:
                    between_firsts(1)
                if known(c) == 2:
                    between_firsts(2)
                if known(c) != NCH - 1:
                    front.keep_by_scalar(act, c + 1, 1 - p)
                exp_step(c)
                if known(c) == 2:
                    between_firsts(3)
                if known(c) != 0:
                    local_step(c - 1)
                if known(c) == 0:
                    between_firsts(0)
                if known(c) == 2:
                    between_firsts(4)

            chunks_three(act, body)
            nc.scalar.preload_act_table(ACT.Gelu)
            att_step(NCH - 1)
            local_step(NCH - 1)
            ahead.pair_step(act, 0, 0)
            ahead.rows_kept_step(act, 0, 0)

        @block.vector
        def _(dve):
            def softmax_first(c):
                r = SOFT * c
                dve.wait_ge(scores_done, c + 1)
                wait(dve, soft_step, r)
                for g in range(SPT):
                    rows = slice(SEG * g, SEG * (g + 1))
                    nc.vector.tensor_copy(sc[rows], chip.bank[SCORES][rows, :].rearrange(tiles, t=TPC)[
                        :, :, rows]).then_inc(soft_step, 1)
                dve.wait_ge(soft_step, r + SPT)
                nc.vector.tensor_reduce(top, sc, AX.X, ALU.max).then_inc(soft_step, 1)
                dve.wait_ge(soft_step, r + SPT + 1)
                nc.vector.tensor_tensor(sc, sc, across(top.unsqueeze(2), [P, TPC, SEG]), ALU.subtract).then_inc(
                    soft_step, 1)

            def softmax_second(c):
                r = SOFT * c
                dve.wait_ge(exp_done, c + 1)
                nc.vector.tensor_reduce(total, ex, AX.X, ALU.add).then_inc(soft_step, 1)
                dve.wait_ge(soft_step, r + SPT + 3)
                nc.vector.reciprocal(inv, total).then_inc(soft_step, 1)
                dve.wait_ge(soft_step, r + SPT + 4)
                if known(c) == 0:
                    dve.wait_ge(zeroed, 2)
                wait(dve, att_turn, c)
                for g in range(SPT):
                    rows = slice(SEG * g, SEG * (g + 1))
                    nc.vector.tensor_tensor(att[rows, :, rows], ex[rows], across(inv[rows].unsqueeze(2), [SEG, TPC, SEG]),
                                            ALU.mult).then_inc(soft_step, 1)

            def residual(c):
                dve.wait_ge(o_mm, c + 1)
                dve.wait_ge(bo_added, c + 1)
                tile = x[:, bass.ds(TPC * c, TPC), :]
                nc.vector.tensor_tensor(tile, chip.bank[OUT][:].rearrange(tiles, t=TPC), tile, ALU.add).then_inc(
                    x_new, 1)

            def between_firsts(part):
                if part == 0:
                    dve.wait_ge(g_loaded, 16 * SPT)
                    nc.vector.bn_stats(g_stats, g_x).then_inc(g_dve, 1)
                    dve.wait_ge(g_dve, 1)
                    nc.vector.bn_aggr(g_moments, g_stats).then_inc(g_dve, 1)
                if part == 1:
                    dve.wait_ge(g_pow, 2)
                    nc.vector.tensor_scalar(g_x, g_x, g_moments[:, 0:1], g_r[:, 1:2], ALU.subtract,
                                            ALU.mult).then_inc(g_dve, 1)
                if part == 2:
                    dve.wait_ge(g_pe, 3)
                    for b in range(BATCH):
                        rows = slice(NB * b, NB * (b + 1))
                        nc.vector.tensor_copy(g_sc[rows], g_bank[rows, rows]).then_inc(g_dve, 1)
                    dve.wait_ge(g_dve, 3 + BATCH)
                    nc.vector.tensor_reduce(g_soft[:, 0:1], g_sc, AX.X, ALU.max).then_inc(g_dve, 1)
                    dve.wait_ge(g_dve, 4 + BATCH)
                    nc.vector.tensor_scalar(g_sc, g_sc, g_soft[:, 0:1], None, ALU.subtract).then_inc(g_dve, 1)
                if part == 3:
                    dve.wait_ge(g_act, 5)
                    nc.vector.tensor_reduce(g_soft[:, 1:2], g_sc, AX.X, ALU.add).then_inc(g_dve, 1)
                    dve.wait_ge(g_dve, G_SUB + 1)
                    nc.vector.reciprocal(g_soft[:, 2:3], g_soft[:, 1:2]).then_inc(g_dve, 1)
                    dve.wait_ge(g_dve, G_SUB + 2)
                    for b in range(BATCH):
                        rows = slice(NB * b, NB * (b + 1))
                        nc.vector.tensor_scalar(g_att[rows, rows], g_sc[rows], g_soft[rows, 2:3], None,
                                                ALU.mult).then_inc(g_dve, 1)

            def body(c, p):
                f, n, q = coming(front, ahead, c, p)
                f.moments_step(dve, n, q)
                if known(c) != 0:
                    softmax_second(c - 1)
                if known(c) == 0:
                    between_firsts(0)
                if known(c) == 2:
                    between_firsts(3)
                f.normed_step(dve, n, q)
                softmax_first(c)
                if known(c) not in (0, 1, 2):
                    residual(c - OUT_LAG)
                if known(c) == 0:
                    between_firsts(1)
                if known(c) == 1:
                    between_firsts(2)

            chunks_three(dve, body)
            softmax_second(NCH - 1)
            residual(NCH - 3)
            ahead.keep_step(dve, 0, 0)
            ahead.split_step(dve, 0, 0)
            ahead.route_first(dve, 0, 0)
            residual(NCH - 2)
            residual(NCH - 1)
            ahead.route_second(dve, 0, 0)
            ahead.route_last(dve, 0, 0)

        @block.gpsimd
        def _(pool):
            def add_bias(c):
                if known(c) == 0:
                    pool.wait_ge(g_loaded, 16 * SPT)
                pool.wait_ge(front.xs_ready, TPC * c + TPC)
                tile = x[:, bass.ds(TPC * c, TPC), :]
                nc.gpsimd.tensor_tensor(tile, tile, across(chip.rows[:, ROW["bo"]].unsqueeze(1), [P, TPC, P]),
                                        ALU.add).then_inc(bo_added, 1)

            def sum_step(c):
                pool.wait_ge(local_kept, c + 1)
                wait(pool, o_mm, c)
                nc.gpsimd.tensor_tensor(o_t.rearrange("p (n s) -> p n s", s=SEG),
                                        local[:, bass.ds(CH * c, CH)].rearrange("p (n s) -> p n s", s=SEG),
                                        across(g_out[:, bass.ds(SPC * c, SPC)].unsqueeze(2), [P, SPC, SEG]),
                                        ALU.add).then_inc(o_ready, 1)

            def body(c, p):
                f, n, q = coming(front, ahead, c, p)
                if known(c) not in (0, 1, 2):
                    sum_step(c - OUT_LAG)
                f.power_step(pool, n, q)
                if known(c) == 0:
                    pool.wait_ge(g_dve, 2)
                    nc.gpsimd.tensor_scalar(g_r[:, 0:1], g_moments[:, 1:2], 1.0, EPS, ALU.mult, ALU.add).then_inc(
                        g_pow, 1)
                    pool.wait_ge(g_pow, 1)
                    nc.gpsimd.tensor_tensor(g_r[:, 1:2], g_r[:, 0:1], chip.neg_half[:, 0:1], ALU.pow).then_inc(g_pow, 1)
                add_bias(c)
                if known(c) == OUT_LAG - 1:
                    pool.wait_ge(g_act, 7)

            nc.gpsimd.memset(att, 0.0).then_inc(zeroed, 1)
            nc.gpsimd.memset(g_att, 0.0).then_inc(zeroed, 1)
            chunks_three(pool, body)
            for c in range(NCH - OUT_LAG, NCH):
                sum_step(c)



def attn1_stage(chip, front, ahead):
    nc, x = chip.nc, chip.x

    def s(name):
        return chip.sem("attn1_" + name)

    QKV = ((0, 1, 2), (3, 4, 5))
    V_TURN, GRAM, MIX = (0, 1), (2, 3), 4
    q_all, k_all, v_all = (chip.room[:, k * TOKENS:(k + 1) * TOKENS] for k in range(3))
    names = ("q1", "k1", "v1")
    HALF = NCH // BATCH
    bn, agg, fix = chip.buf("bn", [P, 3, NCH, 6]), chip.buf("bn_agg", [P, 3, 2]), chip.buf("bn_fix", [P, 6, 3])
    head_mask = chip.buf("head_mask", [P, P])
    gram, mix = chip.buf("gram", [P, BATCH, P]), chip.buf("mix", [P, BATCH, P])
    v_tok = chip.buf("v_tok", [P, 2, CH])
    tiles = "p (t d) -> p t d"

    mm, kept, stat = s("mm"), s("kept"), s("stat")
    bn_step, bn_pow, masked = s("bn_step"), s("bn_pow"), s("masked")
    sig_v, sig_q, v_turn, v_kept, gram_mm = s("sig_v"), s("sig_qk"), s("v_turn"), s("v_kept"), s("gram_mm")
    gram_kept, mix_mm, mix_kept = s("gram_kept"), s("mix_mm"), s("mix_kept")
    qk_ready, last_qk_ready, out_mm = s("qk_ready"), s("last_qk_ready"), s("out_mm")
    bp_added, x_new = s("bp_added"), s("x_new")

    with nc.Block() as block:
        @block.tensor
        def _(pe):
            def body(c, p):
                front.wait_xt(pe, c)
                if known(c) not in (0, 1):
                    pe.wait_ge(kept, 3 * (c - 1))
                for k, name in enumerate(names):
                    nc.tensor.matmul(chip.bank[QKV[p][k]][:], chip.mats[:, MAT[name]], chip.xt[:, p, :], start=True,
                                     stop=True).then_inc(mm, 1)
                if known(c) != NCH - 1:
                    front.turn_step(pe, c + 1, 1 - p)

            chunks_two(pe, body)

            pe.wait_ge(kept, 3 * NCH)
            for c in range(NCH + 1):
                if c < NCH:
                    p = c % 2
                    pe.wait_ge(sig_v, c + 1)
                    wait(pe, v_kept, c - 1)
                    for t in range(TPC):
                        last = nc.tensor.transpose(chip.bank[V_TURN[p]][:, t * P:(t + 1) * P],
                                                   v_all[:, c * CH + t * P:c * CH + (t + 1) * P], chip.ident[:])
                    last.then_inc(v_turn, 1)
                if c > 0:
                    b, p = (c - 1) // HALF, (c - 1) % 2
                    pe.wait_ge(v_kept, c)
                    for t in range(TPC):
                        tile = v_tok[:, p, t * P:(t + 1) * P]
                        last = nc.tensor.matmul(chip.bank[GRAM[b]][:, 0:P], tile, tile,
                                                start=(c - 1) % HALF == 0 and t == 0,
                                                stop=(c - 1) % HALF == HALF - 1 and t == TPC - 1)
                    last.then_inc(gram_mm, 1)
            for b in range(BATCH):
                pe.wait_ge(gram_kept, b + 1)
                wait(pe, mix_kept, b)
                nc.tensor.matmul(chip.bank[MIX][:, 0:P], gram[:, b, :], chip.mats[:, MAT["p1"]], start=True,
                                 stop=True).then_inc(mix_mm, 1)
            pe.wait_ge(mix_kept, BATCH)

            for c in range(NCH):
                if c < NCH - 1:
                    pe.wait_ge(qk_ready, c + 1)
                else:
                    pe.wait_ge(last_qk_ready, 1)
                wait(pe, x_new, c - 1)
                for t in range(TPC):
                    last = nc.tensor.matmul(chip.bank[V_TURN[c % 2]][:, t * P:(t + 1) * P],
                                            q_all[:, c * CH + t * P:c * CH + (t + 1) * P], mix[:, c // HALF, :],
                                            start=True, stop=True)
                last.then_inc(out_mm, 1)
                if c == 4:
                    ahead.turn_step(pe, 0, 0)
                if c == 6:
                    ahead.logits_step(pe, 0, 0)
            ahead.rows_turn_step(pe, 0, 0)

        @block.scalar
        def _(act):
            def body(c, p):
                for k, dst in enumerate((q_all, k_all, v_all)):
                    act.wait_ge(mm, 3 * c + k + 1)
                    nc.scalar.activation(dst[:, bass.ds(CH * c, CH)], chip.bank[QKV[p][k]][:], ACT.Copy).then_inc(
                        kept, 1)
                if known(c) != NCH - 1:
                    front.keep_by_scalar(act, c + 1, 1 - p)

            chunks_two(act, body)
            act.wait_ge(bn_step, 3 + 6)
            act.wait_ge(kept, 3 * NCH)
            def sigmoid(c, k, dst, done):
                chunk = dst[:, bass.ds(CH * c, CH)]
                nc.scalar.activation(chunk, chunk, ACT.Sigmoid, bias=fix[:, 5, k:k + 1],
                                     scale=fix[:, 3, k:k + 1]).then_inc(done, 1)

            with act.Fori(0, NCH) as c:
                sigmoid(c, 2, v_all, sig_v)
            with act.Fori(0, NCH) as c:
                sigmoid(c, 0, q_all, sig_q)
                sigmoid(c, 1, k_all, sig_q)
            ahead.rows_kept_step(act, 0, 0)

        @block.vector
        def _(dve):
            def batch_stats(c):
                for k, src in enumerate((q_all, k_all, v_all)):
                    dve.wait_ge(kept, 3 * c + k + 1)
                    nc.vector.bn_stats(bn[:, k, bass.ds(c, 1), :], src[:, bass.ds(CH * c, CH)]).then_inc(stat, 1)

            def body(c, p):
                if known(c) != NCH - 1:
                    front.moments_step(dve, c + 1, 1 - p)
                if known(c) != 0:
                    batch_stats(c - 1)
                if known(c) != NCH - 1:
                    front.normed_step(dve, c + 1, 1 - p)

            chunks_two(dve, body)
            batch_stats(NCH - 1)
            dve.wait_ge(stat, 3 * NCH)
            for k in range(3):
                nc.vector.bn_aggr(agg[:, k, :], bn[:, k, :, :].rearrange("p c s -> p (c s)")).then_inc(bn_step, 1)
            dve.wait_ge(bn_step, 3)
            nc.vector.tensor_scalar(fix[:, 0, :], agg[:, :, 1], EPS, None, ALU.add).then_inc(bn_step, 1)
            dve.wait_ge(bn_pow, 1)
            gammas = chip.cols[:, COL["gq"].start:COL["gv"].stop]
            betas = chip.cols[:, COL["tq"].start:COL["tv"].stop]
            nc.vector.tensor_tensor(fix[:, 2, :], fix[:, 1, :], gammas, ALU.mult).then_inc(bn_step, 1)
            dve.wait_ge(bn_step, 5)
            nc.vector.tensor_scalar(fix[:, 3, :], fix[:, 2, :], 4.0, None, ALU.mult).then_inc(bn_step, 1)
            nc.vector.tensor_tensor(fix[:, 4, :], agg[:, :, 0], fix[:, 2, :], ALU.mult).then_inc(bn_step, 1)
            dve.wait_ge(bn_step, 7)
            nc.vector.tensor_tensor(fix[:, 4, :], betas, fix[:, 4, :], ALU.subtract).then_inc(bn_step, 1)
            dve.wait_ge(bn_step, 8)
            nc.vector.tensor_scalar(fix[:, 5, :], fix[:, 4, :], 4.0, -4.0, ALU.mult, ALU.add).then_inc(bn_step, 1)
            for c in range(NCH):
                p = c % 2
                dve.wait_ge(v_turn, c + 1)
                wait(dve, gram_mm, c - 1)
                nc.vector.tensor_copy(v_tok[:, p, :], chip.bank[V_TURN[p]][:]).then_inc(v_kept, 1)
            dve.wait_ge(masked, 3)
            for b in range(BATCH):
                dve.wait_ge(gram_mm, HALF * (b + 1))
                nc.vector.tensor_tensor(gram[:, b, :], chip.bank[GRAM[b]][:, 0:P], head_mask[:], ALU.mult).then_inc(
                    gram_kept, 1)
            for b in range(BATCH):
                dve.wait_ge(mix_mm, b + 1)
                nc.vector.tensor_scalar(mix[:, b, :], chip.bank[MIX][:, 0:P], SCALE, None, ALU.mult).then_inc(
                    mix_kept, 1)

            def residual(c, p):
                dve.wait_ge(out_mm, c + 1)
                dve.wait_ge(bp_added, c + 1)
                tile = x[:, bass.ds(TPC * c, TPC), :]
                nc.vector.tensor_tensor(tile, chip.bank[V_TURN[p]][:].rearrange(tiles, t=TPC), tile,
                                        ALU.add).then_inc(x_new, 1)

            for c in range(NCH):
                residual(c, c % 2)
                if c == 1:
                    dve.wait_ge(x_new, 1)
                    ahead.moments_step(dve, 0, 0)
                    dve.wait_ge(sig_q, 2 * NCH)
                    chunk = slice((NCH - 1) * CH, NCH * CH)
                    nc.vector.tensor_tensor(q_all[:, chunk], q_all[:, chunk], k_all[:, chunk], ALU.mult).then_inc(
                        last_qk_ready, 1)
                if c == 3:
                    ahead.normed_step(dve, 0, 0)
                if c == 4:
                    ahead.keep_step(dve, 0, 0)
                    ahead.split_step(dve, 0, 0)
                if c == 6:
                    ahead.route_first(dve, 0, 0)
            ahead.route_second(dve, 0, 0)
            ahead.route_last(dve, 0, 0)

        @block.gpsimd
        def _(pool):
            nc.gpsimd.memset(head_mask[:], 1.0).then_inc(masked, 1)
            m = head_mask[:].rearrange("p (h d) -> p h d", d=HEAD)
            for n, (sign, start) in enumerate(((1, 0), (-1, HEAD - 1))):
                pool.wait_ge(masked, n + 1)
                nc.gpsimd.affine_select(out=m, in_=m, compare_op=ALU.is_ge, fill=0.0, base=start,
                                        pattern=[[-sign * HEAD, P // HEAD], [0, HEAD]],
                                        channel_multiplier=sign).then_inc(masked, 1)

            def body(c, p):
                if known(c) != NCH - 1:
                    front.power_step(pool, c + 1, 1 - p)
                pool.wait_ge(front.xs_ready, TPC * c + TPC)
                tile = x[:, bass.ds(TPC * c, TPC), :]
                nc.gpsimd.tensor_tensor(tile, tile, across(chip.rows[:, ROW["bp"]].unsqueeze(1), [P, TPC, P]),
                                        ALU.add).then_inc(bp_added, 1)

            chunks_two(pool, body)
            pool.wait_ge(bn_step, 4)
            nc.gpsimd.tensor_tensor(fix[:, 1, :], fix[:, 0, :], chip.neg_half[:, 0:3], ALU.pow).then_inc(bn_pow, 1)
            for c in range(NCH - 1):
                pool.wait_ge(sig_q, 2 * c + 2)
                chunk = slice(c * CH, (c + 1) * CH)
                nc.gpsimd.tensor_tensor(q_all[:, chunk], q_all[:, chunk], k_all[:, chunk], ALU.mult).then_inc(
                    qk_ready, 1)
            ahead.power_step(pool, 0, 0)



_LAID = ("x", "cols", "rows", "mats", "gens", "gens_t", "ew1", "ew2", "w1", "w2", "b2", "b1_row")


def macaron(nc, args, out):
    with ExitStack() as ctx:
        chip = Chip(nc, ctx)
        fronts, front = [], None
        for k, name in enumerate(STAGES):
            call = STAGES[:k].count(name)
            if name == "ffn0":
                front = Front0(chip, call, front)
            elif name == "ffn1":
                front = Front1(chip, call, front)
            else:
                front = Front(chip, name, 0, front, twice=False, affine=False, split=False)
            fronts.append(front)
        setup(chip, args, fronts[0])
        for name, front, ahead in zip(STAGES, fronts, fronts[1:] + [None]):
            if name == "ffn0":
                ffn0_stage(chip, front, ahead)
            elif name == "attn0":
                attn0_stage(chip, front, ahead)
            elif name == "ffn1":
                ffn1_stage(chip, front, ahead, out)
            elif name == "attn1":
                attn1_stage(chip, front, ahead)


def lay_out(a):
    import numpy as np

    g = {k: np.asarray(v) for k, v in a.items()}
    col = lambda v: v.reshape(P, 1)
    row = lambda v: np.broadcast_to(v.reshape(1, -1), (P, v.size))
    cols = [col(g["L0_ffn_ln_gamma"]), col(g["L0_ffn_ln_beta"]), g["L0_ffn_eb1"].reshape(U0, P).T, g["L0_ffn_eb2"].T,
            col(g["L0_attn_bq"]), col(g["L0_attn_bk"]), col(g["L0_attn_bv"]),
            col(g["L1_attn_gq"]), col(g["L1_attn_gk"]), col(g["L1_attn_gv"]),
            col(g["L1_attn_bq"]), col(g["L1_attn_bk"]), col(g["L1_attn_bv"])]
    rows = [row(g["L0_ffn_moe_gate_b"]), row(g["L0_ffn_abel_b"]), row(g["L0_ffn_gc_w"][:P, 0]),
            row(g["L0_ffn_gc_w"][P:, 0]), row(g["L0_ffn_gc_b"]), row(g["L0_attn_bo"]), row(g["L1_attn_bp"]),
            row(g["L1_ffn_router_b"])]
    mats = [g["L0_ffn_abel_w"], g["L0_ffn_moe_gate_w"], g["L0_attn_Wq"].T, g["L0_attn_Wk"].T, g["L0_attn_Wv"].T,
            g["L0_attn_Wo"].T, g["L1_attn_Wq"].T, g["L1_attn_Wk"].T, g["L1_attn_Wv"].T, g["L1_attn_Wp"].T,
            g["L1_ffn_router_w"].T]
    laid = {
        "x": g["L0_attn_x"].reshape(TOKENS, P),
        "cols": np.concatenate(cols, 1), "rows": np.concatenate(rows, 1), "mats": np.concatenate(mats, 1),
        "gens": g["L0_ffn_gens"].transpose(1, 0, 2), "gens_t": g["L0_ffn_gens"].transpose(2, 0, 1),
        "ew1": g["L0_ffn_ew1"].transpose(1, 0, 2).reshape(P, U0, P),
        "ew2": g["L0_ffn_ew2"].reshape(U0, P, P).transpose(1, 0, 2),
        "w1": g["L1_ffn_weights1"].transpose(1, 0, 2).reshape(P, U1, P),
        "w2": g["L1_ffn_weights2"].reshape(U1, P, P).transpose(1, 0, 2),
        "b2": g["L1_ffn_bias2"],
        "b1_row": g["L1_ffn_bias1"].reshape(1, U1, P),
    }
    return {k: np.ascontiguousarray(v) for k, v in laid.items()}


def kernel(**inputs):
    import concourse.bacc as bacc
    from concourse.bass_utils import run_bass_kernel_spmd

    nc = bacc.Bacc("TRN2", target_bir_lowering=False, num_devices=1)
    laid = lay_out(inputs)
    args = {k: nc.dram_tensor(f"in_{k}", laid[k].shape, F32, kind="ExternalInput").ap() for k in _LAID}
    out = nc.dram_tensor("out", (TOKENS, P), F32, kind="ExternalOutput").ap()
    macaron(nc, args, out)
    run = run_bass_kernel_spmd(nc, [{f"in_{k}": laid[k] for k in _LAID}], core_ids=[0])
    return run.results[0]["out"].reshape(BATCH, LENGTH, P)
```
